# Optimizing a Trainium2 kernel written in Bass

```python
import numpy as np
import jax
import jax.numpy as jnp

def _softmax(x, axis=-1):
    return jax.nn.softmax(x, axis=axis)

def _gelu(x):
    return jax.nn.gelu(x, approximate=True)

def _silu(x):
    return jax.nn.silu(x)

def _sigmoid(x):
    return jax.nn.sigmoid(x)

def _layernorm(x, axis=-1, eps=1e-05):
    m = jnp.mean(x, axis=axis, keepdims=True)
    v = jnp.var(x, axis=axis, keepdims=True)
    return (x - m) / jnp.sqrt(v + eps)

def _scatter_add(tgt, idx, src, axis=0):
    return tgt.at[idx].add(src)

def _segment_sum(src, seg, n):
    return jax.ops.segment_sum(src, seg, n)
kernel_name = 'mk_gnn_resnorm_d4_gnn_r32_96996b'

def setup_inputs(seed: int=0):
    np.random.seed(seed)
    _w = jnp.asarray

    def _rec_inputs():
        import jax
        import jax.numpy as jnp
        _gk = jax.random.key(seed)
        x = -0.000202 + 1 * jax.random.normal(jax.random.fold_in(_gk, 1), (50000, 128), jnp.float32)
        src = jax.random.randint(jax.random.fold_in(_gk, 2), (50000,), 0, 50000, jnp.int32)
        dst = jnp.minimum((50000 * jax.random.uniform(jax.random.fold_in(_gk, 3), (50000,)) ** 2.0).astype(jnp.int32), 49999)
        _o = jnp.argsort(dst, stable=True)
        src = src[_o]
        dst = dst[_o]
        edge_attr_128 = 5.93493e-05 + 1.00006 * jax.random.normal(jax.random.fold_in(_gk, 12), (50000, 128), jnp.float32)
        edge_attr_3 = -0.000451519 + 1.00018 * jax.random.normal(jax.random.fold_in(_gk, 13), (50000, 3), jnp.float32)
        edge_weight = jax.random.uniform(jax.random.fold_in(_gk, 15), (50000,), jnp.float32, 0.0, 0.999998)
        return (x, src, dst, edge_attr_128, edge_attr_3, edge_weight)
    x, src, dst, edge_attr_128, edge_attr_3, edge_weight = _rec_inputs()

    def _L0_gnn_setup():
        import jax, jax.numpy as jnp
        import numpy as np
        N = 50000
        E = 25000
        MUL = 32
        NB = 8
        R_MAX = 1.0
        AVG = 16.0
        SQ3 = 3.0 ** 0.5

        def _radial_embedding(r):
            x = jnp.clip(r / R_MAX, 0.0, 1.0)
            centers = jnp.arange(NB, dtype=jnp.float32) / (NB - 1)
            sigma = 1.0 / (NB - 1)
            emb = jnp.exp(-0.5 * ((x[:, None] - centers[None, :]) / sigma) ** 2)
            emb = emb * NB ** 0.5 * (r <= R_MAX).astype(jnp.float32)[:, None]
            return emb
        key = jax.random.key(seed)
        k = jax.random.split(key, 12)
        inp = {'node_feats': jax.random.normal(k[0], (N, 4 * MUL), dtype=jnp.float32), 'edge_vec': jax.random.normal(k[1], (E, 3), dtype=jnp.float32), 'edge_length': jax.random.uniform(k[2], (E,), dtype=jnp.float32), 'senders': jax.random.randint(k[3], (E,), 0, N, dtype=jnp.int32), 'receivers': jax.random.randint(k[4], (E,), 0, N, dtype=jnp.int32), 'num_nodes': N, 'W_up0': jax.random.normal(k[5], (MUL, MUL), dtype=jnp.float32), 'W_up1': jax.random.normal(k[6], (MUL, MUL), dtype=jnp.float32), 'mlp_w0': jax.random.normal(k[7], (NB, 64), dtype=jnp.float32) / NB ** 0.5, 'mlp_b0': jnp.zeros((64,), dtype=jnp.float32), 'mlp_w1': jax.random.normal(k[8], (64, 64), dtype=jnp.float32) / 8.0, 'mlp_b1': jnp.zeros((64,), dtype=jnp.float32), 'mlp_w2': jax.random.normal(k[9], (64, 4 * MUL), dtype=jnp.float32) / 8.0, 'mlp_b2': jnp.zeros((4 * MUL,), dtype=jnp.float32), 'W_out0': jax.random.normal(k[10], (2 * MUL, MUL), dtype=jnp.float32), 'W_out1': jax.random.normal(k[11], (2 * MUL, MUL), dtype=jnp.float32)}
        return inp
    _L0_gnn_all = _L0_gnn_setup()
    _L0_gnn_in = {k: v for k, v in _L0_gnn_all.items() if k in ('W_up0', 'W_up1', 'mlp_w0', 'mlp_b0', 'mlp_w1', 'mlp_b1', 'mlp_w2', 'mlp_b2', 'W_out0', 'W_out1')}
    del _L0_gnn_all

    def _L1_gnn_setup():
        import jax, jax.numpy as jnp
        import numpy as np
        N = 50000
        E = 18750
        D = 128

        def _gcn_stack(x, row, col, norm, W1, R1, W2, R2, W3, Wh, bh):
            n = x.shape[0]

            def conv(x, W, R, act):
                h = x @ W
                msg = h[row] * norm[:, None]
                agg = jax.ops.segment_sum(msg, col, num_segments=n)
                if R is not None:
                    agg = agg + x @ R
                if act:
                    agg = jax.nn.relu(agg)
                return agg
            x = conv(x, W1, R1, True)
            x = conv(x, W2, R2, True)
            x = conv(x, W3, None, False)
            return x @ Wh + bh
        key = jax.random.key(seed)
        ks = jax.random.split(key, 10)
        scale = 1.0 / np.sqrt(D)
        inp = {'x': jax.random.normal(ks[0], (N, D), dtype=jnp.float32), 'edge_index': jax.random.randint(ks[1], (2, E), 0, N, dtype=jnp.int64), 'W1': jax.random.normal(ks[2], (D, D), dtype=jnp.float32) * scale, 'R1': jax.random.normal(ks[3], (D, D), dtype=jnp.float32) * scale, 'W2': jax.random.normal(ks[4], (D, D), dtype=jnp.float32) * scale, 'R2': jax.random.normal(ks[5], (D, D), dtype=jnp.float32) * scale, 'W3': jax.random.normal(ks[6], (D, D), dtype=jnp.float32) * scale, 'Wh': jax.random.normal(ks[7], (D, D), dtype=jnp.float32) * scale, 'bh': jnp.zeros((D,), dtype=jnp.float32)}
        return inp
    _L1_gnn_all = _L1_gnn_setup()
    _L1_gnn_in = {k: v for k, v in _L1_gnn_all.items() if k in ('W1', 'R1', 'W2', 'R2', 'W3', 'Wh', 'bh')}
    del _L1_gnn_all

    def _L2_gnn_setup():
        import jax, jax.numpy as jnp
        import numpy as np
        N_NODE = 3125
        N_EDGE = 50000
        D_IN = 128
        D_OUT = 128
        key = jax.random.key(seed)
        k1, k2, k3, k4, k5 = jax.random.split(key, 5)
        x = jax.random.normal(k1, (N_NODE, D_IN), dtype=jnp.float32)
        lim = 1.0 / np.sqrt(D_IN)
        W = jax.random.uniform(k2, (D_OUT, D_IN), dtype=jnp.float32, minval=-lim, maxval=lim)
        b = jax.random.uniform(k3, (D_OUT,), dtype=jnp.float32, minval=-lim, maxval=lim)
        edge_index = jax.random.randint(k4, (2, N_EDGE), 0, N_NODE, dtype=jnp.int64)
        edge_weight = jax.random.uniform(k5, (N_EDGE,), dtype=jnp.float32)
        return {'x': x, 'W': W, 'b': b, 'edge_index': edge_index, 'edge_weight': edge_weight}
    _L2_gnn_all = _L2_gnn_setup()
    _L2_gnn_in = {k: v for k, v in _L2_gnn_all.items() if k in ('W', 'b')}
    del _L2_gnn_all

    def _L3_gnn_setup():
        import jax, jax.numpy as jnp
        import numpy as np
        BN_EPS = 1e-05

        def _bn(x, g, b):
            mu = jnp.mean(x, axis=0)
            var = jnp.mean(jnp.square(x - mu), axis=0)
            return g * (x - mu) * jax.lax.rsqrt(var + BN_EPS) + b
        key = jax.random.key(seed)
        ks = jax.random.split(key, 18)
        N, E, Cin, H, L, Cout = (50000, 18750, 128, 128, 3, 128)
        s_in = 1.0 / np.sqrt(Cin)
        s_h = 1.0 / np.sqrt(H)
        s_2h = 1.0 / np.sqrt(2 * H)
        return {'x': jax.random.normal(ks[0], (N, Cin), jnp.float32), 'edge_index': jax.random.randint(ks[1], (2, E), 0, N, jnp.int32), 'edge_attr': jax.random.normal(ks[2], (E, Cin), jnp.float32), 'W_atom': jax.random.normal(ks[3], (Cin, H), jnp.float32) * s_in, 'b_atom': jnp.zeros((H,), jnp.float32), 'W_bond': jax.random.normal(ks[4], (Cin, H), jnp.float32) * s_in, 'b_bond': jnp.zeros((H,), jnp.float32), 'eps': jnp.zeros((L,), jnp.float32), 'W1': jax.random.normal(ks[5], (L, H, 2 * H), jnp.float32) * s_h, 'b1': jnp.zeros((L, 2 * H), jnp.float32), 'g1': jnp.ones((L, 2 * H), jnp.float32), 'be1': jnp.zeros((L, 2 * H), jnp.float32), 'W2': jax.random.normal(ks[6], (L, 2 * H, H), jnp.float32) * s_2h, 'b2': jnp.zeros((L, H), jnp.float32), 'gn': jnp.ones((L, H), jnp.float32), 'bet': jnp.zeros((L, H), jnp.float32), 'W_out': jax.random.normal(ks[7], (H, Cout), jnp.float32) * s_h, 'b_out': jnp.zeros((Cout,), jnp.float32)}
    _L3_gnn_all = _L3_gnn_setup()
    _L3_gnn_in = {k: v for k, v in _L3_gnn_all.items() if k in ('W_atom', 'b_atom', 'W_bond', 'b_bond', 'eps', 'W1', 'b1', 'g1', 'be1', 'W2', 'b2', 'gn', 'bet', 'W_out', 'b_out')}
    del _L3_gnn_all
    return {'x': x, 'src': src, 'dst': dst, 'edge_attr_128': edge_attr_128, 'edge_attr_3': edge_attr_3, 'edge_weight': edge_weight, 'L0_gnn_W_up0': _L0_gnn_in['W_up0'], 'L0_gnn_W_up1': _L0_gnn_in['W_up1'], 'L0_gnn_mlp_w0': _L0_gnn_in['mlp_w0'], 'L0_gnn_mlp_b0': _L0_gnn_in['mlp_b0'], 'L0_gnn_mlp_w1': _L0_gnn_in['mlp_w1'], 'L0_gnn_mlp_b1': _L0_gnn_in['mlp_b1'], 'L0_gnn_mlp_w2': _L0_gnn_in['mlp_w2'], 'L0_gnn_mlp_b2': _L0_gnn_in['mlp_b2'], 'L0_gnn_W_out0': _L0_gnn_in['W_out0'], 'L0_gnn_W_out1': _L0_gnn_in['W_out1'], 'L1_gnn_W1': _L1_gnn_in['W1'], 'L1_gnn_R1': _L1_gnn_in['R1'], 'L1_gnn_W2': _L1_gnn_in['W2'], 'L1_gnn_R2': _L1_gnn_in['R2'], 'L1_gnn_W3': _L1_gnn_in['W3'], 'L1_gnn_Wh': _L1_gnn_in['Wh'], 'L1_gnn_bh': _L1_gnn_in['bh'], 'L2_gnn_W': _L2_gnn_in['W'], 'L2_gnn_b': _L2_gnn_in['b'], 'L3_gnn_W_atom': _L3_gnn_in['W_atom'], 'L3_gnn_b_atom': _L3_gnn_in['b_atom'], 'L3_gnn_W_bond': _L3_gnn_in['W_bond'], 'L3_gnn_b_bond': _L3_gnn_in['b_bond'], 'L3_gnn_eps': _L3_gnn_in['eps'], 'L3_gnn_W1': _L3_gnn_in['W1'], 'L3_gnn_b1': _L3_gnn_in['b1'], 'L3_gnn_g1': _L3_gnn_in['g1'], 'L3_gnn_be1': _L3_gnn_in['be1'], 'L3_gnn_W2': _L3_gnn_in['W2'], 'L3_gnn_b2': _L3_gnn_in['b2'], 'L3_gnn_gn': _L3_gnn_in['gn'], 'L3_gnn_bet': _L3_gnn_in['bet'], 'L3_gnn_W_out': _L3_gnn_in['W_out'], 'L3_gnn_b_out': _L3_gnn_in['b_out']}

def reference(x, src, dst, edge_attr_128, edge_attr_3, edge_weight, L0_gnn_W_up0, L0_gnn_W_up1, L0_gnn_mlp_w0, L0_gnn_mlp_b0, L0_gnn_mlp_w1, L0_gnn_mlp_b1, L0_gnn_mlp_w2, L0_gnn_mlp_b2, L0_gnn_W_out0, L0_gnn_W_out1, L1_gnn_W1, L1_gnn_R1, L1_gnn_W2, L1_gnn_R2, L1_gnn_W3, L1_gnn_Wh, L1_gnn_bh, L2_gnn_W, L2_gnn_b, L3_gnn_W_atom, L3_gnn_b_atom, L3_gnn_W_bond, L3_gnn_b_bond, L3_gnn_eps, L3_gnn_W1, L3_gnn_b1, L3_gnn_g1, L3_gnn_be1, L3_gnn_W2, L3_gnn_b2, L3_gnn_gn, L3_gnn_bet, L3_gnn_W_out, L3_gnn_b_out):
    import jax
    import jax.numpy as jnp

    def _L0_gnn_ref(node_feats, edge_vec, edge_length, senders, receivers, num_nodes, W_up0, W_up1, mlp_w0, mlp_b0, mlp_w1, mlp_b1, mlp_w2, mlp_b2, W_out0, W_out1):
        import jax, jax.numpy as jnp
        import numpy as np
        N = 50000
        E = 25000
        MUL = 32
        NB = 8
        R_MAX = 1.0
        AVG = 16.0
        SQ3 = 3.0 ** 0.5

        def _radial_embedding(r):
            x = jnp.clip(r / R_MAX, 0.0, 1.0)
            centers = jnp.arange(NB, dtype=jnp.float32) / (NB - 1)
            sigma = 1.0 / (NB - 1)
            emb = jnp.exp(-0.5 * ((x[:, None] - centers[None, :]) / sigma) ** 2)
            emb = emb * NB ** 0.5 * (r <= R_MAX).astype(jnp.float32)[:, None]
            return emb
        f32 = jnp.float32
        rhat = edge_vec / (jnp.linalg.norm(edge_vec, axis=-1, keepdims=True) + 1e-12)
        Y1 = SQ3 * rhat
        emb = _radial_embedding(edge_length)
        h = jax.nn.silu(emb @ mlp_w0 + mlp_b0)
        h = jax.nn.silu(h @ mlp_w1 + mlp_b1)
        w = (h @ mlp_w2 + mlp_b2).reshape(-1, 4, MUL)
        s = node_feats[:, :MUL]
        v = node_feats[:, MUL:].reshape(-1, MUL, 3)
        xs = s @ W_up0 / f32(MUL) ** 0.5
        xv = jnp.einsum('nmc,mk->nkc', v, W_up1) / f32(MUL) ** 0.5
        ss = xs[senders]
        vv = xv[senders]
        m0 = w[:, 0] * ss
        m1 = w[:, 1][:, :, None] * ss[:, :, None] * Y1[:, None, :]
        m2 = w[:, 2][:, :, None] * vv
        m3 = w[:, 3] * (jnp.einsum('emc,ec->em', vv, Y1) / SQ3)
        mid_s = jnp.concatenate([m0, m3], axis=1)
        mid_v = jnp.concatenate([m1, m2], axis=1)
        msg_s = jax.ops.segment_sum(mid_s, receivers, num_segments=num_nodes)
        msg_v = jax.ops.segment_sum(mid_v, receivers, num_segments=num_nodes)
        out_s = msg_s @ W_out0 / f32(2 * MUL) ** 0.5
        out_v = jnp.einsum('nmc,mk->nkc', msg_v, W_out1) / f32(2 * MUL) ** 0.5
        out = jnp.concatenate([out_s, out_v.reshape(-1, 3 * MUL)], axis=1)
        return out / max(AVG, 1e-08)

    def _L1_gnn_ref(x, edge_index, W1, R1, W2, R2, W3, Wh, bh):
        import jax, jax.numpy as jnp
        import numpy as np
        N = 50000
        E = 18750
        D = 128

        def _gcn_stack(x, row, col, norm, W1, R1, W2, R2, W3, Wh, bh):
            n = x.shape[0]

            def conv(x, W, R, act):
                h = x @ W
                msg = h[row] * norm[:, None]
                agg = jax.ops.segment_sum(msg, col, num_segments=n)
                if R is not None:
                    agg = agg + x @ R
                if act:
                    agg = jax.nn.relu(agg)
                return agg
            x = conv(x, W1, R1, True)
            x = conv(x, W2, R2, True)
            x = conv(x, W3, None, False)
            return x @ Wh + bh
        n = x.shape[0]
        loops = jnp.arange(n, dtype=edge_index.dtype)
        row = jnp.concatenate([edge_index[0], loops])
        col = jnp.concatenate([edge_index[1], loops])
        deg = jax.ops.segment_sum(jnp.ones_like(col, dtype=x.dtype), col, num_segments=n)
        dinv = deg ** (-0.5)
        norm = dinv[row] * dinv[col]
        return _gcn_stack(x, row, col, norm, W1, R1, W2, R2, W3, Wh, bh)

    def _L2_gnn_ref(x, W, b, edge_index, edge_weight):
        import jax, jax.numpy as jnp
        import numpy as np
        N_NODE = 3125
        N_EDGE = 50000
        D_IN = 128
        D_OUT = 128
        n_node = x.shape[0]
        row, col = (edge_index[0], edge_index[1])
        deg = jax.ops.segment_sum(edge_weight, row, num_segments=n_node)
        deg = jnp.where(deg < 0.5, deg + 1.0, deg)
        w = edge_weight / deg[row]
        h = jax.nn.relu(x @ W.T + b)
        out = jax.ops.segment_sum(w[:, None] * h[col], row, num_segments=n_node)
        return out

    def _L3_gnn_ref(x, edge_index, edge_attr, W_atom, b_atom, W_bond, b_bond, eps, W1, b1, g1, be1, W2, b2, gn, bet, W_out, b_out):
        import jax, jax.numpy as jnp
        import numpy as np
        BN_EPS = 1e-05

        def _bn(x, g, b):
            mu = jnp.mean(x, axis=0)
            var = jnp.mean(jnp.square(x - mu), axis=0)
            return g * (x - mu) * jax.lax.rsqrt(var + BN_EPS) + b
        N = x.shape[0]
        L = eps.shape[0]
        src, dst = (edge_index[0], edge_index[1])
        h = x @ W_atom + b_atom
        ea = edge_attr @ W_bond + b_bond
        for i in range(L):
            msg = jax.nn.relu(h[src] + ea)
            agg = jax.ops.segment_sum(msg, dst, num_segments=N)
            z = (1.0 + eps[i]) * h + agg
            z = z @ W1[i] + b1[i]
            z = jax.nn.relu(_bn(z, g1[i], be1[i]))
            z = z @ W2[i] + b2[i]
            h = jax.nn.relu(_bn(z, gn[i], bet[i]))
        return h @ W_out + b_out
    edge_index = jnp.stack([src, dst])
    x = _layernorm(x + _L0_gnn_ref(x, edge_attr_3, edge_weight, src, dst, 50000, L0_gnn_W_up0, L0_gnn_W_up1, L0_gnn_mlp_w0, L0_gnn_mlp_b0, L0_gnn_mlp_w1, L0_gnn_mlp_b1, L0_gnn_mlp_w2, L0_gnn_mlp_b2, L0_gnn_W_out0, L0_gnn_W_out1), axis=-1)
    x = _layernorm(x + _L1_gnn_ref(x, edge_index, L1_gnn_W1, L1_gnn_R1, L1_gnn_W2, L1_gnn_R2, L1_gnn_W3, L1_gnn_Wh, L1_gnn_bh), axis=-1)
    x = _layernorm(x + _L2_gnn_ref(x, L2_gnn_W, L2_gnn_b, edge_index, edge_weight), axis=-1)
    x = _layernorm(x + _L3_gnn_ref(x, edge_index, edge_attr_128, L3_gnn_W_atom, L3_gnn_b_atom, L3_gnn_W_bond, L3_gnn_b_bond, L3_gnn_eps, L3_gnn_W1, L3_gnn_b1, L3_gnn_g1, L3_gnn_be1, L3_gnn_W2, L3_gnn_b2, L3_gnn_gn, L3_gnn_bet, L3_gnn_W_out, L3_gnn_b_out), axis=-1)
    return x

_drawn_inputs = setup_inputs


def setup_inputs(seed=0):
    import zlib

    import numpy as np

    out = dict(_drawn_inputs(seed))
    spreads = {'L0_gnn_mlp_b0': (0.0, 0.8),
     'L0_gnn_mlp_b1': (0.0, 0.8),
     'L0_gnn_mlp_b2': (0.0, 2.0),
     'L1_gnn_bh': (0.0, 0.1),
     'L3_gnn_b_atom': (0.0, 0.276),
     'L3_gnn_b_bond': (0.0, 0.1),
     'L3_gnn_eps': (0.0, 0.471),
     'L3_gnn_b1': (0.0, 2.0),
     'L3_gnn_g1': (1.0, 0.2),
     'L3_gnn_be1': (0.0, 0.1),
     'L3_gnn_b2': (0.0, 2.0),
     'L3_gnn_gn': (1.0, 0.2),
     'L3_gnn_bet': (0.0, 0.1),
     'L3_gnn_b_out': (0.0, 0.1)}
    factors = {'edge_attr_3': 4.381,
     'L0_gnn_W_up0': 4.226,
     'L0_gnn_W_up1': 4.13,
     'L0_gnn_mlp_w0': 3.563,
     'L0_gnn_mlp_w1': 3.031,
     'L0_gnn_mlp_w2': 2.991,
     'L0_gnn_W_out0': 6.081,
     'L0_gnn_W_out1': 3.442}
    for name, (base, spread) in spreads.items():
        noise = np.random.default_rng([zlib.crc32(name.encode()), seed]).standard_normal(out[name].shape)
        drawn = base * np.exp(spread * noise) if base else spread * noise
        out[name] = jnp.asarray(drawn.astype(out[name].dtype))
    for name, factor in factors.items():
        out[name] = (out[name] * factor).astype(out[name].dtype)
    return out
```

```python
from contextlib import ExitStack

import numpy as np

import concourse.bass as bass
from concourse import mybir

F32 = mybir.dt.float32
F16 = mybir.dt.float16
I32 = mybir.dt.int32
ALU = mybir.AluOpType
ACT = mybir.ActivationFunctionType

P = 128
N = 50000
J = 4
G = (N + P * J - 1) // (P * J)
T = G * J
NP = T * P
W = J * P
FULL = N // T
REST = N - FULL * T
LASTP = (N - (G - 1) * W) // J
PAD = NP - 1
SKIP = 1 << 20
MUL = 32
NB = 8
HID = 64
AVG = 16.0
LN_EPS = 1e-5
BN_EPS = 1e-5
LAYERS = 3


def ds(i, n=1):
    return slice(i, i + n) if isinstance(i, int) else bass.DynSlice(i, n)


def block_of(t, g):
    return t[g] if isinstance(g, int) else t[bass.DynSlice(g, 1)].rearrange("a p f -> (a p) f")


def rows_of(t, g):
    return block_of(t.rearrange("(g p j) d -> g p (j d)", p=P, j=J), g)


def x_rows(t, last=False):
    if last:
        return t[(G - 1) * W:N, :].rearrange("(p j) d -> p (j d)", j=J)
    return t[0:(G - 1) * W, :].rearrange("(g p j) d -> g p (j d)", p=P, j=J)


def loop(eng, body):
    body(0)
    with eng.Fori(1, G // 2 - 1) as i:
        body(i)
    body(G // 2 - 1)


def front_and_back(eng, front, back):
    def body(i, last=False):
        front(i, 2 * i + 1, 1)
        back(i, 2 * i, 0)
        if not last:
            front(i + 1, 2 * i + 2, 0)
        back(i, 2 * i + 1, 1)
    front(0, 0, 0)
    body(0)
    with eng.Fori(1, G // 2 - 1) as i:
        body(i)
    body(G // 2 - 1, last=True)


class Phase:

    def __init__(self, nc, ctx):
        self.nc, self.ctx = nc, ctx
        self.n = 0

    def sb(self, name, shape, dt=F32):
        return self.ctx.enter_context(self.nc.sbuf_tensor(f"{name}_{self.nc.next_id()}", shape, dt))

    def ps(self, name, shape, dt=F32):
        return self.ctx.enter_context(self.nc.psum_tensor(f"{name}_{self.nc.next_id()}", shape, dt))

    def sem(self, name):
        return self.nc.alloc_semaphore(name=f"{name}_{self.nc.next_id()}")


def wait(eng, sem, value, passed=None):
    if isinstance(value, int):
        if value > 0:
            eng.wait_ge(sem, value)
        return
    eng.wait_ge(sem, value)
    if passed is not None:
        eng.sem_inc(passed, 1)


def fixed_tiles(nc, ctx):
    def sb(name, shape, dt=F32):
        return ctx.enter_context(nc.sbuf_tensor(name, shape, dt))

    k = {
        "ident": sb("ident", [P, P]), "ident16": sb("ident16", [P, P], F16),
        "below": sb("below", [P, P]), "below16": sb("below16", [P, P], F16),
        "ones": sb("ones", [P, P]), "cols16": sb("cols16", [P, T], F16),
        "dinv": sb("dinv", [P, T]), "one_row": sb("one_row", [1, P]),
        "eps": sb("eps", [P, 1]),
    }
    for c in "rs":
        k["key_" + c] = sb("key_" + c, [P, T])
        k["before_" + c] = sb("before_" + c, [P, T])
        k["from_" + c] = sb("from_" + c, [P, T], I32)
        k["to_" + c] = sb("to_" + c, [P, T], I32)
    k["edge_r"] = sb("edge_r", [P, T], I32)
    k["weight_r"] = sb("weight_r", [P, T])
    k["weight_s"] = sb("weight_s", [P, T])
    k["vec_r"] = sb("vec_r", [P, T, 3])
    return k


def count_and_rank(nc, k, d, src, dst, edge_weight, edge_attr_3):
    with nc.cleanup_on_exit(), ExitStack() as ctx:
        ph = Phase(nc, ctx)
        sb, ps, sem = ph.sb, ph.ps, ph.sem
        key = [sb("key0", [P, T], I32), sb("key1", [P, T], I32)]
        other = sb("other", [P, T], I32)
        number = sb("number", [P, T], I32)
        cols_i = sb("cols_i", [P, T], I32)
        part = sb("part", [P, 2, T], I32)
        lo = [sb("lo0", [P, T]), sb("lo1", [P, T])]
        hi = [sb("hi0", [P, T]), sb("hi1", [P, T])]
        attr = sb("attr", [P, T * 3])
        weight = sb("weight", [P, T])
        fields = [sb("fields0", [P, T, 8]), sb("fields1", [P, T, 8])]
        one_lo = sb("one_lo", [P, 2, 4, P], F16)
        one_hi = sb("one_hi", [P, 2, 4, T], F16)
        lo_t = sb("lo_t", [P, 2, 2, P])
        lo_t16 = sb("lo_t16", [P, 2, 2, P], F16)
        same16 = sb("same16", [P, 2, 2, P], F16)
        table = sb("table", [P, 2, T])
        count = sb("count", [P, 2, T])
        begin = sb("begin", [P, 2, T])
        total = sb("total", [P, T])
        scan = sb("scan", [P, T])
        picked = sb("picked", [P, 2, T])
        found = sb("found", [P, 2, 4])
        place = sb("place", [P, 2, T])
        place_i = sb("place_i", [P, 2, T], I32)
        row_i = sb("row_i", [P, 2, T], I32)
        degree = sb("degree", [P, T])
        ones_row = sb("ones_row", [P, T])
        idx = sb("idx", [P, 2, 2, J], I32)
        out_rows = sb("out_rows", [P, 2, 2, J, 8])
        run_ps = [ps("run0", [P, 512]), ps("run1", [P, 512])]
        look_ps = [ps("look0", [P, 512]), ps("look1", [P, 512])]
        turn_ps = [ps("turn0", [P, 1024], F16), ps("turn1", [P, 1024], F16)]
        same_ps = [ps("same0", [P, 512]), ps("same1", [P, 512])]

        fills, loaded, iotas = sem("fills"), sem("loaded"), sem("iotas")
        made, ready = sem("made"), sem("ready")
        hot, counted, hist, begun = sem("hot"), sem("counted"), sem("hist"), sem("begun")
        summed, hot2 = sem("summed"), sem("hot2")
        turned, turned_out, tabled = sem("turned"), sem("turned_out"), sem("tabled")
        same, masked, looked, ranked, updated = sem("same"), sem("masked"), sem("looked"), sem("ranked"), sem("updated")
        placed = sem("placed")
        rooted, rowed, staged = sem("rooted"), sem("rowed"), sem("staged")
        sent = [sem("sent0"), sem("sent1")]
        passed = sem("passed")
        block = ctx.enter_context(nc.Block())

        def edges(t, c=1):
            return (t[0:FULL * T * c].rearrange("(p t) -> p t", t=T * c),
                    t[FULL * T * c:N * c].rearrange("(a t) -> a t", a=1))

        @block.sync
        def _(sp):
            sp.wait_ge(fills, 6)
            flat = edge_attr_3.rearrange("n c -> (n c)")
            for tile, array, c in ((key[0], dst, 1), (key[1], src, 1), (other, dst, 1),
                                   (weight, edge_weight, 1), (attr, flat, 3)):
                a, b = edges(array, c)
                sp.dma_start(tile[0:FULL, :], a).then_inc(loaded, 16)
                sp.dma_start(tile[FULL:FULL + 1, 0:REST * c], b).then_inc(loaded, 16)
            a, b = edges(src)
            sp.dma_start(number[0:FULL, :], a).then_inc(loaded, 16)
            sp.dma_start(number[FULL:FULL + 1, 0:REST], b).then_inc(loaded, 16)

        @block.gpsimd
        def _(pool):
            nc.gpsimd.memset(k["ones"][:, :], 1.0).then_inc(made, 1)
            nc.gpsimd.iota(cols_i[:, :], pattern=[[1, T]], base=0, channel_multiplier=0).then_inc(iotas, 1)
            nc.gpsimd.iota(part[:, 0, :], pattern=[[1, T]], base=0, channel_multiplier=T).then_inc(iotas, 1)
            pool.wait_ge(made, 1)
            nc.gpsimd.affine_select(out=k["ident"][:, :], in_=k["ones"][:, :], compare_op=ALU.is_equal, fill=0.0,
                                    base=0, pattern=[[-1, P]], channel_multiplier=1).then_inc(made, 1)
            nc.gpsimd.affine_select(out=k["below"][:, :], in_=k["ones"][:, :], compare_op=ALU.is_gt, fill=0.0,
                                    base=0, pattern=[[1, P]], channel_multiplier=-1).then_inc(made, 1)

            def body(i):
                for par in range(2):
                    g = 2 * i + par
                    for c in range(2):
                        wait(pool, staged, 2 * g + c + 1, passed)
                        for j in range(J):
                            nc.gpsimd.indirect_dma_start(
                                d[f"sorted_{'rs'[c]}"], bass.IndirectOffsetOnAxis(ap=idx[:, par, c, j:j + 1], axis=0),
                                out_rows[:, par, c, j, :], None).then_inc(sent[par], 16)
            loop(pool, body)
            pool.wait_ge(sent[0], 16 * J * G)
            pool.wait_ge(sent[1], 16 * J * G)

        @block.vector
        def _(v):
            steps = [0]

            def step(ins):
                steps[0] += 1
                ins.then_inc(ready, 1)
                v.wait_ge(ready, steps[0])

            for tile, value in ((key[0], PAD), (key[1], PAD), (other, 0), (number, 0), (weight, 0), (attr, 0)):
                nc.vector.memset(tile[:, :], value).then_inc(fills, 1)
            nc.vector.memset(k["eps"][:, :], LN_EPS)
            nc.vector.memset(k["one_row"][:, :], 1.0)
            nc.vector.memset(ones_row[:, :], 1.0)
            nc.vector.memset(fields[0][:, :, :], 0.0)
            step(nc.vector.memset(fields[1][:, :, :], 0.0))
            v.wait_ge(made, 3)
            nc.vector.tensor_copy(k["ident16"][:, :], k["ident"][:, :])
            nc.vector.tensor_copy(k["below16"][:, :], k["below"][:, :])
            v.wait_ge(iotas, 2)
            nc.vector.tensor_copy(k["cols16"][:, :], cols_i[:, :])
            v.wait_ge(loaded, 16 * 12)
            f0, f1 = fields
            nc.vector.tensor_copy(f0[:, :, 0], key[0][:, :])
            nc.vector.tensor_copy(f0[:, :, 1], number[:, :])
            nc.vector.tensor_scalar(f0[:, :, 2], part[:, 0, :], float(N - 1), None, ALU.min)
            nc.vector.tensor_copy(f0[:, :, 3], weight[:, :])
            nc.vector.tensor_copy(f0[:, :, 4:7], attr[:, :].rearrange("p (t c) -> p t c", c=3))
            nc.vector.tensor_copy(f1[:, :, 0], key[1][:, :])
            nc.vector.tensor_copy(f1[:, :, 1], other[:, :])
            step(nc.vector.tensor_copy(f1[:, :, 3], weight[:, :]))
            for c in range(2):
                step(nc.vector.tensor_scalar(part[:, 0, :], key[c][:, :], 2, P - 1, ALU.logical_shift_right, ALU.bitwise_and))
                step(nc.vector.tensor_copy(lo[c][:, :], part[:, 0, :]))
                step(nc.vector.tensor_scalar(part[:, 0, :], key[c][:, :], 9, 2, ALU.logical_shift_right, ALU.logical_shift_left))
                step(nc.vector.tensor_scalar(part[:, 1, :], key[c][:, :], J - 1, None, ALU.bitwise_and))
                step(nc.vector.tensor_tensor(part[:, 0, :], part[:, 0, :], part[:, 1, :], ALU.bitwise_or))
                step(nc.vector.tensor_copy(hi[c][:, :], part[:, 0, :]))

            def one_hots(t, slot, done):
                for c in range(2):
                    nc.vector.tensor_scalar(one_lo[:, c, slot, :], k["cols16"][:, 0:P], lo[c][:, ds(t)], None, ALU.is_equal)
                    nc.vector.tensor_scalar(one_hi[:, c, slot, :], k["cols16"][:, :], hi[c][:, ds(t)], None,
                                            ALU.is_equal).then_inc(done, 1)

            def count_body(i):
                for r in range(4):
                    wait(v, counted, 2 * (4 * i + r - 3))
                    one_hots(4 * i + r, r, hot)
            count_body(0)
            with v.Fori(1, G) as i:
                count_body(i)
            v.wait_ge(counted, 2 * T)
            for c in range(2):
                step(nc.vector.tensor_copy(count[:, c, :], run_ps[c][:, 0:T]))
            v.sem_inc(hist, 1)
            step(nc.vector.tensor_scalar(degree[:, :], count[:, 0, :], 1.0, None, ALU.add))
            v.sem_inc(hist, 1)
            for c in range(2):
                v.wait_ge(summed, c + 1)
                step(nc.vector.tensor_copy(total[:, :], look_ps[c][:, 0:T]))
                step(nc.vector.tensor_tensor_scan(scan[:, :], ones_row[:, :], total[:, :], 0.0, ALU.mult, ALU.add))
                step(nc.vector.tensor_tensor(scan[:, :], scan[:, :], total[:, :], ALU.subtract))
                step(nc.vector.tensor_tensor(begin[:, c, :], scan[:, :], same_ps[c][:, 0:T], ALU.add))
            v.sem_inc(begun, 1)
            v.wait_ge(rooted, 1)
            nc.vector.reciprocal(k["dinv"][:, :], degree[:, :])

            def rank_body(i, last=False):
                for r in range(4):
                    t = 4 * i + r
                    if not (last and r >= 2):
                        wait(v, updated, 2 * (t - 1))
                        one_hots(t + 2, (r + 2) % 4, hot2)
                    for c in range(2):
                        wait(v, looked, 2 * t + c + 1)
                        wait(v, ranked, 2 * t + c - 1)
                        if r == 0:
                            wait(v, placed, i)
                        nc.vector.tensor_tensor_reduce(picked[:, c, :], look_ps[c][:, 0:T], one_hi[:, c, r, :], 1.0, 0.0,
                                                       ALU.mult, ALU.add, found[:, c, r:r + 1]).then_inc(ranked, 1)
                    if not (last and r == 3):
                        for c in range(2):
                            wait(v, same, 2 * t + c + 3)
                            nc.vector.tensor_tensor(same16[:, c, (r + 1) % 2, :], same_ps[c][:, 0:P], k["below16"][:, :],
                                                    ALU.mult).then_inc(masked, 1)
                wait(v, ranked, 8 * (i + 1))
                nc.vector.tensor_copy(place[:, :, ds(4 * i, 4)], found[:, :, :]).then_inc(placed, 1)
            one_hots(0, 0, hot2)
            one_hots(1, 1, hot2)
            for c in range(2):
                wait(v, same, c + 1)
                nc.vector.tensor_tensor(same16[:, c, 0, :], same_ps[c][:, 0:P], k["below16"][:, :],
                                        ALU.mult).then_inc(masked, 1)
            rank_body(0)
            with v.Fori(1, G - 1) as i:
                rank_body(i)
            rank_body(G - 1, last=True)
            v.wait_ge(placed, G)
            step(nc.vector.tensor_copy(place_i[:, :, :], place[:, :, :]))
            step(nc.vector.tensor_scalar(row_i[:, :, :], place_i[:, :, :], P - 1, None, ALU.bitwise_and))
            step(nc.vector.tensor_scalar(place_i[:, :, :], place_i[:, :, :], 7, None, ALU.logical_shift_right))
            step(nc.vector.tensor_copy(place[:, :, :], place_i[:, :, :]))
            step(nc.vector.tensor_copy(begin[:, :, :], row_i[:, :, :]))
            step(nc.vector.scalar_tensor_tensor(place[:, :, :], begin[:, :, :], float(T), place[:, :, :], ALU.mult, ALU.add))
            step(nc.vector.tensor_copy(row_i[:, :, :], place[:, :, :]))

            def stage_body(i):
                for par in range(2):
                    g = 2 * i + par
                    wait(v, sent[par], 16 * 2 * J * i)
                    for c in range(2):
                        nc.vector.tensor_copy(idx[:, par, c, :], row_i[:, c, ds(g * J, J)])
                        nc.vector.tensor_copy(out_rows[:, par, c, :, :], fields[c][:, ds(g * J, J), :]).then_inc(staged, 1)
            loop(v, stage_body)

        @block.scalar
        def _(act):
            act.wait_ge(hist, 2)
            nc.scalar.activation(degree[:, :], degree[:, :], ACT.Sqrt).then_inc(rooted, 1)

            def transposed(t_wait, c, slot, free):
                wait(act, turned, t_wait)
                wait(act, updated, free)
                nc.scalar.copy(lo_t16[:, c, slot, :], turn_ps[c][:, 0:P])
                nc.scalar.copy(lo_t[:, c, slot, :], turn_ps[c][:, 0:P]).then_inc(turned_out, 1)

            def running(c, need):
                wait(act, updated, need)
                nc.scalar.copy(table[:, c, :], run_ps[c][:, 0:T]).then_inc(tabled, 1)

            def body(i, last=False):
                for r in range(4):
                    t = 4 * i + r
                    if last and r == 3:
                        continue
                    for c in range(2):
                        transposed(2 * t + c + 3, c, (r + 1) % 2, 2 * t)
                    for c in range(2):
                        running(c, 2 * t + c + 1)
            for c in range(2):
                transposed(c + 1, c, 0, 0)
            act.wait_ge(summed, 3)
            for c in range(2):
                nc.scalar.copy(table[:, c, :], run_ps[c][:, 0:T]).then_inc(tabled, 1)
            body(0)
            with act.Fori(1, G - 1) as i:
                body(i)
            body(G - 1, last=True)

        @block.tensor
        def _(pe):
            def count_body(i, first=False, last=False):
                for r in range(4):
                    for c in range(2):
                        wait(pe, hot, 2 * (4 * i + r) + c + 1)
                        nc.tensor.matmul(run_ps[c][:, 0:T], one_lo[:, c, r, :], one_hi[:, c, r, :],
                                         start=first and r == 0, stop=last and r == 3).then_inc(counted, 1)
            count_body(0, first=True)
            with pe.Fori(1, G - 1) as i:
                count_body(i)
            count_body(G - 1, last=True)
            pe.wait_ge(hist, 2)
            pe.wait_ge(made, 3)
            for c in range(2):
                nc.tensor.matmul(look_ps[c][:, 0:T], k["ones"][:, :], count[:, c, :], start=True, stop=True)
                nc.tensor.matmul(same_ps[c][:, 0:T], k["below"][:, :], count[:, c, :], start=True, stop=True).then_inc(summed, 1)
            pe.wait_ge(begun, 1)
            for c in range(2):
                last = nc.tensor.matmul(run_ps[c][:, 0:T], k["ident"][:, :], begin[:, c, :], start=True, stop=True)
            last.then_inc(summed, 1)

            def turn(slot, need, free):
                for c in range(2):
                    wait(pe, hot2, need + c)
                    wait(pe, turned_out, free)
                    nc.tensor.transpose(turn_ps[c][:, 0:P], one_lo[:, c, slot, :], k["ident16"][:, :]).then_inc(turned, 1)

            def alike(slot, need, free):
                for c in range(2):
                    wait(pe, turned_out, need + c)
                    wait(pe, masked, free)
                    nc.tensor.matmul(same_ps[c][:, 0:P], lo_t16[:, c, slot, :], lo_t16[:, c, slot, :],
                                     start=True, stop=True).then_inc(same, 1)

            def body(i, last=False):
                for r in range(4):
                    t = 4 * i + r
                    more = not (last and r == 3)
                    if more:
                        turn((r + 1) % 4, 2 * t + 3, 2 * t + 2)
                    for c in range(2):
                        wait(pe, tabled, 2 * t + c + 1)
                        wait(pe, masked, 2 * t + c + 1)
                        wait(pe, ranked, 2 * (t - 1) + c + 1)
                        nc.tensor.matmul(look_ps[c][:, 0:T], lo_t[:, c, r % 2, :], table[:, c, :], start=True, stop=False)
                        nc.tensor.matmul(look_ps[c][:, 0:T], same16[:, c, r % 2, :], one_hi[:, c, r, :],
                                         start=False, stop=True).then_inc(looked, 1)
                        nc.tensor.matmul(run_ps[c][:, 0:T], one_lo[:, c, r, :], one_hi[:, c, r, :],
                                         start=False, stop=True, skip_group_check=True).then_inc(updated, 1)
                    if more:
                        alike((r + 1) % 2, 2 * t + 3, 2 * t + 2)
            turn(0, 1, 0)
            alike(0, 1, 0)
            body(0)
            with pe.Fori(1, G - 1) as i:
                body(i)
            body(G - 1, last=True)


def order_tables(nc, k, d):
    H = T // J
    with nc.cleanup_on_exit(), ExitStack() as ctx:
        ph = Phase(nc, ctx)
        sb, ps, sem = ph.sb, ph.ps, ph.sem
        ZC = 28 * P
        fields = [sb("fields0", [P, T, 8]), sb("fields1", [P, T, 8])]
        zeros = sb("zeros", [P, 32 * (P + 1)])
        minus = sb("minus", [1, 1])
        turned_sb = sb("turned_sb", [H, J, P])
        after = sb("after", [H, J, P])
        differs = sb("differs", [H, J, P])
        target = sb("target", [P, T])
        turn_ps = ps("turn", [H, 512])
        back_ps = ps("back", [P, 512])
        loaded, made, ready, stored, cleared = sem("loaded"), sem("made"), sem("ready"), sem("stored"), sem("cleared")
        cut, turned, copied, lined, read, compared, back = (sem(n) for n in
                                                            ("cut", "turned", "copied", "lined", "read", "compared", "back"))
        block = ctx.enter_context(nc.Block())

        def line_blocks(c, shift):
            return d["line_" + c][shift:NP + shift].rearrange("(b r e) -> r b e", r=H, e=P)

        @block.sync
        def _(sp):
            for n, c in enumerate("rs"):
                sp.dma_start(fields[n][:, :, :], d["sorted_" + c].rearrange("(p t) f -> p t f", t=T)).then_inc(loaded, 16)
            sp.wait_ge(made, 2)
            for c in "rs":
                sp.dma_start(d["line_" + c][NP:NP + 1].rearrange("(a b) -> a b", a=1), minus[:, :]).then_inc(stored, 16)
            for n, c in enumerate("rs"):
                sp.wait_ge(copied, n + 1)
                sp.dma_start(line_blocks(c, 0), turned_sb[:, :, :]).then_inc(lined, 16)
                sp.wait_ge(lined, 16 * (n + 1))
                sp.wait_ge(stored, 32)
                sp.dma_start(after[:, :, :], line_blocks(c, 1)).then_inc(read, 16)

        @block.scalar
        def _(act):
            act.wait_ge(made, 2)
            sums = (("sum_r", T * P, 28 * P), ("sum_s", T * (P + 1), 28 * (P + 1)))
            for name, width, step in sums:
                flat = d[name].rearrange("(p t) d -> p (t d)", p=P)
                for at in range(0, width, step):
                    act.dma_start(flat[:, at:at + step], zeros[:, 0:step]).then_inc(cleared, 16)
            act.wait_ge(cleared, 16 * 2 * (T // 28))

        @block.tensor
        def _(pe):
            for n, c in enumerate("rs"):
                pe.wait_ge(cut, n + 1)
                for b in range(J):
                    last = nc.tensor.transpose(turn_ps[:, b * P:(b + 1) * P], k["key_" + c][:, b * H:(b + 1) * H], k["ident"][:, :])
                last.then_inc(turned, 1)
                pe.wait_ge(compared, n + 1)
                for b in range(J):
                    last = nc.tensor.transpose(back_ps[:, b * H:(b + 1) * H], differs[:, b, :], k["ident"][0:H, 0:H])
                last.then_inc(back, 1)

        @block.vector
        def _(v):
            steps = [0]

            def step(ins):
                steps[0] += 1
                ins.then_inc(ready, 1)
                v.wait_ge(ready, steps[0])

            nc.vector.memset(zeros[:, :], 0.0).then_inc(made, 1)
            nc.vector.memset(minus[:, :], -1.0).then_inc(made, 1)
            v.wait_ge(loaded, 32)
            for n, c in enumerate("rs"):
                nc.vector.tensor_copy(k["key_" + c][:, :], fields[n][:, :, 0]).then_inc(cut, 1)
                nc.vector.tensor_copy(k["from_" + c][:, :], fields[n][:, :, 1])
                nc.vector.tensor_copy(k["weight_" + c][:, :], fields[n][:, :, 3])
            nc.vector.tensor_copy(k["edge_r"][:, :], fields[0][:, :, 2])
            nc.vector.tensor_copy(k["vec_r"][:, :, :], fields[0][:, :, 4:7])
            for n, c in enumerate("rs"):
                v.wait_ge(cut, n + 1)
                step(nc.vector.memset(k["before_" + c][:, :], -1.0))
                step(nc.vector.tensor_scalar(target[:, 1:T], k["key_" + c][:, 0:T - 1], 1.0, k["ident"][:, P - 1:P],
                                             ALU.add, ALU.mult))
                step(nc.vector.tensor_scalar(k["before_" + c][:, 1:T], target[:, 1:T], -1.0, None, ALU.add))
                v.wait_ge(turned, n + 1)
                if n:
                    v.wait_ge(lined, 16)
                step(nc.vector.tensor_copy(turned_sb[:, :, :], turn_ps[:, :].rearrange("r (b e) -> r b e", b=J)))
                v.sem_inc(copied, 1)
                v.wait_ge(read, 16 * (n + 1))
                if n:
                    v.wait_ge(back, 1)
                nc.vector.tensor_tensor(differs[:, :, :], turned_sb[:, :, :], after[:, :, :], ALU.not_equal).then_inc(compared, 1)
                v.wait_ge(back, n + 1)
                step(nc.vector.tensor_scalar(target[:, :], back_ps[:, 0:T], -float(SKIP), float(SKIP), ALU.mult, ALU.add))
                step(nc.vector.tensor_tensor(target[:, :], target[:, :], k["key_" + c][:, :], ALU.add))
                step(nc.vector.tensor_copy(k["to_" + c][:, :], target[:, :]))


def segment_sum(nc, k, c, sums, width=P, table=None, messages=None, added=None, weight=None):
    with nc.cleanup_on_exit(), ExitStack() as ctx:
        ph = Phase(nc, ctx)
        sb, ps, sem = ph.sb, ph.ps, ph.sem
        key, before, to, source = (k[n + c] for n in ("key_", "before_", "to_", "from_"))
        rows = sb("rows", [P, 2, J, width])
        plus = sb("plus", [P, 2, W]) if added is not None else None
        relu = sb("relu", [P, 2, J, P]) if added is not None else None
        line = sb("line", [P, 2, W])
        equal = sb("equal", [P, 2, J, P])
        carry = sb("carry", [P, 2, J, P])
        sum_sb = sb("sum_sb", [P, 2, J, width])
        idx = sb("idx", [P, 2, J], I32)
        to_idx = sb("to_idx", [P, 2, J], I32)
        sum_ps = [ps(f"sum{n}", [P, 512]) for n in range(2 * J)]
        came = [sem("came0"), sem("came1")]
        lined = [sem("lined0"), sem("lined1")]
        plussed = [sem("plussed0"), sem("plussed1")]
        sent = [sem("sent0"), sem("sent1")]
        staged, to_staged, built, summed, taken = (sem(n) for n in ("staged", "to_staged", "built", "summed", "taken"))
        both, ready, ones_in, passed, passed_sp = (sem(n) for n in ("both", "ready", "ones_in", "passed", "passed_sp"))
        block = ctx.enter_context(nc.Block())
        line_rows = k["line"][c][0:NP].rearrange("(g w) -> g w", w=W)
        source_rows = relu if added is not None else rows

        def psum(par, j):
            return sum_ps[J * par + j][:, 0:width]

        @block.sync
        def _(sp):
            def body(i):
                for par in range(2):
                    g = 2 * i + par
                    wait(sp, built, g - 1, passed_sp)
                    sp.dma_start(line[:, par, :], line_rows[ds(g), :].to_broadcast([P, W])).then_inc(lined[par], 16)
                    if added is not None:
                        wait(sp, ready, g - 1, passed_sp)
                        sp.dma_start(plus[:, par, :], block_of(added, g)).then_inc(plussed[par], 16)
                    if messages is not None:
                        wait(sp, summed, J * (g - 1), passed_sp)
                        sp.dma_start(rows[:, par, :, :].rearrange("p j d -> p (j d)"), block_of(messages, g)).then_inc(came[par], 16)
            loop(sp, body)

        @block.gpsimd
        def _(pool):
            def gather(g, par, i):
                wait(pool, staged, g + 1, passed)
                wait(pool, summed, J * (g - 1), passed)
                for j in range(J):
                    nc.gpsimd.indirect_dma_start(rows[:, par, j, 0:P], None, table,
                                                 bass.IndirectOffsetOnAxis(ap=idx[:, par, j:j + 1], axis=0)).then_inc(came[par], 16)

            def scatter(g, par):
                wait(pool, to_staged, g + 1, passed)
                wait(pool, taken, J * (g + 1), passed)
                for j in range(J):
                    nc.gpsimd.indirect_dma_start(sums, bass.IndirectOffsetOnAxis(ap=to_idx[:, par, j:j + 1], axis=0),
                                                 sum_sb[:, par, j, :], None, bounds_check=NP - 1,
                                                 oob_is_err=False).then_inc(sent[par], 16)

            def body(i, last=False):
                for par in range(2):
                    g = 2 * i + par
                    if table is not None and not (last and par == 1):
                        gather(g + 1, 1 - par, i)
                    scatter(g, par)
            if width > P:
                nc.gpsimd.memset(rows[:, :, :, P:width], 1.0).then_inc(ones_in, 1)
            if table is not None:
                gather(0, 0, 0)
            body(0)
            with pool.Fori(1, G // 2 - 1) as i:
                body(i)
            body(G // 2 - 1, last=True)
            for par in range(2):
                pool.wait_ge(sent[par], 16 * J * (G // 2))

        @block.scalar
        def _(act):
            def body(i):
                for par in range(2):
                    g = 2 * i + par
                    if table is not None:
                        wait(act, came[par], 16 * J * i)
                        nc.scalar.copy(idx[:, par, :], source[:, ds(g * J, J)]).then_inc(staged, 1)
                    wait(act, sent[par], 16 * J * i)
                    nc.scalar.copy(to_idx[:, par, :], to[:, ds(g * J, J)]).then_inc(to_staged, 1)
                    if added is not None:
                        wait(act, both, g + 1)
                        wait(act, summed, J * (g - 1))
                        nc.scalar.activation(relu[:, par, :, :].rearrange("p j d -> p (j d)"), plus[:, par, :], ACT.Relu).then_inc(ready, 1)
                    for j in range(J):
                        wait(act, summed, J * g + j + 1)
                        nc.scalar.copy(sum_sb[:, par, j, :], psum(par, j)).then_inc(taken, 1)
            loop(act, body)

        @block.vector
        def _(v):
            def body(i):
                for par in range(2):
                    g = 2 * i + par
                    wait(v, lined[par], 16 * (i + 1))
                    wait(v, summed, J * (g - 1))
                    for j in range(J):
                        t = g * J + j
                        row = line[:, par, j * P:(j + 1) * P]
                        if weight is None:
                            nc.vector.tensor_scalar(equal[:, par, j, :], row, key[:, ds(t)], None, ALU.is_equal)
                        else:
                            nc.vector.tensor_scalar(equal[:, par, j, :], row, key[:, ds(t)], weight[:, ds(t)],
                                                    ALU.is_equal, ALU.mult)
                        last = nc.vector.tensor_scalar(carry[:, par, j, :], row, before[:, ds(t)], None, ALU.is_equal)
                    last.then_inc(built, 1)
                    if added is not None:
                        wait(v, came[par], 16 * J * (i + 1))
                        wait(v, plussed[par], 16 * (i + 1))
                        nc.vector.tensor_tensor(plus[:, par, :], plus[:, par, :], rows[:, par, :, :].rearrange("p j d -> p (j d)"),
                                                ALU.add).then_inc(both, 1)
            loop(v, body)

        @block.tensor
        def _(pe):
            def body(i, first=False):
                for par in range(2):
                    g = 2 * i + par
                    wait(pe, built, g + 1)
                    if added is not None:
                        wait(pe, ready, g + 1)
                    else:
                        wait(pe, came[par], 16 * (J if table is not None else 1) * (i + 1))
                    wait(pe, taken, J * (g - 1))
                    for j in range(J):
                        end = first and par == 0 and j == 0
                        m = nc.tensor.matmul(psum(par, j), equal[:, par, j, :], source_rows[:, par, j, :], start=True, stop=end)
                        if end:
                            m.then_inc(summed, 1)
                            continue
                        wait(pe, taken, J * g + j)
                        before_sb = sum_sb[:, par, j - 1, :] if j else sum_sb[:, 1 - par, J - 1, :]
                        nc.tensor.matmul(psum(par, j), carry[:, par, j, :], before_sb, start=False, stop=True).then_inc(summed, 1)
            if width > P:
                pe.wait_ge(ones_in, 1)
            body(0, first=True)
            with pe.Fori(1, G // 2 - 1) as i:
                body(i)
            body(G // 2 - 1)


def tensor_product_weights(nc, k, w, ctx):
    t = {n: ctx.enter_context(nc.sbuf_tensor("tp_" + n, s, F32)) for n, s in {
        "up": [P, P], "mlp0": [J * NB, J, HID], "mlp1": [HID, HID], "mlp2": [HID, P], "mb0": [HID, 1], "mb1": [HID, 1],
        "mb2": [1, P], "out": [P, 2, P], "basis": [P, T, NB], "unit": [P, T, 3], "dir": [P, T, 3]}.items()}
    with nc.cleanup_on_exit(), ExitStack() as inner:
        ph = Phase(nc, inner)
        sb, sem = ph.sb, ph.sem
        up1 = sb("up1", [P, MUL])
        out0 = sb("out0", [2 * MUL, MUL])
        out1 = sb("out1", [P, 2, MUL])
        centre_i = sb("centre_i", [P, NB], I32)
        centre = sb("centre", [P, NB])
        clipped = sb("clipped", [P, T])
        away = sb("away", [P, T, NB])
        square = sb("square", [P, T, 3])
        length = sb("length", [P, T])
        cleared, loaded, ready, numbered, away_in, rooted, squared, waved = (sem(n) for n in (
            "cleared", "loaded", "ready", "numbered", "away_in", "rooted", "squared", "waved"))
        block = inner.enter_context(nc.Block())

        @block.sync
        def _(sp):
            sp.wait_ge(cleared, 3)
            sp.dma_start(t["up"][0:MUL, 0:MUL], w["W_up0"]).then_inc(loaded, 16)
            for c in range(3):
                sp.dma_start(t["up"][MUL + c:P:3, MUL * (c + 1):MUL * (c + 2)], w["W_up1"]).then_inc(loaded, 16)
            for j in range(J):
                sp.dma_start(t["mlp0"][j * NB:(j + 1) * NB, j, :], w["mlp_w0"]).then_inc(loaded, 16)
            sp.dma_start(t["mlp1"][:, :], w["mlp_w1"]).then_inc(loaded, 16)
            sp.dma_start(t["mlp2"][:, :], w["mlp_w2"]).then_inc(loaded, 16)
            sp.dma_start(t["mb0"][:, :], w["mlp_b0"].rearrange("(n a) -> n a", a=1)).then_inc(loaded, 16)
            sp.dma_start(t["mb1"][:, :], w["mlp_b1"].rearrange("(n a) -> n a", a=1)).then_inc(loaded, 16)
            sp.dma_start(t["mb2"][:, :], w["mlp_b2"].rearrange("(a n) -> a n", a=1)).then_inc(loaded, 16)
            sp.dma_start(t["out"][0:2 * MUL, 0, 0:MUL], w["W_out0"]).then_inc(loaded, 16)
            for half in range(2):
                sp.dma_start(out1[half * 2 * MUL:(half + 1) * 2 * MUL, 0, :], w["W_out1"]).then_inc(loaded, 16)

        @block.gpsimd
        def _(pool):
            nc.gpsimd.iota(centre_i[:, :], pattern=[[1, NB]], base=0, channel_multiplier=0).then_inc(numbered, 1)

        @block.scalar
        def _(act):
            act.wait_ge(squared, 1)
            nc.scalar.activation(length[:, :], length[:, :], ACT.Sqrt).then_inc(rooted, 1)
            act.wait_ge(away_in, 1)
            nc.scalar.activation(t["basis"][:, :, :], away[:, :, :], ACT.Exp, scale=-0.5 * (NB - 1) ** 2).then_inc(waved, 1)

        @block.vector
        def _(v):
            steps = [0]

            def step(ins):
                steps[0] += 1
                ins.then_inc(ready, 1)
                v.wait_ge(ready, steps[0])

            for name in ("up", "mlp0", "out"):
                tile = t[name]
                nc.vector.memset(tile[:, :] if name == "up" else tile[:, :, :], 0.0).then_inc(cleared, 1)
            step(nc.vector.tensor_tensor(square[:, :, :], k["vec_r"][:, :, :], k["vec_r"][:, :, :], ALU.mult))
            step(nc.vector.tensor_tensor(length[:, :], square[:, :, 0], square[:, :, 1], ALU.add))
            nc.vector.tensor_tensor(length[:, :], length[:, :], square[:, :, 2], ALU.add).then_inc(squared, 1)
            weight = k["weight_r"]
            v.wait_ge(numbered, 1)
            step(nc.vector.tensor_copy(centre[:, :], centre_i[:, :]))
            step(nc.vector.tensor_scalar(centre[:, :], centre[:, :], 1.0 / (NB - 1), None, ALU.mult))
            step(nc.vector.tensor_scalar(clipped[:, :], weight[:, :], 0.0, 1.0, ALU.max, ALU.min))
            step(nc.vector.tensor_tensor(away[:, :, :], clipped[:, :].unsqueeze(2).to_broadcast([P, T, NB]),
                                         centre[:, :].unsqueeze(1).to_broadcast([P, T, NB]), ALU.subtract))
            nc.vector.tensor_tensor(away[:, :, :], away[:, :, :], away[:, :, :], ALU.mult).then_inc(away_in, 1)
            v.wait_ge(rooted, 1)
            step(nc.vector.tensor_scalar(length[:, :], length[:, :], 1e-12, None, ALU.add))
            step(nc.vector.reciprocal(length[:, :], length[:, :]))
            step(nc.vector.tensor_tensor(t["unit"][:, :, :], k["vec_r"][:, :, :],
                                         length[:, :].unsqueeze(2).to_broadcast([P, T, 3]), ALU.mult))
            step(nc.vector.tensor_scalar(t["dir"][:, :, :], t["unit"][:, :, :], 3.0 ** 0.5, None, ALU.mult))
            step(nc.vector.tensor_scalar(clipped[:, :], weight[:, :], 1.0, NB ** 0.5, ALU.is_le, ALU.mult))
            v.wait_ge(waved, 1)
            nc.vector.tensor_tensor(t["basis"][:, :, :], t["basis"][:, :, :],
                                    clipped[:, :].unsqueeze(2).to_broadcast([P, T, NB]), ALU.mult)
            v.wait_ge(loaded, 16 * 16)
            nc.vector.tensor_scalar(t["up"][:, :], t["up"][:, :], MUL ** -0.5, None, ALU.mult)
            scale = (2 * MUL) ** -0.5 / AVG
            nc.vector.tensor_scalar(t["out"][0:2 * MUL, 0, 0:MUL], t["out"][0:2 * MUL, 0, 0:MUL], scale, None, ALU.mult)
            for c in range(3):
                half, at = (c + 1) % 2, (c + 1) // 2
                rows = slice(half * 2 * MUL, (half + 1) * 2 * MUL)
                nc.vector.tensor_scalar(t["out"][rows, at, MUL + c:P:3], out1[rows, 0, :], scale, None, ALU.mult)
    return t


def edge_products(nc, k, x, t, messages):
    with nc.cleanup_on_exit(), ExitStack() as ctx:
        ph = Phase(nc, ctx)
        sb, ps, sem = ph.sb, ph.ps, ph.sem
        rows = sb("rows", [P, 2, J, P])
        idx = sb("idx", [P, 2, J], I32)
        wave = sb("wave", [P, J * NB])
        wave_t = sb("wave_t", [J * NB, P])
        rows_t = sb("rows_t", [P, W])
        hid0 = sb("hid0", [HID, W])
        hid1 = sb("hid1", [HID, W])
        gate = sb("gate", [P, J, P])
        mixed = sb("mixed", [P, J, 2 * P])
        along = sb("along", [P, J, MUL])
        part = sb("part", [P, 3, J, MUL])
        dot = sb("dot", [P, J, MUL])
        mixed_t = sb("mixed_t", [P, 2, W])
        out = sb("out", [P, 2, W])
        wave_ps = ps("wave", [J * NB, 512])
        turn_ps = ps("turn", [P, 512])
        up_ps = ps("up", [P, J, P])
        hid_ps = ps("hid", [HID, 512])
        gate_ps = ps("gate", [P, J, P])
        mix_ps = [ps("mix0", [P, 512]), ps("mix1", [P, 512])]
        out_ps = ps("out", [P, 512])
        came = [sem("came0"), sem("came1")]
        stored = [sem("stored0"), sem("stored1")]
        (staged, waved, wave_up, wave_down, turned, rows_down, upped, hid_up, hid_down, gated, gate_down,
         scaled, dots, mixed_in, mixed_up, mixed_down, made, out_down, passed, passed_sp, passed_pe) = (sem(n) for n in (
            "staged", "waved", "wave_up", "wave_down", "turned", "rows_down", "upped", "hid_up", "hid_down", "gated",
            "gate_down", "scaled", "dots", "mixed_in", "mixed_up", "mixed_down", "made", "out_down", "passed", "passed_sp", "passed_pe"))
        block = ctx.enter_context(nc.Block())

        @block.gpsimd
        def _(pool):
            def body(i):
                for par in range(2):
                    g = 2 * i + par
                    wait(pool, staged, g + 1, passed)
                    wait(pool, turned, g - 1, passed)
                    for j in range(J):
                        nc.gpsimd.indirect_dma_start(rows[:, par, j, :], None, x,
                                                     bass.IndirectOffsetOnAxis(ap=idx[:, par, j:j + 1], axis=0)).then_inc(came[par], 16)
            loop(pool, body)

        @block.sync
        def _(sp):
            def body(i):
                for par in range(2):
                    g = 2 * i + par
                    wait(sp, out_down, g + 1, passed_sp)
                    sp.dma_start(block_of(messages, g), out[:, par, :]).then_inc(stored[par], 16)
            loop(sp, body)
            for par in range(2):
                sp.wait_ge(stored[par], 16 * (G // 2))

        @block.scalar
        def _(act):
            def body(i):
                for par in range(2):
                    g = 2 * i + par
                    wait(act, came[par], 16 * J * i)
                    nc.scalar.copy(idx[:, par, :], k["from_r"][:, ds(g * J, J)]).then_inc(staged, 1)
                    wait(act, wave_up, g)
                    nc.scalar.copy(wave[:, :], t["basis"][:, ds(g * J, J), :].rearrange("p t n -> p (t n)")).then_inc(waved, 1)
                    wait(act, wave_up, g + 1)
                    wait(act, hid_up, 2 * g)
                    nc.scalar.copy(wave_t[:, :], wave_ps[:, 0:P]).then_inc(wave_down, 1)
                    wait(act, turned, g + 1)
                    wait(act, upped, g)
                    nc.scalar.copy(rows_t[:, :], turn_ps[:, :]).then_inc(rows_down, 1)
                    wait(act, hid_up, 2 * g + 1)
                    nc.scalar.activation(hid0[:, :], hid_ps[:, :], ACT.Silu, bias=t["mb0"][:, :]).then_inc(hid_down, 1)
                    wait(act, hid_up, 2 * g + 2)
                    wait(act, gated, g)
                    nc.scalar.activation(hid1[:, :], hid_ps[:, :], ACT.Silu, bias=t["mb1"][:, :]).then_inc(hid_down, 1)
                    wait(act, gated, g + 1)
                    wait(act, scaled, g)
                    nc.scalar.copy(gate[:, :, :], gate_ps[:, :, :]).then_inc(gate_down, 1)
                    wait(act, mixed_up, 2 * g + 2)
                    wait(act, made, g)
                    nc.scalar.copy(mixed_t[:, 1, :], mix_ps[1][:, :]).then_inc(mixed_down, 1)
                    wait(act, made, g + 1)
                    wait(act, stored[par], 16 * i)
                    nc.scalar.copy(out[:, par, :], out_ps[:, :]).then_inc(out_down, 1)
            loop(act, body)

        @block.vector
        def _(v):
            def body(i):
                for par in range(2):
                    g = 2 * i + par
                    wait(v, gate_down, g + 1)
                    wait(v, upped, g + 1)
                    wait(v, mixed_up, 2 * g)
                    up = up_ps[:, :, :]
                    unit, along_dir = (t[n][:, ds(g * J, J), :] for n in ("unit", "dir"))
                    nc.vector.tensor_tensor(along[:, :, :], gate[:, :, MUL:2 * MUL], up[:, :, 0:MUL], ALU.mult)
                    for c in range(3):
                        last = nc.vector.tensor_tensor(part[:, c, :, :], up[:, :, MUL * (c + 1):MUL * (c + 2)],
                                                       unit[:, :, c:c + 1].to_broadcast([P, J, MUL]), ALU.mult)
                    last.then_inc(dots, 1)
                    nc.vector.tensor_tensor(mixed[:, :, 0:MUL], gate[:, :, 0:MUL], up[:, :, 0:MUL], ALU.mult)
                    for c in range(3):
                        at = 2 * MUL * (c + 1)
                        nc.vector.tensor_tensor(mixed[:, :, at + MUL:at + 2 * MUL], gate[:, :, 2 * MUL:3 * MUL],
                                                up[:, :, MUL * (c + 1):MUL * (c + 2)], ALU.mult)
                    wait(v, dots, 3 * g + 1)
                    nc.vector.tensor_tensor(dot[:, :, :], part[:, 0, :, :], part[:, 1, :, :], ALU.add).then_inc(dots, 1)
                    for c in range(3):
                        at = 2 * MUL * (c + 1)
                        nc.vector.tensor_tensor(mixed[:, :, at:at + MUL], along[:, :, :],
                                                along_dir[:, :, c:c + 1].to_broadcast([P, J, MUL]), ALU.mult)
                    wait(v, dots, 3 * g + 2)
                    nc.vector.tensor_tensor(part[:, 0, :, :], dot[:, :, :], part[:, 2, :, :], ALU.add).then_inc(dots, 1)
                    wait(v, dots, 3 * g + 3)
                    nc.vector.tensor_tensor(mixed[:, :, MUL:2 * MUL], part[:, 0, :, :], gate[:, :, 3 * MUL:4 * MUL],
                                            ALU.mult).then_inc(scaled, 1)
                    wait(v, mixed_up, 2 * g + 1)
                    wait(v, made, g)
                    nc.vector.tensor_copy(mixed_t[:, 0, :], mix_ps[0][:, :]).then_inc(mixed_down, 1)
            loop(v, body)

        @block.tensor
        def _(pe):
            def body(i):
                for par in range(2):
                    g = 2 * i + par
                    wait(pe, waved, g + 1)
                    wait(pe, wave_down, g)
                    nc.tensor.transpose(wave_ps[:, 0:P], wave[:, :], k["ident"][:, :]).then_inc(wave_up, 1)
                    wait(pe, came[par], 16 * J * (i + 1))
                    wait(pe, rows_down, g)
                    for j in range(J):
                        m = nc.tensor.transpose(turn_ps[:, j * P:(j + 1) * P], rows[:, par, j, :], k["ident"][:, :])
                    m.then_inc(turned, 1)
                    wait(pe, wave_down, g + 1)
                    wait(pe, hid_down, 2 * g)
                    for j in range(J):
                        m = nc.tensor.matmul(hid_ps[:, j * P:(j + 1) * P], t["mlp0"][:, j, :], wave_t[:, :], start=True, stop=True)
                    m.then_inc(hid_up, 1)
                    wait(pe, rows_down, g + 1)
                    wait(pe, scaled, g)
                    for j in range(J):
                        m = nc.tensor.matmul(up_ps[:, j, :], rows_t[:, j * P:(j + 1) * P], t["up"][:, :], start=True, stop=True)
                    m.then_inc(upped, 1)
                    wait(pe, hid_down, 2 * g + 1, passed_pe)
                    nc.tensor.matmul(hid_ps[:, :], t["mlp1"][:, :], hid0[:, :], start=True, stop=True).then_inc(hid_up, 1)
                    wait(pe, hid_down, 2 * g + 2)
                    wait(pe, gate_down, g)
                    for j in range(J):
                        nc.tensor.matmul(gate_ps[:, j, :], hid1[:, j * P:(j + 1) * P], t["mlp2"][:, :], start=True, stop=False)
                        m = nc.tensor.matmul(gate_ps[:, j, :], k["one_row"][:, :], t["mb2"][:, :], start=False, stop=True)
                    m.then_inc(gated, 1)
                    wait(pe, scaled, g + 1)
                    wait(pe, mixed_down, 2 * g)
                    for h in range(2):
                        for j in range(J):
                            m = nc.tensor.transpose(mix_ps[h][:, j * P:(j + 1) * P], mixed[:, j, h * P:(h + 1) * P], k["ident"][:, :])
                        m.then_inc(mixed_up, 1)
                    wait(pe, mixed_down, 2 * g + 2)
                    wait(pe, out_down, g)
                    for j in range(J):
                        for h in range(2):
                            m = nc.tensor.matmul(out_ps[:, j * P:(j + 1) * P], mixed_t[:, h, j * P:(j + 1) * P], t["out"][:, h, :],
                                                 start=h == 0, stop=h == 1)
                    m.then_inc(made, 1)
            loop(pe, body)


def load_weights(nc, k, ctx, w):
    shapes = {"W1": [P, P], "R1": [P, P], "W2": [P, P], "R2": [P, P], "W3Wh": [P, P], "bh": [1, P], "lin_t": [P, P],
              "lin_b": [1, P], "atom": [P, P], "atom_b": [1, P], "bond": [P, P], "bond_b": [1, P],
              "gin1": [P, LAYERS, 2 * P], "gin2": [P, LAYERS, 2, P], "final": [P, P], "final_b": [1, P],
              "eps_row": [P, LAYERS], "b1": [P, LAYERS, 2], "g1": [P, LAYERS, 2], "be1": [P, LAYERS, 2],
              "b2": [P, LAYERS], "gn": [P, LAYERS], "bet": [P, LAYERS]}
    m = {n: ctx.enter_context(nc.sbuf_tensor("w_" + n, s, F32)) for n, s in shapes.items()}

    def row(a):
        return a.rearrange("(a n) -> a n", a=1)

    loads = [(m["W1"][:, :], w["L1_gnn_W1"]), (m["R1"][:, :], w["L1_gnn_R1"]), (m["W2"][:, :], w["L1_gnn_W2"]),
             (m["R2"][:, :], w["L1_gnn_R2"]), (m["bh"][:, :], row(w["L1_gnn_bh"])), (m["lin_b"][:, :], row(w["L2_gnn_b"])),
             (m["atom"][:, :], w["L3_gnn_W_atom"]), (m["atom_b"][:, :], row(w["L3_gnn_b_atom"])),
             (m["bond"][:, :], w["L3_gnn_W_bond"]), (m["bond_b"][:, :], row(w["L3_gnn_b_bond"])),
             (m["final"][:, :], w["L3_gnn_W_out"]), (m["final_b"][:, :], row(w["L3_gnn_b_out"])),
             (m["eps_row"][:, :], row(w["L3_gnn_eps"]).to_broadcast([P, LAYERS]))]
    for i in range(LAYERS):
        loads.append((m["gin1"][:, i, :], w["L3_gnn_W1"][i]))
        for h in range(2):
            loads.append((m["gin2"][:, i, h, :], w["L3_gnn_W2"][i, h * P:(h + 1) * P, :]))
            for n in ("b1", "g1", "be1"):
                loads.append((m[n][:, i, h:h + 1], w["L3_gnn_" + n][i, h * P:(h + 1) * P].rearrange("(p a) -> p a", a=1)))
        for n in ("b2", "gn", "bet"):
            loads.append((m[n][:, i:i + 1], w["L3_gnn_" + n][i].rearrange("(p a) -> p a", a=1)))
    with nc.cleanup_on_exit(), ExitStack() as inner:
        ph = Phase(nc, inner)
        w3, wh, lin, w3t = (ph.sb(n, [P, P]) for n in ("w3", "wh", "lin", "w3t"))
        turn_ps, lin_ps, product_ps = (ph.ps(n, [P, 512]) for n in ("turn", "lin", "product"))
        loaded, turned, copied, multiplied = (ph.sem(n) for n in ("loaded", "turned", "copied", "multiplied"))
        loads += [(w3[:, :], w["L1_gnn_W3"]), (wh[:, :], w["L1_gnn_Wh"]), (lin[:, :], w["L2_gnn_W"])]
        block = inner.enter_context(nc.Block())

        @block.sync
        def _(sp):
            for to, of in loads:
                sp.dma_start(to, of).then_inc(loaded, 16)

        @block.tensor
        def _(pe):
            pe.wait_ge(loaded, 16 * len(loads))
            nc.tensor.transpose(turn_ps[:, 0:P], w3[:, :], k["ident"][:, :]).then_inc(turned, 1)
            nc.tensor.transpose(lin_ps[:, 0:P], lin[:, :], k["ident"][:, :]).then_inc(turned, 1)
            pe.wait_ge(copied, 1)
            nc.tensor.matmul(product_ps[:, 0:P], w3t[:, :], wh[:, :], start=True, stop=True).then_inc(multiplied, 1)

        @block.vector
        def _(v):
            v.wait_ge(loaded, 16 * len(loads))
            nc.vector.tensor_scalar(m["eps_row"][:, :], m["eps_row"][:, :], 1.0, None, ALU.add)
            v.wait_ge(turned, 1)
            nc.vector.tensor_copy(w3t[:, :], turn_ps[:, 0:P]).then_inc(copied, 1)
            v.wait_ge(turned, 2)
            nc.vector.tensor_copy(m["lin_t"][:, :], lin_ps[:, 0:P])
            v.wait_ge(multiplied, 1)
            nc.vector.tensor_copy(m["W3Wh"][:, :], product_ps[:, 0:P])
    return m


def bond_rows(nc, k, edge_attr, m, bonds):
    with nc.cleanup_on_exit(), ExitStack() as ctx:
        ph = Phase(nc, ctx)
        sb, ps, sem = ph.sb, ph.ps, ph.sem
        rows = sb("rows", [P, 2, J, P])
        idx = sb("idx", [P, 2, J], I32)
        rows_t = sb("rows_t", [P, 2, W])
        out = sb("out", [P, 2, W])
        turn_ps = [ps("turn0", [P, 512]), ps("turn1", [P, 512])]
        out_ps = [ps("out0", [P, 512]), ps("out1", [P, 512])]
        came = [sem("came0"), sem("came1")]
        stored = [sem("stored0"), sem("stored1")]
        staged, turned, rows_down, made, out_down, passed, passed_sp = (sem(n) for n in (
            "staged", "turned", "rows_down", "made", "out_down", "passed", "passed_sp"))
        block = ctx.enter_context(nc.Block())

        @block.gpsimd
        def _(pool):
            def body(i):
                for par in range(2):
                    g = 2 * i + par
                    wait(pool, staged, g + 1, passed)
                    wait(pool, turned, g - 1, passed)
                    for j in range(J):
                        nc.gpsimd.indirect_dma_start(rows[:, par, j, :], None, edge_attr,
                                                     bass.IndirectOffsetOnAxis(ap=idx[:, par, j:j + 1], axis=0)).then_inc(came[par], 16)
            loop(pool, body)

        @block.sync
        def _(sp):
            def body(i):
                for par in range(2):
                    g = 2 * i + par
                    wait(sp, out_down, g + 1, passed_sp)
                    sp.dma_start(block_of(bonds, g), out[:, par, :]).then_inc(stored[par], 16)
            loop(sp, body)
            for par in range(2):
                sp.wait_ge(stored[par], 16 * (G // 2))

        @block.scalar
        def _(act):
            def body(i):
                for par in range(2):
                    g = 2 * i + par
                    wait(act, turned, g + 1)
                    wait(act, made, g - 1)
                    nc.scalar.copy(rows_t[:, par, :], turn_ps[par][:, :]).then_inc(rows_down, 1)
            loop(act, body)

        @block.vector
        def _(v):
            def body(i):
                for par in range(2):
                    g = 2 * i + par
                    wait(v, came[par], 16 * J * i)
                    nc.vector.tensor_copy(idx[:, par, :], k["edge_r"][:, ds(g * J, J)]).then_inc(staged, 1)
                    wait(v, made, g)
                    if par or not isinstance(i, int) or i:
                        before = 1 - par
                        wait(v, stored[before], 16 * (i if par else i - 1))
                        nc.vector.tensor_copy(out[:, before, :], out_ps[before][:, :]).then_inc(out_down, 1)
            loop(v, body)
            v.wait_ge(made, G)
            v.wait_ge(stored[1], 16 * (G // 2 - 1))
            nc.vector.tensor_copy(out[:, 1, :], out_ps[1][:, :]).then_inc(out_down, 1)

        @block.tensor
        def _(pe):
            def body(i):
                for par in range(2):
                    g = 2 * i + par
                    wait(pe, came[par], 16 * J * (i + 1))
                    wait(pe, rows_down, g - 1)
                    for j in range(J):
                        t = nc.tensor.transpose(turn_ps[par][:, j * P:(j + 1) * P], rows[:, par, j, :], k["ident"][:, :])
                    t.then_inc(turned, 1)
                    wait(pe, rows_down, g + 1)
                    wait(pe, out_down, g - 1)
                    for j in range(J):
                        nc.tensor.matmul(out_ps[par][:, j * P:(j + 1) * P], rows_t[:, par, j * P:(j + 1) * P], m["bond"][:, :],
                                         start=True, stop=False)
                        t = nc.tensor.matmul(out_ps[par][:, j * P:(j + 1) * P], k["one_row"][:, :], m["bond_b"][:, :],
                                             start=False, stop=True)
                    t.then_inc(made, 1)
            loop(pe, body)


def node_rows(nc, k, x, sums, out1, out2, *, gcn=False, first=(), bias1=None, residual=None, norm=True,
              weighted=False, second=None, bias2=None, relu2=False, outside=False):
    width = P + 1 if weighted else P
    with nc.cleanup_on_exit(), ExitStack() as ctx:
        ph = Phase(nc, ctx)
        sb, ps, sem = ph.sb, ph.ps, ph.sem
        x_in = sb("x_in", [P, 2, J, P])
        s_in = sb("s_in", [P, 2, J, width])
        r_in = sb("r_in", [P, 2, W]) if residual is not None else None
        u = sb("u", [P, 2, W])
        u_t = sb("u_t", [P, 2, W])
        x_t = sb("x_t", [P, 2, W])
        y = sb("y", [P, 2, W])
        o1 = sb("o1", [P, 2, J, P])
        o1_t = sb("o1_t", [P, 2, W])
        o2 = sb("o2", [P, 2, J, P])
        parts = sb("parts", [P, 2, J, 6])
        moments = sb("moments", [P, 2, J, 2])
        spread = sb("spread", [P, 2, J])
        inverse = sb("inverse", [P, 2, J])
        low = sb("low", [P, 2, J])
        share = sb("share", [P, 2, J])
        minus_half = sb("minus_half", [P, J])
        tu_ps, tx_ps, t2_ps = (ps(n, [P, 512]) for n in ("tu", "tx", "t2"))
        m1_ps = [ps("m10", [P, 512]), ps("m11", [P, 512])]
        m2_ps = [ps("m20", [P, 512]), ps("m21", [P, 512])]
        came, stored1, stored2 = ([sem(n + "0"), sem(n + "1")] for n in ("came", "stored1", "stored2"))
        (u_step, u_made, y_made, halved, measured, joined, spread_in, raised, o1_made, o2_made, tu, tx, u_down, x_down,
         m1, t2, o1_down, m2, lows, passed, passed_sp, passed_v) = (sem(n) for n in (
            "u_step", "u_made", "y_made", "halved", "measured", "joined", "spread_in", "raised", "o1_made", "o2_made",
            "tu", "tx", "u_down", "x_down", "m1", "t2", "o1_down", "m2", "lows", "passed", "passed_sp", "passed_v"))
        loads = 2 + (residual is not None)
        used = y_made if (residual is not None or not gcn) else u_made
        block = ctx.enter_context(nc.Block())

        @block.sync
        def _(sp):
            def front(i, g, par):
                wait(sp, used, g - 1, passed_sp)
                if len(first) == 2:
                    wait(sp, tx, g - 1, passed_sp)
                flat = x_in[:, par, :, :].rearrange("p j d -> p (j d)")
                if outside and isinstance(g, int) and g == G - 1:
                    sp.dma_start(flat[0:LASTP, :], x_rows(x, last=True)).then_inc(came[par], 16)
                else:
                    source = block_of(x_rows(x), g) if outside else rows_of(x, g)
                    sp.dma_start(flat, source).then_inc(came[par], 16)
                sp.dma_start(s_in[:, par, :, :].rearrange("p j d -> p (j d)"), rows_of(sums, g)).then_inc(came[par], 16)
                if residual is not None:
                    sp.dma_start(r_in[:, par, :], rows_of(residual, g)).then_inc(came[par], 16)

            def back(i, g, par):
                wait(sp, o1_made, g + 1, passed_sp)
                sp.dma_start(rows_of(out1, g), o1[:, par, :, :].rearrange("p j d -> p (j d)")).then_inc(stored1[par], 16)
                wait(sp, o2_made, g + 1, passed_sp)
                sp.dma_start(rows_of(out2, g), o2[:, par, :, :].rearrange("p j d -> p (j d)")).then_inc(stored2[par], 16)
            front_and_back(sp, front, back)
            for par in range(2):
                sp.wait_ge(stored1[par], 16 * (G // 2))
                sp.wait_ge(stored2[par], 16 * (G // 2))

        @block.gpsimd
        def _(pool):
            nc.gpsimd.memset(minus_half[:, :], -0.5).then_inc(halved, 1)
            pool.wait_ge(halved, 1)
            if norm:
                def body(i):
                    for par in range(2):
                        wait(pool, spread_in, 2 * i + par + 1, passed)
                        nc.gpsimd.tensor_tensor(inverse[:, par, :], spread[:, par, :], minus_half[:, :], ALU.pow).then_inc(raised, 1)
                loop(pool, body)

        @block.vector
        def _(v):
            def front(i, g, par):
                wait(v, came[par], 16 * loads * (i + 1))
                if norm and not gcn:
                    wait(v, o1_made, g - 1)
                x2d = x_in[:, par, :, :].rearrange("p j d -> p (j d)")
                if gcn:
                    dinv = k["dinv"][:, ds(g * J, J)].unsqueeze(2).to_broadcast([P, J, P])
                    u3 = u[:, par, :].rearrange("p (j d) -> p j d", j=J)
                    wait(v, tu, g - 1)
                    nc.vector.tensor_tensor(u3, x_in[:, par, :, :], dinv, ALU.mult).then_inc(u_step, 1)
                    wait(v, u_step, 2 * g + 1)
                    nc.vector.tensor_tensor(u3, u3, s_in[:, par, :, :], ALU.add).then_inc(u_step, 1)
                    wait(v, u_step, 2 * g + 2)
                    nc.vector.tensor_tensor(u3, u3, dinv, ALU.mult).then_inc(u_made, 1)
                elif weighted:
                    nc.vector.tensor_scalar(low[:, par, :], s_in[:, par, :, P], 0.5, None, ALU.is_lt).then_inc(lows, 1)
                    wait(v, lows, 3 * g + 1)
                    nc.vector.tensor_tensor(low[:, par, :], low[:, par, :], s_in[:, par, :, P], ALU.add).then_inc(lows, 1)
                    wait(v, lows, 3 * g + 2)
                    nc.vector.reciprocal(share[:, par, :], low[:, par, :]).then_inc(lows, 1)
                    wait(v, lows, 3 * g + 3)
                    for j in range(J):
                        last = nc.vector.scalar_tensor_tensor(y[:, par, j * P:(j + 1) * P], s_in[:, par, j, 0:P], share[:, par, j:j + 1],
                                                              x_in[:, par, j, :], ALU.mult, ALU.add)
                    last.then_inc(y_made, 1)
                else:
                    nc.vector.tensor_tensor(y[:, par, :], x2d, s_in[:, par, :, :].rearrange("p j d -> p (j d)"),
                                            ALU.add).then_inc(y_made, 1)

            def back(i, g, par):
                if not norm:
                    return
                if gcn:
                    wait(v, m1, g + 1)
                    wait(v, o1_made, g - 1)
                    nc.vector.tensor_tensor(y[:, par, :], m1_ps[par][:, :], r_in[:, par, :], ALU.add).then_inc(y_made, 1)
                wait(v, y_made, g + 1)
                for j in range(J):
                    last = nc.vector.bn_stats(parts[:, par, j, :], y[:, par, j * P:(j + 1) * P])
                last.then_inc(measured, 1)
                wait(v, measured, g + 1, passed_v)
                for j in range(J):
                    last = nc.vector.bn_aggr(moments[:, par, j, :], parts[:, par, j, :])
                last.then_inc(joined, 1)
                wait(v, joined, g + 1)
                nc.vector.tensor_scalar(spread[:, par, :], moments[:, par, :, 1], LN_EPS, None, ALU.add).then_inc(spread_in, 1)
                wait(v, stored1[par], 16 * i)
                if second is None:
                    wait(v, o2_made, g - 1)
                else:
                    wait(v, t2, g - 1)
                wait(v, raised, g + 1)
                for j in range(J):
                    last = nc.vector.tensor_scalar(o1[:, par, j, :], y[:, par, j * P:(j + 1) * P], moments[:, par, j, 0:1],
                                                   inverse[:, par, j:j + 1], ALU.subtract, ALU.mult)
                last.then_inc(o1_made, 1)
            front_and_back(v, front, back)

        @block.scalar
        def _(act):
            def front(i, g, par):
                if not gcn:
                    return
                wait(act, tu, g + 1)
                wait(act, m1, g - 1)
                nc.scalar.copy(u_t[:, par, :], tu_ps[:, :]).then_inc(u_down, 1)
                if len(first) == 2:
                    wait(act, tx, g + 1)
                    nc.scalar.copy(x_t[:, par, :], tx_ps[:, :]).then_inc(x_down, 1)

            def back(i, g, par):
                if not norm:
                    wait(act, m1, g + 1)
                    wait(act, stored1[par], 16 * i)
                    wait(act, o2_made, g - 1)
                    nc.scalar.activation(o1[:, par, :, :].rearrange("p j d -> p (j d)"), m1_ps[par][:, :], ACT.Relu).then_inc(o1_made, 1)
                wait(act, stored2[par], 16 * i)
                if second is None:
                    wait(act, o1_made, g + 1)
                    for j in range(J):
                        last = nc.scalar.activation(o2[:, par, j, :], o1[:, par, j, :], ACT.Copy, scale=k["dinv"][:, ds(g * J + j)])
                    last.then_inc(o2_made, 1)
                else:
                    wait(act, t2, g + 1)
                    wait(act, m2, g - 1)
                    nc.scalar.copy(o1_t[:, par, :], t2_ps[:, :]).then_inc(o1_down, 1)
                    wait(act, m2, g + 1)
                    nc.scalar.activation(o2[:, par, :, :].rearrange("p j d -> p (j d)"), m2_ps[par][:, :],
                                         ACT.Relu if relu2 else ACT.Copy).then_inc(o2_made, 1)
            front_and_back(act, front, back)

        @block.tensor
        def _(pe):
            def front(i, g, par):
                if not gcn:
                    return
                wait(pe, u_made, g + 1)
                wait(pe, u_down, g)
                for j in range(J):
                    t = nc.tensor.transpose(tu_ps[:, j * P:(j + 1) * P], u[:, par, j * P:(j + 1) * P], k["ident"][:, :])
                t.then_inc(tu, 1)
                if len(first) == 2:
                    wait(pe, x_down, g)
                    for j in range(J):
                        t = nc.tensor.transpose(tx_ps[:, j * P:(j + 1) * P], x_in[:, par, j, :], k["ident"][:, :])
                    t.then_inc(tx, 1)
                wait(pe, u_down, g + 1)
                if len(first) == 2:
                    wait(pe, x_down, g + 1)
                wait(pe, y_made if norm else o1_made, g - 1)
                sources = (u_t, x_t)[0:len(first)]
                for j in range(J):
                    for n, (a, b) in enumerate(zip(sources, first)):
                        t = nc.tensor.matmul(m1_ps[par][:, j * P:(j + 1) * P], a[:, par, j * P:(j + 1) * P], b[:, :],
                                             start=n == 0, stop=n == len(first) - 1 and bias1 is None)
                    if bias1 is not None:
                        t = nc.tensor.matmul(m1_ps[par][:, j * P:(j + 1) * P], k["one_row"][:, :], bias1[:, :], start=False, stop=True)
                t.then_inc(m1, 1)

            def back(i, g, par):
                if second is None:
                    return
                wait(pe, o1_made, g + 1)
                wait(pe, o1_down, g)
                for j in range(J):
                    t = nc.tensor.transpose(t2_ps[:, j * P:(j + 1) * P], o1[:, par, j, :], k["ident"][:, :])
                t.then_inc(t2, 1)
                wait(pe, o1_down, g + 1)
                wait(pe, o2_made, g - 1)
                for j in range(J):
                    nc.tensor.matmul(m2_ps[par][:, j * P:(j + 1) * P], o1_t[:, par, j * P:(j + 1) * P], second[:, :],
                                     start=True, stop=False)
                    t = nc.tensor.matmul(m2_ps[par][:, j * P:(j + 1) * P], k["one_row"][:, :], bias2[:, :], start=False, stop=True)
                t.then_inc(m2, 1)
            front_and_back(pe, front, back)


def batch_norm(nc, ph, stats, gain, shift, bias, halves):
    sb, sem = ph.sb, ph.sem
    moments, spread, power, root = sb("moments", [P, halves, 2]), sb("spread", [P, halves]), sb("power", [P, halves]), sb("root", [P, halves])
    affine, mean = sb("affine", [P, halves, 2]), sb("mean", [P, halves])
    stepped, spread_in, raised, done = sem("stepped"), sem("spread_in"), sem("raised"), sem("affine_in")

    def pool_part(pool):
        nc.gpsimd.memset(power[:, :], -0.5).then_inc(stepped, 1)
        pool.wait_ge(spread_in, 1)
        pool.wait_ge(stepped, 1)
        nc.gpsimd.tensor_tensor(root[:, :], spread[:, :], power[:, :], ALU.pow).then_inc(raised, 1)

    def v_part(v):
        n = sem("n")
        count = [0]

        def step(ins):
            count[0] += 1
            ins.then_inc(n, 1)
            v.wait_ge(n, count[0])

        for h in range(halves):
            step(nc.vector.bn_aggr(moments[:, h, :], stats[:, h, :]))
        nc.vector.tensor_scalar(spread[:, :], moments[:, :, 1], BN_EPS, None, ALU.add).then_inc(spread_in, 1)
        step(nc.vector.tensor_tensor(mean[:, :], moments[:, :, 0], bias, ALU.add))
        step(nc.vector.tensor_tensor(mean[:, :], bias, mean[:, :], ALU.subtract))
        v.wait_ge(raised, 1)
        step(nc.vector.tensor_tensor(affine[:, :, 0], root[:, :], gain, ALU.mult))
        step(nc.vector.tensor_tensor(mean[:, :], mean[:, :], affine[:, :, 0], ALU.mult))
        nc.vector.tensor_tensor(affine[:, :, 1], mean[:, :], shift, ALU.add).then_inc(done, 1)
    return affine, done, pool_part, v_part


def group_stats(nc, stats, h, g, product, last):
    if last:
        product = product.rearrange("p (j n) -> p j n", j=J)[:, :, 0:LASTP]
    return nc.vector.bn_stats(stats[:, h, ds(g * 6, 6)], product)


def gin_in(nc, k, m, layer, h_rows, sums, z_cols, stats):
    with nc.cleanup_on_exit(), ExitStack() as ctx:
        ph = Phase(nc, ctx)
        sb, ps, sem = ph.sb, ph.ps, ph.sem
        h_in, s_in, z, z_t = (sb(n, [P, 2, W]) for n in ("h_in", "s_in", "z", "z_t"))
        turn_ps = [ps("turn0", [P, 512]), ps("turn1", [P, 512])]
        wide_ps = [[ps(f"wide{n}{h}", [P, 512]) for h in range(2)] for n in range(2)]
        came, stored = ([sem(n + "0"), sem(n + "1")] for n in ("came", "stored"))
        z_made, turned, z_down, wide, counted, passed_sp = (sem(n) for n in (
            "z_made", "turned", "z_down", "wide", "counted", "passed_sp"))
        block = ctx.enter_context(nc.Block())

        @block.sync
        def _(sp):
            def front(i, g, par):
                wait(sp, z_made, g - 1, passed_sp)
                sp.dma_start(h_in[:, par, :], rows_of(h_rows, g)).then_inc(came[par], 16)
                sp.dma_start(s_in[:, par, :], rows_of(sums, g)).then_inc(came[par], 16)

            def back(i, g, par):
                wait(sp, z_down, g + 1, passed_sp)
                sp.dma_start(block_of(z_cols, g), z_t[:, par, :]).then_inc(stored[par], 16)
            front_and_back(sp, front, back)
            for par in range(2):
                sp.wait_ge(stored[par], 16 * (G // 2))

        @block.vector
        def _(v):
            def front(i, g, par):
                wait(v, came[par], 32 * (i + 1))
                wait(v, turned, g - 1)
                nc.vector.scalar_tensor_tensor(z[:, par, :], h_in[:, par, :], m["eps_row"][:, layer:layer + 1], s_in[:, par, :],
                                               ALU.mult, ALU.add).then_inc(z_made, 1)

            def back(i, g, par):
                last = isinstance(g, int) and g == G - 1
                for h in range(2):
                    wait(v, wide, 2 * g + h + 1)
                    group_stats(nc, stats, h, g, wide_ps[par][h][:, :], last).then_inc(counted, 1)
            front_and_back(v, front, back)

        @block.scalar
        def _(act):
            def body(i):
                for par in range(2):
                    g = 2 * i + par
                    wait(act, turned, g + 1)
                    wait(act, wide, 2 * (g - 1))
                    wait(act, stored[par], 16 * i)
                    nc.scalar.copy(z_t[:, par, :], turn_ps[par][:, :]).then_inc(z_down, 1)
            loop(act, body)

        @block.tensor
        def _(pe):
            def front(i, g, par):
                wait(pe, z_made, g + 1)
                wait(pe, z_down, g - 1)
                for j in range(J):
                    t = nc.tensor.transpose(turn_ps[par][:, j * P:(j + 1) * P], z[:, par, j * P:(j + 1) * P], k["ident"][:, :])
                t.then_inc(turned, 1)

            def back(i, g, par):
                wait(pe, z_down, g + 1)
                wait(pe, counted, 2 * (g - 1))
                for h in range(2):
                    nc.tensor.matmul(wide_ps[par][h][:, :], m["gin1"][:, layer, h * P:(h + 1) * P], z_t[:, par, :],
                                     start=True, stop=True).then_inc(wide, 1)
            front_and_back(pe, front, back)


def gin_middle(nc, k, m, layer, z_cols, stats, y_cols, stats2):
    with nc.cleanup_on_exit(), ExitStack() as ctx:
        ph = Phase(nc, ctx)
        sb, ps, sem = ph.sb, ph.ps, ph.sem
        z_t, y_t = (sb(n, [P, 2, W]) for n in ("z_t", "y_t"))
        wide_sb = sb("wide_sb", [P, 2, 2, W])
        wide_ps = [[ps(f"wide{n}{h}", [P, 512]) for h in range(2)] for n in range(2)]
        y_ps = [ps("y0", [P, 512]), ps("y1", [P, 512])]
        came, stored = ([sem(n + "0"), sem(n + "1")] for n in ("came", "stored"))
        wide, wide_down, product, y_down, counted, passed_sp = (sem(n) for n in (
            "wide", "wide_down", "product", "y_down", "counted", "passed_sp"))
        affine, affine_in, pool_part, v_part = batch_norm(nc, ph, stats, m["g1"][:, layer, :], m["be1"][:, layer, :],
                                                          m["b1"][:, layer, :], 2)
        block = ctx.enter_context(nc.Block())

        @block.gpsimd
        def _(pool):
            pool_part(pool)

        @block.sync
        def _(sp):
            def front(i, g, par):
                wait(sp, wide, 2 * (g - 1), passed_sp)
                sp.dma_start(z_t[:, par, :], block_of(z_cols, g)).then_inc(came[par], 16)

            def back(i, g, par):
                wait(sp, y_down, g + 1, passed_sp)
                sp.dma_start(block_of(y_cols, g), y_t[:, par, :]).then_inc(stored[par], 16)
            front_and_back(sp, front, back)
            for par in range(2):
                sp.wait_ge(stored[par], 16 * (G // 2))

        @block.scalar
        def _(act):
            act.wait_ge(affine_in, 1)

            def body(i):
                for par in range(2):
                    g = 2 * i + par
                    wait(act, product, g - 1)
                    for h in range(2):
                        wait(act, wide, 2 * g + h + 1)
                        nc.scalar.activation(wide_sb[:, par, h, :], wide_ps[par][h][:, :], ACT.Relu, bias=affine[:, h, 1:2],
                                             scale=affine[:, h, 0:1]).then_inc(wide_down, 1)
            loop(act, body)

        @block.vector
        def _(v):
            v_part(v)

            def body(i, last=False):
                for par in range(2):
                    g = 2 * i + par
                    wait(v, product, g + 1)
                    group_stats(nc, stats2, 0, g, y_ps[par][:, :], isinstance(g, int) and g == G - 1).then_inc(counted, 1)
                    wait(v, stored[par], 16 * i)
                    nc.vector.tensor_copy(y_t[:, par, :], y_ps[par][:, :]).then_inc(y_down, 1)
            loop(v, body)

        @block.tensor
        def _(pe):
            def front(i, g, par):
                wait(pe, came[par], 16 * (i + 1))
                wait(pe, wide_down, 2 * (g - 1))
                for h in range(2):
                    nc.tensor.matmul(wide_ps[par][h][:, :], m["gin1"][:, layer, h * P:(h + 1) * P], z_t[:, par, :],
                                     start=True, stop=True).then_inc(wide, 1)

            def back(i, g, par):
                wait(pe, wide_down, 2 * g + 2)
                wait(pe, y_down, g - 1)
                for h in range(2):
                    t = nc.tensor.matmul(y_ps[par][:, :], m["gin2"][:, layer, h, :], wide_sb[:, par, h, :], start=h == 0, stop=h == 1)
                t.then_inc(product, 1)
            front_and_back(pe, front, back)


def gin_out(nc, k, m, layer, y_cols, stats2, h_rows):
    with nc.cleanup_on_exit(), ExitStack() as ctx:
        ph = Phase(nc, ctx)
        sb, ps, sem = ph.sb, ph.ps, ph.sem
        y_t, h_t, h_sb = (sb(n, [P, 2, W]) for n in ("y_t", "h_t", "h_sb"))
        turn_ps = [ps("turn0", [P, 512]), ps("turn1", [P, 512])]
        came, stored = ([sem(n + "0"), sem(n + "1")] for n in ("came", "stored"))
        normed, turned, h_down, passed_sp = (sem(n) for n in ("normed", "turned", "h_down", "passed_sp"))
        affine, affine_in, pool_part, v_part = batch_norm(nc, ph, stats2, m["gn"][:, layer:layer + 1],
                                                          m["bet"][:, layer:layer + 1], m["b2"][:, layer:layer + 1], 1)
        block = ctx.enter_context(nc.Block())

        @block.gpsimd
        def _(pool):
            pool_part(pool)

        @block.sync
        def _(sp):
            def front(i, g, par):
                wait(sp, normed, g - 1, passed_sp)
                sp.dma_start(y_t[:, par, :], block_of(y_cols, g)).then_inc(came[par], 16)

            def back(i, g, par):
                wait(sp, h_down, g + 1, passed_sp)
                sp.dma_start(rows_of(h_rows, g), h_sb[:, par, :]).then_inc(stored[par], 16)
            front_and_back(sp, front, back)
            for par in range(2):
                sp.wait_ge(stored[par], 16 * (G // 2))

        @block.scalar
        def _(act):
            act.wait_ge(affine_in, 1)

            def body(i):
                for par in range(2):
                    g = 2 * i + par
                    wait(act, came[par], 16 * (i + 1))
                    wait(act, turned, g - 1)
                    nc.scalar.activation(h_t[:, par, :], y_t[:, par, :], ACT.Relu, bias=affine[:, 0, 1:2],
                                         scale=affine[:, 0, 0:1]).then_inc(normed, 1)
            loop(act, body)

        @block.vector
        def _(v):
            v_part(v)

            def body(i):
                for par in range(2):
                    g = 2 * i + par
                    wait(v, turned, g + 1)
                    wait(v, stored[par], 16 * i)
                    nc.vector.tensor_copy(h_sb[:, par, :], turn_ps[par][:, :]).then_inc(h_down, 1)
            loop(v, body)

        @block.tensor
        def _(pe):
            def body(i):
                for par in range(2):
                    g = 2 * i + par
                    wait(pe, normed, g + 1)
                    wait(pe, h_down, g - 1)
                    for j in range(J):
                        t = nc.tensor.transpose(turn_ps[par][:, j * P:(j + 1) * P], h_t[:, par, j * P:(j + 1) * P], k["ident"][:, :])
                    t.then_inc(turned, 1)
            loop(pe, body)


def final_rows(nc, k, m, y_cols, stats2, x, out):
    layer = LAYERS - 1
    with nc.cleanup_on_exit(), ExitStack() as ctx:
        ph = Phase(nc, ctx)
        sb, ps, sem = ph.sb, ph.ps, ph.sem
        y_t, h_t, x_in, y, o = (sb(n, [P, 2, W]) for n in ("y_t", "h_t", "x_in", "y", "o"))
        parts, aggregate = sb("parts", [P, 2, J, 6]), sb("aggregate", [P, 2, J, 2])
        spread_r, inverse, minus_half = sb("spread_r", [P, 2, J]), sb("inverse", [P, 2, J]), sb("minus_half", [P, J])
        out_ps = [ps("out0", [P, 512]), ps("out1", [P, 512])]
        came, stored = ([sem(n + "0"), sem(n + "1")] for n in ("came", "stored"))
        normed, product, summed, measured, joined, rows_spread, halved, raised_r, o_made, passed_sp, passed, passed_v = (sem(n) for n in (
            "normed", "product", "summed", "measured", "joined", "rows_spread", "halved", "raised_r", "o_made", "passed_sp", "passed", "passed_v"))
        affine, affine_in, pool_part, v_part = batch_norm(nc, ph, stats2, m["gn"][:, layer:layer + 1],
                                                          m["bet"][:, layer:layer + 1], m["b2"][:, layer:layer + 1], 1)
        block = ctx.enter_context(nc.Block())

        @block.gpsimd
        def _(pool):
            pool_part(pool)
            nc.gpsimd.memset(minus_half[:, :], -0.5).then_inc(halved, 1)
            pool.wait_ge(halved, 1)

            def body(i):
                for par in range(2):
                    wait(pool, rows_spread, 2 * i + par + 1, passed)
                    nc.gpsimd.tensor_tensor(inverse[:, par, :], spread_r[:, par, :], minus_half[:, :], ALU.pow).then_inc(raised_r, 1)
            loop(pool, body)

        @block.sync
        def _(sp):
            def front(i, g, par):
                wait(sp, normed, g - 1, passed_sp)
                sp.dma_start(y_t[:, par, :], block_of(y_cols, g)).then_inc(came[par], 16)
                wait(sp, summed, g - 1, passed_sp)
                sp.dma_start(x_in[:, par, :], rows_of(x, g)).then_inc(came[par], 16)

            def back(i, g, par):
                wait(sp, o_made, g + 1, passed_sp)
                if isinstance(g, int) and g == G - 1:
                    sp.dma_start(x_rows(out, last=True), o[0:LASTP, par, :]).then_inc(stored[par], 16)
                else:
                    sp.dma_start(block_of(x_rows(out), g), o[:, par, :]).then_inc(stored[par], 16)
            front_and_back(sp, front, back)
            for par in range(2):
                sp.wait_ge(stored[par], 16 * (G // 2))

        @block.scalar
        def _(act):
            act.wait_ge(affine_in, 1)

            def body(i):
                for par in range(2):
                    g = 2 * i + par
                    wait(act, came[par], 32 * (i + 1))
                    wait(act, product, g - 1)
                    nc.scalar.activation(h_t[:, par, :], y_t[:, par, :], ACT.Relu, bias=affine[:, 0, 1:2],
                                         scale=affine[:, 0, 0:1]).then_inc(normed, 1)
            loop(act, body)

        @block.tensor
        def _(pe):
            def body(i):
                for par in range(2):
                    g = 2 * i + par
                    wait(pe, normed, g + 1)
                    wait(pe, summed, g - 1)
                    for j in range(J):
                        nc.tensor.matmul(out_ps[par][:, j * P:(j + 1) * P], h_t[:, par, j * P:(j + 1) * P], m["final"][:, :],
                                         start=True, stop=False)
                        t = nc.tensor.matmul(out_ps[par][:, j * P:(j + 1) * P], k["one_row"][:, :], m["final_b"][:, :],
                                             start=False, stop=True)
                    t.then_inc(product, 1)
            loop(pe, body)

        @block.vector
        def _(v):
            v_part(v)

            def body(i):
                for par in range(2):
                    g = 2 * i + par
                    wait(v, product, g + 1)
                    wait(v, o_made, g - 1)
                    nc.vector.tensor_tensor(y[:, par, :], out_ps[par][:, :], x_in[:, par, :], ALU.add).then_inc(summed, 1)
                    wait(v, summed, g + 1)
                    for j in range(J):
                        last = nc.vector.bn_stats(parts[:, par, j, :], y[:, par, j * P:(j + 1) * P])
                    last.then_inc(measured, 1)
                    wait(v, measured, g + 1, passed_v)
                    for j in range(J):
                        last = nc.vector.bn_aggr(aggregate[:, par, j, :], parts[:, par, j, :])
                    last.then_inc(joined, 1)
                    wait(v, joined, g + 1)
                    nc.vector.tensor_scalar(spread_r[:, par, :], aggregate[:, par, :, 1], LN_EPS, None, ALU.add).then_inc(rows_spread, 1)
                    wait(v, stored[par], 16 * i)
                    wait(v, raised_r, g + 1)
                    for j in range(J):
                        last = nc.vector.tensor_scalar(o[:, par, j * P:(j + 1) * P], y[:, par, j * P:(j + 1) * P],
                                                       aggregate[:, par, j, 0:1], inverse[:, par, j:j + 1], ALU.subtract, ALU.mult)
                    last.then_inc(o_made, 1)
            loop(v, body)


INPUTS = ["x", "src", "dst", "edge_attr_128", "edge_attr_3", "edge_weight", "L0_gnn_W_up0", "L0_gnn_W_up1", "L0_gnn_mlp_w0",
          "L0_gnn_mlp_b0", "L0_gnn_mlp_w1", "L0_gnn_mlp_b1", "L0_gnn_mlp_w2", "L0_gnn_mlp_b2", "L0_gnn_W_out0",
          "L0_gnn_W_out1", "L1_gnn_W1", "L1_gnn_R1", "L1_gnn_W2", "L1_gnn_R2", "L1_gnn_W3", "L1_gnn_Wh", "L1_gnn_bh",
          "L2_gnn_W", "L2_gnn_b", "L3_gnn_W_atom", "L3_gnn_b_atom", "L3_gnn_W_bond", "L3_gnn_b_bond", "L3_gnn_eps",
          "L3_gnn_W1", "L3_gnn_b1", "L3_gnn_g1", "L3_gnn_be1", "L3_gnn_W2", "L3_gnn_b2", "L3_gnn_gn", "L3_gnn_bet",
          "L3_gnn_W_out", "L3_gnn_b_out"]


def program(nc, w, out):
    def scratch(name, shape):
        return nc.dram_tensor(name, shape, F32, kind="Internal").ap()

    x = w["x"]
    d = {"sorted_r": scratch("sorted_r", [NP, 8]), "sorted_s": scratch("sorted_s", [NP, 8]),
         "line_r": scratch("line_r", [NP + P]), "line_s": scratch("line_s", [NP + P]),
         "sum_r": scratch("sum_r", [NP, P]), "sum_s": scratch("sum_s", [NP, P + 1])}
    groups = [scratch(f"groups{n}", [G, P, W]) for n in range(3)]
    messages, bonds, z_cols = groups
    y_cols = messages
    x1, x2, x3, xa, xb, scaled, h = (scratch(n, [NP, P]) for n in ("x1", "x2", "x3", "xa", "xb", "scaled", "h"))
    with ExitStack() as ctx:
        k = fixed_tiles(nc, ctx)
        k["line"] = {"r": d["line_r"], "s": d["line_s"]}
        count_and_rank(nc, k, d, w["src"], w["dst"], w["edge_weight"], w["edge_attr_3"])
        order_tables(nc, k, d)
        with ExitStack() as inner:
            t = tensor_product_weights(nc, k, {n[len("L0_gnn_"):]: a for n, a in w.items() if n.startswith("L0")}, inner)
            edge_products(nc, k, x, t, messages)
        segment_sum(nc, k, "r", d["sum_r"], messages=messages)
        m = load_weights(nc, k, ctx, w)
        node_rows(nc, k, x, d["sum_r"], x1, scaled, outside=True)
        segment_sum(nc, k, "r", d["sum_r"], table=scaled)
        node_rows(nc, k, x1, d["sum_r"], xa, scaled, gcn=True, first=(m["W1"], m["R1"]), norm=False)
        segment_sum(nc, k, "r", d["sum_r"], table=scaled)
        node_rows(nc, k, xa, d["sum_r"], xb, scaled, gcn=True, first=(m["W2"], m["R2"]), norm=False)
        segment_sum(nc, k, "r", d["sum_r"], table=scaled)
        node_rows(nc, k, xb, d["sum_r"], x2, h, gcn=True, first=(m["W3Wh"],), bias1=m["bh"], residual=x1,
                  second=m["lin_t"], bias2=m["lin_b"], relu2=True)
        segment_sum(nc, k, "s", d["sum_s"], width=P + 1, table=h, weight=k["weight_s"])
        node_rows(nc, k, x2, d["sum_s"], x3, h, weighted=True, second=m["atom"], bias2=m["atom_b"])
        bond_rows(nc, k, w["edge_attr_128"], m, bonds)
        stats = ctx.enter_context(nc.sbuf_tensor("stats", [P, 2, G * 6], F32))
        stats2 = ctx.enter_context(nc.sbuf_tensor("stats2", [P, 1, G * 6], F32))
        for layer in range(LAYERS):
            segment_sum(nc, k, "r", d["sum_r"], table=h, added=bonds)
            gin_in(nc, k, m, layer, h, d["sum_r"], z_cols, stats)
            gin_middle(nc, k, m, layer, z_cols, stats, y_cols, stats2)
            if layer < LAYERS - 1:
                gin_out(nc, k, m, layer, y_cols, stats2, h)
        final_rows(nc, k, m, y_cols, stats2, x3, out)


def kernel(**inputs):
    import concourse.bacc as bacc
    from concourse.bass_utils import run_bass_kernel_spmd

    nc = bacc.Bacc("TRN2", target_bir_lowering=False, num_devices=1)
    arrays, handles = {}, {}
    for name in INPUTS:
        a = np.ascontiguousarray(inputs[name])
        arrays["in_" + name] = a
        handles[name] = nc.dram_tensor("in_" + name, a.shape, mybir.dt.from_np(a.dtype), kind="ExternalInput").ap()
    out = nc.dram_tensor("out_nodes", (N, P), F32, kind="ExternalOutput").ap()
    program(nc, handles, out)
    return run_bass_kernel_spmd(nc, [arrays], core_ids=[0]).results[0]["out_nodes"]
```

```python
from contextlib import ExitStack

import numpy as np

import concourse.bass as bass
from concourse import mybir

F32 = mybir.dt.float32
F16 = mybir.dt.float16
BF16 = mybir.dt.bfloat16
I32 = mybir.dt.int32
ALU = mybir.AluOpType
ACT = mybir.ActivationFunctionType

P = 128
N = 50000
J = 4
G = (N + P * J - 1) // (P * J)
T = G * J
NP = T * P
W = J * P
FULL = N // T
REST = N - FULL * T
LASTP = (N - (G - 1) * W) // J
PAD = NP - 1
SKIP = 1 << 20
MUL = 32
NB = 8
HID = 64
AVG = 16.0
LN_EPS = 1e-5
BN_EPS = 1e-5
LAYERS = 3


def ds(i, n=1):
    return slice(i, i + n) if isinstance(i, int) else bass.DynSlice(i, n)


def block_of(t, g):
    return t[g] if isinstance(g, int) else t[bass.DynSlice(g, 1)].rearrange("a p f -> (a p) f")


def rows_of(t, g):
    return block_of(t.rearrange("(g p j) d -> g p (j d)", p=P, j=J), g)


def x_rows(t, last=False):
    if last:
        return t[(G - 1) * W:N, :].rearrange("(p j) d -> p (j d)", j=J)
    return t[0:(G - 1) * W, :].rearrange("(g p j) d -> g p (j d)", p=P, j=J)


def loop(eng, body):
    body(0)
    with eng.Fori(1, G // 2 - 1) as i:
        body(i)
    body(G // 2 - 1)


def paced(eng, *stages):
    leads = [lead for _, lead in stages]
    low, high = min(leads), max(leads)
    begin = 2 - low + low % 2
    end = G - 1 - high
    end -= end % 2

    def step(half, q):
        for part, lead in stages:
            g = 2 * half + q + lead
            if not isinstance(g, int) or 0 <= g < G:
                part(half + (q + lead) // 2, g, (q + lead) % 2)

    for n in range(-high, begin):
        step(n // 2, n % 2)
    with eng.Fori(begin // 2, end // 2) as half:
        step(half, 0)
        step(half, 1)
    for n in range(end, G - low):
        step(n // 2, n % 2)


class Phase:

    def __init__(self, nc, ctx):
        self.nc, self.ctx = nc, ctx
        self.n = 0

    def sb(self, name, shape, dt=F32):
        return self.ctx.enter_context(self.nc.sbuf_tensor(f"{name}_{self.nc.next_id()}", shape, dt))

    def ps(self, name, shape, dt=F32):
        return self.ctx.enter_context(self.nc.psum_tensor(f"{name}_{self.nc.next_id()}", shape, dt))

    def sem(self, name):
        return self.nc.alloc_semaphore(name=f"{name}_{self.nc.next_id()}")


def wait(eng, sem, value, passed=None):
    if isinstance(value, int):
        if value > 0:
            eng.wait_ge(sem, value)
        return
    eng.wait_ge(sem, value)
    if passed is not None:
        eng.sem_inc(passed, 1)


def fixed_tiles(nc, ctx):
    def sb(name, shape, dt=F32):
        return ctx.enter_context(nc.sbuf_tensor(name, shape, dt))

    k = {
        "ident": sb("ident", [P, P]), "ident16": sb("ident16", [P, P], F16),
        "below": sb("below", [P, P]), "below16": sb("below16", [P, P], F16),
        "ones": sb("ones", [P, P]), "cols16": sb("cols16", [P, T], F16),
        "dinv": sb("dinv", [P, T]), "one_rows": sb("one_rows", [3, P], BF16),
        "eps": sb("eps", [P, 1]),
    }
    for c in "rs":
        k["key_" + c] = sb("key_" + c, [P, T])
        k["before_" + c] = sb("before_" + c, [P, T])
        k["from_" + c] = sb("from_" + c, [P, T], I32)
        k["to_" + c] = sb("to_" + c, [P, T], I32)
    k["edge_r"] = sb("edge_r", [P, T], I32)
    k["weight_r"] = sb("weight_r", [P, T])
    k["weight_s"] = sb("weight_s", [P, T])
    k["vec_r"] = sb("vec_r", [P, T, 3])
    return k


def count_and_rank(nc, k, d, src, dst, edge_weight, edge_attr_3):
    with nc.cleanup_on_exit(), ExitStack() as ctx:
        ph = Phase(nc, ctx)
        sb, ps, sem = ph.sb, ph.ps, ph.sem
        key = [sb("key0", [P, T], I32), sb("key1", [P, T], I32)]
        other = sb("other", [P, T], I32)
        number = sb("number", [P, T], I32)
        cols_i = sb("cols_i", [P, T], I32)
        part = sb("part", [P, 2, T], I32)
        lo = [sb("lo0", [P, T]), sb("lo1", [P, T])]
        hi = [sb("hi0", [P, T]), sb("hi1", [P, T])]
        attr = sb("attr", [P, T * 3])
        weight = sb("weight", [P, T])
        fields = [sb("fields0", [P, T, 8]), sb("fields1", [P, T, 8])]
        one_lo = sb("one_lo", [P, 2, 4, P], F16)
        one_hi = sb("one_hi", [P, 2, 4, T], F16)
        lo_t = sb("lo_t", [P, 2, 2, P])
        lo_t16 = sb("lo_t16", [P, 2, 2, P], F16)
        same16 = sb("same16", [P, 2, 2, P], F16)
        table = sb("table", [P, 2, T])
        count = sb("count", [P, 2, T])
        begin = sb("begin", [P, 2, T])
        total = sb("total", [P, T])
        scan = sb("scan", [P, T])
        picked = sb("picked", [P, 2, T])
        found = sb("found", [P, 2, 4])
        place = sb("place", [P, 2, T])
        place_i = sb("place_i", [P, 2, T], I32)
        row_i = sb("row_i", [P, 2, T], I32)
        degree = sb("degree", [P, T])
        ones_row = sb("ones_row", [P, T])
        idx = sb("idx", [P, 2, 2, J], I32)
        out_rows = sb("out_rows", [P, 2, 2, J, 8])
        run_ps = [ps("run0", [P, 512]), ps("run1", [P, 512])]
        look_ps = [ps("look0", [P, 512]), ps("look1", [P, 512])]
        turn_ps = [ps("turn0", [P, 1024], F16), ps("turn1", [P, 1024], F16)]
        same_ps = [ps("same0", [P, 512]), ps("same1", [P, 512])]

        fills, loaded, iotas = sem("fills"), sem("loaded"), sem("iotas")
        made, ready = sem("made"), sem("ready")
        hot, counted, hist, begun = sem("hot"), sem("counted"), sem("hist"), sem("begun")
        summed, hot2 = sem("summed"), sem("hot2")
        turned, turned_out, tabled = sem("turned"), sem("turned_out"), sem("tabled")
        same, masked, looked, ranked, updated = sem("same"), sem("masked"), sem("looked"), sem("ranked"), sem("updated")
        placed = sem("placed")
        rooted, rowed, staged = sem("rooted"), sem("rowed"), sem("staged")
        sent = [sem("sent0"), sem("sent1")]
        passed = sem("passed")
        block = ctx.enter_context(nc.Block())

        def edges(t, c=1):
            return (t[0:FULL * T * c].rearrange("(p t) -> p t", t=T * c),
                    t[FULL * T * c:N * c].rearrange("(a t) -> a t", a=1))

        @block.sync
        def _(sp):
            sp.wait_ge(fills, 6)
            flat = edge_attr_3.rearrange("n c -> (n c)")
            for tile, array, c in ((key[0], dst, 1), (key[1], src, 1), (other, dst, 1),
                                   (weight, edge_weight, 1), (attr, flat, 3)):
                a, b = edges(array, c)
                sp.dma_start(tile[0:FULL, :], a).then_inc(loaded, 16)
                sp.dma_start(tile[FULL:FULL + 1, 0:REST * c], b).then_inc(loaded, 16)
            a, b = edges(src)
            sp.dma_start(number[0:FULL, :], a).then_inc(loaded, 16)
            sp.dma_start(number[FULL:FULL + 1, 0:REST], b).then_inc(loaded, 16)

        @block.gpsimd
        def _(pool):
            nc.gpsimd.memset(k["ones"][:, :], 1.0).then_inc(made, 1)
            nc.gpsimd.iota(cols_i[:, :], pattern=[[1, T]], base=0, channel_multiplier=0).then_inc(iotas, 1)
            nc.gpsimd.iota(part[:, 0, :], pattern=[[1, T]], base=0, channel_multiplier=T).then_inc(iotas, 1)
            pool.wait_ge(made, 1)
            nc.gpsimd.affine_select(out=k["ident"][:, :], in_=k["ones"][:, :], compare_op=ALU.is_equal, fill=0.0,
                                    base=0, pattern=[[-1, P]], channel_multiplier=1).then_inc(made, 1)
            nc.gpsimd.affine_select(out=k["below"][:, :], in_=k["ones"][:, :], compare_op=ALU.is_gt, fill=0.0,
                                    base=0, pattern=[[1, P]], channel_multiplier=-1).then_inc(made, 1)

            def body(i):
                for par in range(2):
                    g = 2 * i + par
                    for c in range(2):
                        wait(pool, staged, 2 * g + c + 1, passed)
                        for j in range(J):
                            nc.gpsimd.indirect_dma_start(
                                d[f"sorted_{'rs'[c]}"], bass.IndirectOffsetOnAxis(ap=idx[:, par, c, j:j + 1], axis=0),
                                out_rows[:, par, c, j, :], None).then_inc(sent[par], 16)
            loop(pool, body)
            pool.wait_ge(sent[0], 16 * J * G)
            pool.wait_ge(sent[1], 16 * J * G)

        @block.vector
        def _(v):
            steps = [0]

            def step(ins):
                steps[0] += 1
                ins.then_inc(ready, 1)
                v.wait_ge(ready, steps[0])

            for tile, value in ((key[0], PAD), (key[1], PAD), (other, 0), (number, 0), (weight, 0), (attr, 0)):
                nc.vector.memset(tile[:, :], value).then_inc(fills, 1)
            nc.vector.memset(k["eps"][:, :], LN_EPS)
            nc.vector.memset(k["one_rows"][:, :], 1.0)
            nc.vector.memset(ones_row[:, :], 1.0)
            nc.vector.memset(fields[0][:, :, :], 0.0)
            step(nc.vector.memset(fields[1][:, :, :], 0.0))
            v.wait_ge(made, 3)
            nc.vector.tensor_copy(k["ident16"][:, :], k["ident"][:, :])
            nc.vector.tensor_copy(k["below16"][:, :], k["below"][:, :])
            v.wait_ge(iotas, 2)
            nc.vector.tensor_copy(k["cols16"][:, :], cols_i[:, :])
            v.wait_ge(loaded, 16 * 12)
            f0, f1 = fields
            nc.vector.tensor_copy(f0[:, :, 0], key[0][:, :])
            nc.vector.tensor_copy(f0[:, :, 1], number[:, :])
            nc.vector.tensor_scalar(f0[:, :, 2], part[:, 0, :], float(N - 1), None, ALU.min)
            nc.vector.tensor_copy(f0[:, :, 3], weight[:, :])
            nc.vector.tensor_copy(f0[:, :, 4:7], attr[:, :].rearrange("p (t c) -> p t c", c=3))
            nc.vector.tensor_copy(f1[:, :, 0], key[1][:, :])
            nc.vector.tensor_copy(f1[:, :, 1], other[:, :])
            step(nc.vector.tensor_copy(f1[:, :, 3], weight[:, :]))
            for c in range(2):
                step(nc.vector.tensor_scalar(part[:, 0, :], key[c][:, :], 2, P - 1, ALU.logical_shift_right, ALU.bitwise_and))
                step(nc.vector.tensor_copy(lo[c][:, :], part[:, 0, :]))
                step(nc.vector.tensor_scalar(part[:, 0, :], key[c][:, :], 9, 2, ALU.logical_shift_right, ALU.logical_shift_left))
                step(nc.vector.tensor_scalar(part[:, 1, :], key[c][:, :], J - 1, None, ALU.bitwise_and))
                step(nc.vector.tensor_tensor(part[:, 0, :], part[:, 0, :], part[:, 1, :], ALU.bitwise_or))
                step(nc.vector.tensor_copy(hi[c][:, :], part[:, 0, :]))

            def one_hots(t, slot, done):
                for c in range(2):
                    nc.vector.tensor_scalar(one_lo[:, c, slot, :], k["cols16"][:, 0:P], lo[c][:, ds(t)], None, ALU.is_equal)
                    nc.vector.tensor_scalar(one_hi[:, c, slot, :], k["cols16"][:, :], hi[c][:, ds(t)], None,
                                            ALU.is_equal).then_inc(done, 1)

            def count_body(i):
                for r in range(4):
                    wait(v, counted, 2 * (4 * i + r - 3))
                    one_hots(4 * i + r, r, hot)
            count_body(0)
            with v.Fori(1, G) as i:
                count_body(i)
            v.wait_ge(counted, 2 * T)
            for c in range(2):
                step(nc.vector.tensor_copy(count[:, c, :], run_ps[c][:, 0:T]))
            v.sem_inc(hist, 1)
            step(nc.vector.tensor_scalar(degree[:, :], count[:, 0, :], 1.0, None, ALU.add))
            v.sem_inc(hist, 1)
            for c in range(2):
                v.wait_ge(summed, c + 1)
                step(nc.vector.tensor_copy(total[:, :], look_ps[c][:, 0:T]))
                step(nc.vector.tensor_tensor_scan(scan[:, :], ones_row[:, :], total[:, :], 0.0, ALU.mult, ALU.add))
                step(nc.vector.tensor_tensor(scan[:, :], scan[:, :], total[:, :], ALU.subtract))
                step(nc.vector.tensor_tensor(begin[:, c, :], scan[:, :], same_ps[c][:, 0:T], ALU.add))
            v.sem_inc(begun, 1)
            v.wait_ge(rooted, 1)
            nc.vector.reciprocal(k["dinv"][:, :], degree[:, :])

            def rank_body(i, last=False):
                for r in range(4):
                    t = 4 * i + r
                    if not (last and r >= 2):
                        wait(v, updated, 2 * (t - 1))
                        one_hots(t + 2, (r + 2) % 4, hot2)
                    for c in range(2):
                        wait(v, looked, 2 * t + c + 1)
                        wait(v, ranked, 2 * t + c - 1)
                        if r == 0:
                            wait(v, placed, i)
                        nc.vector.tensor_tensor_reduce(picked[:, c, :], look_ps[c][:, 0:T], one_hi[:, c, r, :], 1.0, 0.0,
                                                       ALU.mult, ALU.add, found[:, c, r:r + 1]).then_inc(ranked, 1)
                    if not (last and r == 3):
                        for c in range(2):
                            wait(v, same, 2 * t + c + 3)
                            nc.vector.tensor_tensor(same16[:, c, (r + 1) % 2, :], same_ps[c][:, 0:P], k["below16"][:, :],
                                                    ALU.mult).then_inc(masked, 1)
                wait(v, ranked, 8 * (i + 1))
                nc.vector.tensor_copy(place[:, :, ds(4 * i, 4)], found[:, :, :]).then_inc(placed, 1)
            one_hots(0, 0, hot2)
            one_hots(1, 1, hot2)
            for c in range(2):
                wait(v, same, c + 1)
                nc.vector.tensor_tensor(same16[:, c, 0, :], same_ps[c][:, 0:P], k["below16"][:, :],
                                        ALU.mult).then_inc(masked, 1)
            rank_body(0)
            with v.Fori(1, G - 1) as i:
                rank_body(i)
            rank_body(G - 1, last=True)
            v.wait_ge(placed, G)
            step(nc.vector.tensor_copy(place_i[:, :, :], place[:, :, :]))
            step(nc.vector.tensor_scalar(row_i[:, :, :], place_i[:, :, :], P - 1, None, ALU.bitwise_and))
            step(nc.vector.tensor_scalar(place_i[:, :, :], place_i[:, :, :], 7, None, ALU.logical_shift_right))
            step(nc.vector.tensor_copy(place[:, :, :], place_i[:, :, :]))
            step(nc.vector.tensor_copy(begin[:, :, :], row_i[:, :, :]))
            step(nc.vector.scalar_tensor_tensor(place[:, :, :], begin[:, :, :], float(T), place[:, :, :], ALU.mult, ALU.add))
            step(nc.vector.tensor_copy(row_i[:, :, :], place[:, :, :]))

            def stage_body(i):
                for par in range(2):
                    g = 2 * i + par
                    wait(v, sent[par], 16 * 2 * J * i)
                    for c in range(2):
                        nc.vector.tensor_copy(idx[:, par, c, :], row_i[:, c, ds(g * J, J)])
                        nc.vector.tensor_copy(out_rows[:, par, c, :, :], fields[c][:, ds(g * J, J), :]).then_inc(staged, 1)
            loop(v, stage_body)

        @block.scalar
        def _(act):
            act.wait_ge(hist, 2)
            nc.scalar.activation(degree[:, :], degree[:, :], ACT.Sqrt).then_inc(rooted, 1)

            def transposed(t_wait, c, slot, free):
                wait(act, turned, t_wait)
                wait(act, updated, free)
                nc.scalar.copy(lo_t16[:, c, slot, :], turn_ps[c][:, 0:P])
                nc.scalar.copy(lo_t[:, c, slot, :], turn_ps[c][:, 0:P]).then_inc(turned_out, 1)

            def running(c, need):
                wait(act, updated, need)
                nc.scalar.copy(table[:, c, :], run_ps[c][:, 0:T]).then_inc(tabled, 1)

            def body(i, last=False):
                for r in range(4):
                    t = 4 * i + r
                    if last and r == 3:
                        continue
                    for c in range(2):
                        transposed(2 * t + c + 3, c, (r + 1) % 2, 2 * t)
                    for c in range(2):
                        running(c, 2 * t + c + 1)
            for c in range(2):
                transposed(c + 1, c, 0, 0)
            act.wait_ge(summed, 3)
            for c in range(2):
                nc.scalar.copy(table[:, c, :], run_ps[c][:, 0:T]).then_inc(tabled, 1)
            body(0)
            with act.Fori(1, G - 1) as i:
                body(i)
            body(G - 1, last=True)

        @block.tensor
        def _(pe):
            def count_body(i, first=False, last=False):
                for r in range(4):
                    for c in range(2):
                        wait(pe, hot, 2 * (4 * i + r) + c + 1)
                        nc.tensor.matmul(run_ps[c][:, 0:T], one_lo[:, c, r, :], one_hi[:, c, r, :],
                                         start=first and r == 0, stop=last and r == 3).then_inc(counted, 1)
            count_body(0, first=True)
            with pe.Fori(1, G - 1) as i:
                count_body(i)
            count_body(G - 1, last=True)
            pe.wait_ge(hist, 2)
            pe.wait_ge(made, 3)
            for c in range(2):
                nc.tensor.matmul(look_ps[c][:, 0:T], k["ones"][:, :], count[:, c, :], start=True, stop=True)
                nc.tensor.matmul(same_ps[c][:, 0:T], k["below"][:, :], count[:, c, :], start=True, stop=True).then_inc(summed, 1)
            pe.wait_ge(begun, 1)
            for c in range(2):
                last = nc.tensor.matmul(run_ps[c][:, 0:T], k["ident"][:, :], begin[:, c, :], start=True, stop=True)
            last.then_inc(summed, 1)

            def turn(slot, need, free):
                for c in range(2):
                    wait(pe, hot2, need + c)
                    wait(pe, turned_out, free)
                    nc.tensor.transpose(turn_ps[c][:, 0:P], one_lo[:, c, slot, :], k["ident16"][:, :]).then_inc(turned, 1)

            def alike(slot, need, free):
                for c in range(2):
                    wait(pe, turned_out, need + c)
                    wait(pe, masked, free)
                    nc.tensor.matmul(same_ps[c][:, 0:P], lo_t16[:, c, slot, :], lo_t16[:, c, slot, :],
                                     start=True, stop=True).then_inc(same, 1)

            def body(i, last=False):
                for r in range(4):
                    t = 4 * i + r
                    more = not (last and r == 3)
                    if more:
                        turn((r + 1) % 4, 2 * t + 3, 2 * t + 2)
                    for c in range(2):
                        wait(pe, tabled, 2 * t + c + 1)
                        wait(pe, masked, 2 * t + c + 1)
                        wait(pe, ranked, 2 * (t - 1) + c + 1)
                        nc.tensor.matmul(look_ps[c][:, 0:T], lo_t[:, c, r % 2, :], table[:, c, :], start=True, stop=False)
                        nc.tensor.matmul(look_ps[c][:, 0:T], same16[:, c, r % 2, :], one_hi[:, c, r, :],
                                         start=False, stop=True).then_inc(looked, 1)
                        nc.tensor.matmul(run_ps[c][:, 0:T], one_lo[:, c, r, :], one_hi[:, c, r, :],
                                         start=False, stop=True, skip_group_check=True).then_inc(updated, 1)
                    if more:
                        alike((r + 1) % 2, 2 * t + 3, 2 * t + 2)
            turn(0, 1, 0)
            alike(0, 1, 0)
            body(0)
            with pe.Fori(1, G - 1) as i:
                body(i)
            body(G - 1, last=True)


def order_tables(nc, k, d):
    H = T // J
    with nc.cleanup_on_exit(), ExitStack() as ctx:
        ph = Phase(nc, ctx)
        sb, ps, sem = ph.sb, ph.ps, ph.sem
        ZC = 28 * P
        fields = [sb("fields0", [P, T, 8]), sb("fields1", [P, T, 8])]
        zeros = sb("zeros", [P, 32 * (P + 1)])
        minus = sb("minus", [1, 1])
        turned_sb = sb("turned_sb", [H, J, P])
        after = sb("after", [H, J, P])
        differs = sb("differs", [H, J, P])
        target = sb("target", [P, T])
        turn_ps = ps("turn", [H, 512])
        back_ps = ps("back", [P, 512])
        loaded, made, ready, stored, cleared = sem("loaded"), sem("made"), sem("ready"), sem("stored"), sem("cleared")
        cut, turned, copied, lined, read, compared, back = (sem(n) for n in
                                                            ("cut", "turned", "copied", "lined", "read", "compared", "back"))
        block = ctx.enter_context(nc.Block())

        def line_blocks(c, shift):
            return d["line_" + c][shift:NP + shift].rearrange("(b r e) -> r b e", r=H, e=P)

        @block.sync
        def _(sp):
            for n, c in enumerate("rs"):
                sp.dma_start(fields[n][:, :, :], d["sorted_" + c].rearrange("(p t) f -> p t f", t=T)).then_inc(loaded, 16)
            sp.wait_ge(made, 2)
            for c in "rs":
                sp.dma_start(d["line_" + c][NP:NP + 1].rearrange("(a b) -> a b", a=1), minus[:, :]).then_inc(stored, 16)
            for n, c in enumerate("rs"):
                sp.wait_ge(copied, n + 1)
                sp.dma_start(line_blocks(c, 0), turned_sb[:, :, :]).then_inc(lined, 16)
                sp.wait_ge(lined, 16 * (n + 1))
                sp.wait_ge(stored, 32)
                sp.dma_start(after[:, :, :], line_blocks(c, 1)).then_inc(read, 16)

        @block.scalar
        def _(act):
            act.wait_ge(made, 2)
            sums = (("sum_r", T * P, 28 * P), ("sum_s", T * (P + 1), 28 * (P + 1)))
            for name, width, step in sums:
                flat = d[name].rearrange("(p t) d -> p (t d)", p=P)
                for at in range(0, width, step):
                    act.dma_start(flat[:, at:at + step], zeros[:, 0:step]).then_inc(cleared, 16)
            act.wait_ge(cleared, 16 * 2 * (T // 28))

        @block.tensor
        def _(pe):
            for n, c in enumerate("rs"):
                pe.wait_ge(cut, n + 1)
                for b in range(J):
                    last = nc.tensor.transpose(turn_ps[:, b * P:(b + 1) * P], k["key_" + c][:, b * H:(b + 1) * H], k["ident"][:, :])
                last.then_inc(turned, 1)
                pe.wait_ge(compared, n + 1)
                for b in range(J):
                    last = nc.tensor.transpose(back_ps[:, b * H:(b + 1) * H], differs[:, b, :], k["ident"][0:H, 0:H])
                last.then_inc(back, 1)

        @block.vector
        def _(v):
            steps = [0]

            def step(ins):
                steps[0] += 1
                ins.then_inc(ready, 1)
                v.wait_ge(ready, steps[0])

            nc.vector.memset(zeros[:, :], 0.0).then_inc(made, 1)
            nc.vector.memset(minus[:, :], -1.0).then_inc(made, 1)
            v.wait_ge(loaded, 32)
            for n, c in enumerate("rs"):
                nc.vector.tensor_copy(k["key_" + c][:, :], fields[n][:, :, 0]).then_inc(cut, 1)
                nc.vector.tensor_copy(k["from_" + c][:, :], fields[n][:, :, 1])
                nc.vector.tensor_copy(k["weight_" + c][:, :], fields[n][:, :, 3])
            nc.vector.tensor_copy(k["edge_r"][:, :], fields[0][:, :, 2])
            nc.vector.tensor_copy(k["vec_r"][:, :, :], fields[0][:, :, 4:7])
            for n, c in enumerate("rs"):
                v.wait_ge(cut, n + 1)
                step(nc.vector.memset(k["before_" + c][:, :], -1.0))
                step(nc.vector.tensor_scalar(target[:, 1:T], k["key_" + c][:, 0:T - 1], 1.0, k["ident"][:, P - 1:P],
                                             ALU.add, ALU.mult))
                step(nc.vector.tensor_scalar(k["before_" + c][:, 1:T], target[:, 1:T], -1.0, None, ALU.add))
                v.wait_ge(turned, n + 1)
                if n:
                    v.wait_ge(lined, 16)
                step(nc.vector.tensor_copy(turned_sb[:, :, :], turn_ps[:, :].rearrange("r (b e) -> r b e", b=J)))
                v.sem_inc(copied, 1)
                v.wait_ge(read, 16 * (n + 1))
                if n:
                    v.wait_ge(back, 1)
                nc.vector.tensor_tensor(differs[:, :, :], turned_sb[:, :, :], after[:, :, :], ALU.not_equal).then_inc(compared, 1)
                v.wait_ge(back, n + 1)
                step(nc.vector.tensor_scalar(target[:, :], back_ps[:, 0:T], -float(SKIP), float(SKIP), ALU.mult, ALU.add))
                step(nc.vector.tensor_tensor(target[:, :], target[:, :], k["key_" + c][:, :], ALU.add))
                step(nc.vector.tensor_copy(k["to_" + c][:, :], target[:, :]))


def segment_sum(nc, k, c, sums, width=P, table=None, messages=None, added=None, weight=None):
    with nc.cleanup_on_exit(), ExitStack() as ctx:
        ph = Phase(nc, ctx)
        sb, ps, sem = ph.sb, ph.ps, ph.sem
        key, before, to, source = (k[n + c] for n in ("key_", "before_", "to_", "from_"))
        rows = sb("rows", [P, 2, J, width])
        plus = sb("plus", [P, 2, W]) if added is not None else None
        relu = sb("relu", [P, 2, J, P]) if added is not None else None
        line = sb("line", [P, 2, W])
        equal = sb("equal", [P, 2, J, P])
        carry = sb("carry", [P, 2, J, P])
        sum_sb = sb("sum_sb", [P, 2, J, width])
        idx = sb("idx", [P, 2, J], I32)
        to_idx = sb("to_idx", [P, 2, J], I32)
        sum_ps = [ps(f"sum{n}", [P, 512]) for n in range(2 * J)]
        came = [sem("came0"), sem("came1")]
        lined = [sem("lined0"), sem("lined1")]
        plussed = [sem("plussed0"), sem("plussed1")]
        sent = [sem("sent0"), sem("sent1")]
        staged, to_staged, built, summed, taken = (sem(n) for n in ("staged", "to_staged", "built", "summed", "taken"))
        both, ready, ones_in, passed, passed_sp = (sem(n) for n in ("both", "ready", "ones_in", "passed", "passed_sp"))
        block = ctx.enter_context(nc.Block())
        line_rows = k["line"][c][0:NP].rearrange("(g w) -> g w", w=W)
        source_rows = relu if added is not None else rows

        def psum(par, j):
            return sum_ps[J * par + j][:, 0:width]

        @block.sync
        def _(sp):
            def body(i):
                for par in range(2):
                    g = 2 * i + par
                    wait(sp, built, g - 1, passed_sp)
                    sp.dma_start(line[:, par, :], line_rows[ds(g), :].to_broadcast([P, W])).then_inc(lined[par], 16)
                    if added is not None:
                        wait(sp, ready, g - 1, passed_sp)
                        sp.dma_start(plus[:, par, :], block_of(added, g)).then_inc(plussed[par], 16)
                    if messages is not None:
                        wait(sp, summed, J * (g - 1), passed_sp)
                        sp.dma_start(rows[:, par, :, :].rearrange("p j d -> p (j d)"), block_of(messages, g)).then_inc(came[par], 16)
            loop(sp, body)

        @block.gpsimd
        def _(pool):
            def gather(g, par, i):
                wait(pool, staged, g + 1, passed)
                wait(pool, summed, J * (g - 1), passed)
                for j in range(J):
                    nc.gpsimd.indirect_dma_start(rows[:, par, j, 0:P], None, table,
                                                 bass.IndirectOffsetOnAxis(ap=idx[:, par, j:j + 1], axis=0)).then_inc(came[par], 16)

            def scatter(g, par):
                wait(pool, to_staged, g + 1, passed)
                wait(pool, taken, J * (g + 1), passed)
                for j in range(J):
                    nc.gpsimd.indirect_dma_start(sums, bass.IndirectOffsetOnAxis(ap=to_idx[:, par, j:j + 1], axis=0),
                                                 sum_sb[:, par, j, :], None, bounds_check=NP - 1,
                                                 oob_is_err=False).then_inc(sent[par], 16)

            def body(i, last=False):
                for par in range(2):
                    g = 2 * i + par
                    if table is not None and not (last and par == 1):
                        gather(g + 1, 1 - par, i)
                    scatter(g, par)
            if width > P:
                nc.gpsimd.memset(rows[:, :, :, P:width], 1.0).then_inc(ones_in, 1)
            if table is not None:
                gather(0, 0, 0)
            body(0)
            with pool.Fori(1, G // 2 - 1) as i:
                body(i)
            body(G // 2 - 1, last=True)
            for par in range(2):
                pool.wait_ge(sent[par], 16 * J * (G // 2))

        @block.scalar
        def _(act):
            def body(i, last=False):
                for par in range(2):
                    g = 2 * i + par
                    if table is not None and not last:
                        wait(act, came[par], 16 * J * (i + 1))
                        nc.scalar.copy(idx[:, par, :], source[:, ds((g + 2) * J, J)]).then_inc(staged, 1)
                    wait(act, sent[par], 16 * J * i)
                    nc.scalar.copy(to_idx[:, par, :], to[:, ds(g * J, J)]).then_inc(to_staged, 1)
                    if added is not None:
                        wait(act, both, g + 1)
                        wait(act, summed, J * (g - 1))
                        nc.scalar.activation(relu[:, par, :, :].rearrange("p j d -> p (j d)"), plus[:, par, :], ACT.Relu).then_inc(ready, 1)
                    for j in range(J):
                        wait(act, summed, J * g + j + 1)
                        nc.scalar.copy(sum_sb[:, par, j, :], psum(par, j)).then_inc(taken, 1)
            if table is not None:
                for g in range(2):
                    nc.scalar.copy(idx[:, g, :], source[:, g * J:(g + 1) * J]).then_inc(staged, 1)
            body(0)
            with act.Fori(1, G // 2 - 1) as i:
                body(i)
            body(G // 2 - 1, last=True)

        @block.vector
        def _(v):
            def body(i):
                for par in range(2):
                    g = 2 * i + par
                    wait(v, lined[par], 16 * (i + 1))
                    wait(v, summed, J * (g - 1))
                    for j in range(J):
                        t = g * J + j
                        row = line[:, par, j * P:(j + 1) * P]
                        if weight is None:
                            nc.vector.tensor_scalar(equal[:, par, j, :], row, key[:, ds(t)], None, ALU.is_equal)
                        else:
                            nc.vector.tensor_scalar(equal[:, par, j, :], row, key[:, ds(t)], weight[:, ds(t)],
                                                    ALU.is_equal, ALU.mult)
                        last = nc.vector.tensor_scalar(carry[:, par, j, :], row, before[:, ds(t)], None, ALU.is_equal)
                    last.then_inc(built, 1)
                    if added is not None:
                        wait(v, came[par], 16 * J * (i + 1))
                        wait(v, plussed[par], 16 * (i + 1))
                        nc.vector.tensor_tensor(plus[:, par, :], plus[:, par, :], rows[:, par, :, :].rearrange("p j d -> p (j d)"),
                                                ALU.add).then_inc(both, 1)
            loop(v, body)

        @block.tensor
        def _(pe):
            def body(i, first=False):
                for par in range(2):
                    g = 2 * i + par
                    wait(pe, built, g + 1)
                    if added is not None:
                        wait(pe, ready, g + 1)
                    else:
                        wait(pe, came[par], 16 * (J if table is not None else 1) * (i + 1))
                    wait(pe, taken, J * (g - 1))
                    for j in range(J):
                        end = first and par == 0 and j == 0
                        m = nc.tensor.matmul(psum(par, j), equal[:, par, j, :], source_rows[:, par, j, :], start=True, stop=end)
                        if end:
                            m.then_inc(summed, 1)
                            continue
                        wait(pe, taken, J * g + j)
                        before_sb = sum_sb[:, par, j - 1, :] if j else sum_sb[:, 1 - par, J - 1, :]
                        nc.tensor.matmul(psum(par, j), carry[:, par, j, :], before_sb, start=False, stop=True).then_inc(summed, 1)
            if width > P:
                pe.wait_ge(ones_in, 1)
            body(0, first=True)
            with pe.Fori(1, G // 2 - 1) as i:
                body(i)
            body(G // 2 - 1)


def split_rows(nc, ph, biases):
    n = len(biases)
    row, rest = ph.sb("row", [1, n, P]), ph.sb("rest", [1, n, P])
    pieces = [ph.sb(f"piece{r}", [1, n, J, P], BF16) for r in range(3)]
    came, cut, spread = ph.sem("row_came"), ph.sem("row_cut"), ph.sem("row_spread")

    def sp_part(sp):
        for b, (bias, _) in enumerate(biases):
            sp.dma_start(row[:, b, :], bias.rearrange("(a n) -> a n", a=1)).then_inc(came, 16)
        sp.wait_ge(cut, 5)
        for b, (_, tile) in enumerate(biases):
            for r in range(3):
                sp.dma_start(tile[r:r + 1, :], pieces[r][:, b, :, :].rearrange("p j d -> p (j d)")).then_inc(spread, 16)
        sp.wait_ge(spread, 16 * 3 * n)

    def v_part(v):
        v.wait_ge(came, 16 * n)
        of = row
        for r in range(3):
            wide = of[:, :, :].unsqueeze(2).to_broadcast([1, n, J, P])
            nc.vector.tensor_copy(pieces[r][:, :, :, :], wide).then_inc(cut, 1)
            v.wait_ge(cut, 2 * r + 1)
            if r < 2:
                nc.vector.tensor_tensor(rest[:, :, :], of[:, :, :], pieces[r][:, :, 0, :], ALU.subtract).then_inc(cut, 1)
                v.wait_ge(cut, 2 * r + 2)
                of = rest
    return sp_part, v_part


def tensor_product_weights(nc, k, w, ctx):
    t = {n: ctx.enter_context(nc.sbuf_tensor("tp_" + n, s, F32)) for n, s in {
        "up": [P, P], "mlp0": [J * NB, J, HID], "mlp1": [HID, HID], "mlp2": [HID, P], "mb0": [HID, 1], "mb1": [HID, 1],
        "out": [P, 2, P], "basis": [P, T, NB], "unit": [P, T, 3], "dir": [P, T, 3]}.items()}
    t["mb2"] = ctx.enter_context(nc.sbuf_tensor("tp_mb2", [3, W], BF16))
    with nc.cleanup_on_exit(), ExitStack() as inner:
        ph = Phase(nc, inner)
        sb, sem = ph.sb, ph.sem
        up1 = sb("up1", [P, MUL])
        out0 = sb("out0", [2 * MUL, MUL])
        out1 = sb("out1", [P, 2, MUL])
        centre_i = sb("centre_i", [P, NB], I32)
        centre = sb("centre", [P, NB])
        clipped = sb("clipped", [P, T])
        away = sb("away", [P, T, NB])
        square = sb("square", [P, T, 3])
        length = sb("length", [P, T])
        cleared, loaded, ready, numbered, away_in, rooted, squared, waved = (sem(n) for n in (
            "cleared", "loaded", "ready", "numbered", "away_in", "rooted", "squared", "waved"))
        row_sp, row_v = split_rows(nc, ph, [(w["mlp_b2"], t["mb2"])])
        block = inner.enter_context(nc.Block())

        @block.sync
        def _(sp):
            sp.wait_ge(cleared, 3)
            sp.dma_start(t["up"][0:MUL, 0:MUL], w["W_up0"]).then_inc(loaded, 16)
            for c in range(3):
                sp.dma_start(t["up"][MUL + c:P:3, MUL * (c + 1):MUL * (c + 2)], w["W_up1"]).then_inc(loaded, 16)
            for j in range(J):
                sp.dma_start(t["mlp0"][j * NB:(j + 1) * NB, j, :], w["mlp_w0"]).then_inc(loaded, 16)
            sp.dma_start(t["mlp1"][:, :], w["mlp_w1"]).then_inc(loaded, 16)
            sp.dma_start(t["mlp2"][:, :], w["mlp_w2"]).then_inc(loaded, 16)
            sp.dma_start(t["mb0"][:, :], w["mlp_b0"].rearrange("(n a) -> n a", a=1)).then_inc(loaded, 16)
            sp.dma_start(t["mb1"][:, :], w["mlp_b1"].rearrange("(n a) -> n a", a=1)).then_inc(loaded, 16)
            sp.dma_start(t["out"][0:2 * MUL, 0, 0:MUL], w["W_out0"]).then_inc(loaded, 16)
            for half in range(2):
                sp.dma_start(out1[half * 2 * MUL:(half + 1) * 2 * MUL, 0, :], w["W_out1"]).then_inc(loaded, 16)
            row_sp(sp)

        @block.gpsimd
        def _(pool):
            nc.gpsimd.iota(centre_i[:, :], pattern=[[1, NB]], base=0, channel_multiplier=0).then_inc(numbered, 1)

        @block.scalar
        def _(act):
            act.wait_ge(squared, 1)
            nc.scalar.activation(length[:, :], length[:, :], ACT.Sqrt).then_inc(rooted, 1)
            act.wait_ge(away_in, 1)
            nc.scalar.activation(t["basis"][:, :, :], away[:, :, :], ACT.Exp, scale=-0.5 * (NB - 1) ** 2).then_inc(waved, 1)

        @block.vector
        def _(v):
            steps = [0]

            def step(ins):
                steps[0] += 1
                ins.then_inc(ready, 1)
                v.wait_ge(ready, steps[0])

            for name in ("up", "mlp0", "out"):
                tile = t[name]
                nc.vector.memset(tile[:, :] if name == "up" else tile[:, :, :], 0.0).then_inc(cleared, 1)
            row_v(v)
            step(nc.vector.tensor_tensor(square[:, :, :], k["vec_r"][:, :, :], k["vec_r"][:, :, :], ALU.mult))
            step(nc.vector.tensor_tensor(length[:, :], square[:, :, 0], square[:, :, 1], ALU.add))
            nc.vector.tensor_tensor(length[:, :], length[:, :], square[:, :, 2], ALU.add).then_inc(squared, 1)
            weight = k["weight_r"]
            v.wait_ge(numbered, 1)
            step(nc.vector.tensor_copy(centre[:, :], centre_i[:, :]))
            step(nc.vector.tensor_scalar(centre[:, :], centre[:, :], 1.0 / (NB - 1), None, ALU.mult))
            step(nc.vector.tensor_scalar(clipped[:, :], weight[:, :], 0.0, 1.0, ALU.max, ALU.min))
            step(nc.vector.tensor_tensor(away[:, :, :], clipped[:, :].unsqueeze(2).to_broadcast([P, T, NB]),
                                         centre[:, :].unsqueeze(1).to_broadcast([P, T, NB]), ALU.subtract))
            nc.vector.tensor_tensor(away[:, :, :], away[:, :, :], away[:, :, :], ALU.mult).then_inc(away_in, 1)
            v.wait_ge(rooted, 1)
            step(nc.vector.tensor_scalar(length[:, :], length[:, :], 1e-12, None, ALU.add))
            step(nc.vector.reciprocal(length[:, :], length[:, :]))
            step(nc.vector.tensor_tensor(t["unit"][:, :, :], k["vec_r"][:, :, :],
                                         length[:, :].unsqueeze(2).to_broadcast([P, T, 3]), ALU.mult))
            step(nc.vector.tensor_scalar(t["dir"][:, :, :], t["unit"][:, :, :], 3.0 ** 0.5, None, ALU.mult))
            step(nc.vector.tensor_scalar(clipped[:, :], weight[:, :], 1.0, NB ** 0.5, ALU.is_le, ALU.mult))
            v.wait_ge(waved, 1)
            nc.vector.tensor_tensor(t["basis"][:, :, :], t["basis"][:, :, :],
                                    clipped[:, :].unsqueeze(2).to_broadcast([P, T, NB]), ALU.mult)
            v.wait_ge(loaded, 16 * 15)
            nc.vector.tensor_scalar(t["up"][:, :], t["up"][:, :], MUL ** -0.5, None, ALU.mult)
            scale = (2 * MUL) ** -0.5 / AVG
            nc.vector.tensor_scalar(t["out"][0:2 * MUL, 0, 0:MUL], t["out"][0:2 * MUL, 0, 0:MUL], scale, None, ALU.mult)
            for c in range(3):
                half, at = (c + 1) % 2, (c + 1) // 2
                rows = slice(half * 2 * MUL, (half + 1) * 2 * MUL)
                nc.vector.tensor_scalar(t["out"][rows, at, MUL + c:P:3], out1[rows, 0, :], scale, None, ALU.mult)
    return t


def edge_products(nc, k, x, t, messages):
    with nc.cleanup_on_exit(), ExitStack() as ctx:
        ph = Phase(nc, ctx)
        sb, ps, sem = ph.sb, ph.ps, ph.sem
        rows = sb("rows", [P, 2, J, P])
        idx = sb("idx", [P, 2, J], I32)
        wave = sb("wave", [P, 2, J * NB])
        wave_t = sb("wave_t", [J * NB, 2, P])
        rows_t = sb("rows_t", [P, 2, W])
        hid0 = sb("hid0", [HID, 2, W])
        hid1 = sb("hid1", [HID, 2, W])
        gate = sb("gate", [P, 2, J, P])
        up = sb("up", [P, 2, J, P])
        mixed = sb("mixed", [P, 2, J, 2 * P])
        along = sb("along", [P, J, MUL])
        part = sb("part", [P, 3, J, MUL])
        dot = sb("dot", [P, J, MUL])
        mixed_t = sb("mixed_t", [P, 2, 2, W])
        out = sb("out", [P, 2, W])
        wave_ps = ps("wave", [J * NB, 512])
        turn_ps = ps("turn", [P, 512])
        up_ps = ps("up", [P, J, P])
        hid_ps = ps("hid", [HID, 512])
        gate_ps = ps("gate", [P, J, P])
        mix_ps = [ps("mix0", [P, 512]), ps("mix1", [P, 512])]
        out_ps = ps("out", [P, 512])
        came = [sem("came0"), sem("came1")]
        stored = [sem("stored0"), sem("stored1")]
        (staged, waved, wave_up, wave_down, rows_up, rows_down, up_up, up_down, hid0_up, hid0_down, hid1_up, hid1_down,
         gate_up, gate_down, dots, mixed_in, mix0_up, mix0_down, mix1_up, mix1_down, out_up, out_down, passed, passed_sp,
         passed_pe) = (sem(n) for n in (
            "staged", "waved", "wave_up", "wave_down", "rows_up", "rows_down", "up_up", "up_down", "hid0_up", "hid0_down",
            "hid1_up", "hid1_down", "gate_up", "gate_down", "dots", "mixed_in", "mix0_up", "mix0_down", "mix1_up", "mix1_down",
            "out_up", "out_down", "passed", "passed_sp", "passed_pe"))
        block = ctx.enter_context(nc.Block())

        @block.gpsimd
        def _(pool):
            def gather(i, g, par):
                wait(pool, staged, g + 1, passed)
                wait(pool, rows_up, g - 1, passed)
                for j in range(J):
                    nc.gpsimd.indirect_dma_start(rows[:, par, j, :], None, x,
                                                 bass.IndirectOffsetOnAxis(ap=idx[:, par, j:j + 1], axis=0)).then_inc(came[par], 16)
            paced(pool, (gather, 0))

        @block.sync
        def _(sp):
            def store(i, g, par):
                wait(sp, out_down, g + 1, passed_sp)
                sp.dma_start(block_of(messages, g), out[:, par, :]).then_inc(stored[par], 16)
            paced(sp, (store, 0))
            for par in range(2):
                sp.wait_ge(stored[par], 16 * (G // 2))

        @block.scalar
        def _(act):
            def down(to, of, up_sem, down_sem, used, func=ACT.Copy, bias=None):
                def part(i, g, par):
                    wait(act, up_sem, g + 1)
                    wait(act, used, g - 1)
                    if bias is None:
                        nc.scalar.copy(to(par), of).then_inc(down_sem, 1)
                    else:
                        nc.scalar.activation(to(par), of, func, bias=bias).then_inc(down_sem, 1)
                return part

            def out_part(i, g, par):
                wait(act, out_up, g + 1)
                wait(act, stored[par], 16 * i)
                nc.scalar.copy(out[:, par, :], out_ps[:, :]).then_inc(out_down, 1)

            paced(act,
                  (down(lambda q: hid1[:, q, :], hid_ps[:, :], hid1_up, hid1_down, gate_up, func=ACT.Silu, bias=t["mb1"][:, :]), 1),
                  (down(lambda q: gate[:, q, :, :], gate_ps[:, :, :], gate_up, gate_down, mixed_in), 0),
                  (out_part, -3),
                  (down(lambda q: hid0[:, q, :], hid_ps[:, :], hid0_up, hid0_down, hid1_up, func=ACT.Silu, bias=t["mb0"][:, :]), 2),
                  (down(lambda q: up[:, q, :, :], up_ps[:, :, :], up_up, up_down, mixed_in), 0),
                  (down(lambda q: mixed_t[:, q, 1, :], mix_ps[1][:, :], mix1_up, mix1_down, out_up), -2),
                  (down(lambda q: wave_t[:, q, :], wave_ps[:, 0:P], wave_up, wave_down, hid0_up), 3),
                  (down(lambda q: rows_t[:, q, :], turn_ps[:, :], rows_up, rows_down, up_up), 1))

        @block.vector
        def _(v):
            def stage(i, g, par):
                wait(v, wave_up, g - 1)
                nc.vector.tensor_copy(wave[:, par, :], t["basis"][:, ds(g * J, J), :].rearrange("p t n -> p (t n)")).then_inc(waved, 1)
                wait(v, came[par], 16 * J * i)
                nc.vector.tensor_copy(idx[:, par, :], k["from_r"][:, ds(g * J, J)]).then_inc(staged, 1)

            def mix(i, g, par):
                wait(v, gate_down, g + 1)
                wait(v, up_down, g + 1)
                wait(v, mix1_up, g - 1)
                f, w, m = up[:, par, :, :], gate[:, par, :, :], mixed[:, par, :, :]
                unit, along_dir = (t[n][:, ds(g * J, J), :] for n in ("unit", "dir"))
                nc.vector.tensor_tensor(along[:, :, :], w[:, :, MUL:2 * MUL], f[:, :, 0:MUL], ALU.mult)
                for c in range(3):
                    last = nc.vector.tensor_tensor(part[:, c, :, :], f[:, :, MUL * (c + 1):MUL * (c + 2)],
                                                   unit[:, :, c:c + 1].to_broadcast([P, J, MUL]), ALU.mult)
                last.then_inc(dots, 1)
                nc.vector.tensor_tensor(m[:, :, 0:MUL], w[:, :, 0:MUL], f[:, :, 0:MUL], ALU.mult)
                for c in range(3):
                    at = 2 * MUL * (c + 1)
                    nc.vector.tensor_tensor(m[:, :, at + MUL:at + 2 * MUL], w[:, :, 2 * MUL:3 * MUL],
                                            f[:, :, MUL * (c + 1):MUL * (c + 2)], ALU.mult)
                wait(v, dots, 3 * g + 1)
                nc.vector.tensor_tensor(dot[:, :, :], part[:, 0, :, :], part[:, 1, :, :], ALU.add).then_inc(dots, 1)
                for c in range(3):
                    at = 2 * MUL * (c + 1)
                    nc.vector.tensor_tensor(m[:, :, at:at + MUL], along[:, :, :],
                                            along_dir[:, :, c:c + 1].to_broadcast([P, J, MUL]), ALU.mult)
                wait(v, dots, 3 * g + 2)
                nc.vector.tensor_tensor(part[:, 0, :, :], dot[:, :, :], part[:, 2, :, :], ALU.add).then_inc(dots, 1)
                wait(v, dots, 3 * g + 3)
                nc.vector.tensor_tensor(m[:, :, MUL:2 * MUL], part[:, 0, :, :], w[:, :, 3 * MUL:4 * MUL], ALU.mult).then_inc(mixed_in, 1)

            def mix_down(i, g, par):
                wait(v, mix0_up, g + 1)
                wait(v, out_up, g - 1)
                nc.vector.tensor_copy(mixed_t[:, par, 0, :], mix_ps[0][:, :]).then_inc(mix0_down, 1)

            def head(i, g, par):
                wait(v, mixed_in, g)
            paced(v, (stage, 4), (mix_down, -2), (head, -1), (mix, -1))

        @block.tensor
        def _(pe):
            def hid1_part(i, g, par):
                wait(pe, hid0_down, g + 1, passed_pe)
                wait(pe, hid1_down, g, passed_pe)
                nc.tensor.matmul(hid_ps[:, :], t["mlp1"][:, :], hid0[:, par, :], start=True, stop=True).then_inc(hid1_up, 1)

            def gate_part(i, g, par):
                wait(pe, hid1_down, g + 1)
                wait(pe, gate_down, g)
                nc.tensor.matmul(gate_ps[:, :, :].rearrange("p j d -> p (j d)"), k["one_rows"][:, :], t["mb2"][:, :], start=True, stop=False)
                for j in range(J):
                    m = nc.tensor.matmul(gate_ps[:, j, :], hid1[:, par, j * P:(j + 1) * P], t["mlp2"][:, :], start=False, stop=j == J - 1)
                m.then_inc(gate_up, 1)

            def out_part(i, g, par):
                wait(pe, mix0_down, g + 1)
                wait(pe, mix1_down, g + 1)
                wait(pe, out_down, g)
                for j in range(J):
                    for h in range(2):
                        m = nc.tensor.matmul(out_ps[:, j * P:(j + 1) * P], mixed_t[:, par, h, j * P:(j + 1) * P], t["out"][:, h, :],
                                             start=h == 0, stop=h == 1)
                m.then_inc(out_up, 1)

            def hid0_part(i, g, par):
                wait(pe, wave_down, g + 1)
                wait(pe, hid1_down, g)
                for j in range(J):
                    m = nc.tensor.matmul(hid_ps[:, j * P:(j + 1) * P], t["mlp0"][:, j, :], wave_t[:, par, :], start=True, stop=True)
                m.then_inc(hid0_up, 1)

            def up_part(i, g, par):
                wait(pe, rows_down, g + 1)
                wait(pe, up_down, g)
                for j in range(J):
                    m = nc.tensor.matmul(up_ps[:, j, :], rows_t[:, par, j * P:(j + 1) * P], t["up"][:, :], start=True, stop=True)
                m.then_inc(up_up, 1)

            def mix_part(i, g, par):
                wait(pe, mixed_in, g + 1)
                for h, down, up_sem in ((0, mix0_down, mix0_up), (1, mix1_down, mix1_up)):
                    wait(pe, down, g)
                    for j in range(J):
                        m = nc.tensor.transpose(mix_ps[h][:, j * P:(j + 1) * P], mixed[:, par, j, h * P:(h + 1) * P], k["ident"][:, :])
                    m.then_inc(up_sem, 1)

            def wave_part(i, g, par):
                wait(pe, waved, g + 1)
                wait(pe, wave_down, g)
                nc.tensor.transpose(wave_ps[:, 0:P], wave[:, par, :], k["ident"][:, :]).then_inc(wave_up, 1)

            def rows_part(i, g, par):
                wait(pe, came[par], 16 * J * (i + 1))
                wait(pe, rows_down, g)
                for j in range(J):
                    m = nc.tensor.transpose(turn_ps[:, j * P:(j + 1) * P], rows[:, par, j, :], k["ident"][:, :])
                m.then_inc(rows_up, 1)

            paced(pe, (hid1_part, 1), (gate_part, 0), (out_part, -3), (hid0_part, 2), (up_part, 0), (mix_part, -2),
                  (wave_part, 3), (rows_part, 1))


def load_weights(nc, k, ctx, w):
    shapes = {"W1": [P, P], "R1": [P, P], "W2": [P, P], "R2": [P, P], "W3Wh": [P, P], "lin_t": [P, P],
              "atom": [P, P], "bond": [P, P],
              "gin1": [P, LAYERS, 2 * P], "gin2": [P, LAYERS, 2, P], "final": [P, P],
              "eps_row": [P, LAYERS], "b1": [P, LAYERS, 2], "g1": [P, LAYERS, 2], "be1": [P, LAYERS, 2],
              "b2": [P, LAYERS], "gn": [P, LAYERS], "bet": [P, LAYERS]}
    m = {n: ctx.enter_context(nc.sbuf_tensor("w_" + n, s, F32)) for n, s in shapes.items()}
    rows = {"bh": "L1_gnn_bh", "lin_b": "L2_gnn_b", "atom_b": "L3_gnn_b_atom", "bond_b": "L3_gnn_b_bond", "final_b": "L3_gnn_b_out"}
    for n in rows:
        m[n] = ctx.enter_context(nc.sbuf_tensor("w_" + n, [3, W], BF16))

    def row(a):
        return a.rearrange("(a n) -> a n", a=1)

    loads = [(m["W1"][:, :], w["L1_gnn_W1"]), (m["R1"][:, :], w["L1_gnn_R1"]), (m["W2"][:, :], w["L1_gnn_W2"]),
             (m["R2"][:, :], w["L1_gnn_R2"]), (m["atom"][:, :], w["L3_gnn_W_atom"]), (m["bond"][:, :], w["L3_gnn_W_bond"]),
             (m["final"][:, :], w["L3_gnn_W_out"]),
             (m["eps_row"][:, :], row(w["L3_gnn_eps"]).to_broadcast([P, LAYERS]))]
    for i in range(LAYERS):
        loads.append((m["gin1"][:, i, :], w["L3_gnn_W1"][i]))
        for h in range(2):
            loads.append((m["gin2"][:, i, h, :], w["L3_gnn_W2"][i, h * P:(h + 1) * P, :]))
            for n in ("b1", "g1", "be1"):
                loads.append((m[n][:, i, h:h + 1], w["L3_gnn_" + n][i, h * P:(h + 1) * P].rearrange("(p a) -> p a", a=1)))
        for n in ("b2", "gn", "bet"):
            loads.append((m[n][:, i:i + 1], w["L3_gnn_" + n][i].rearrange("(p a) -> p a", a=1)))
    with nc.cleanup_on_exit(), ExitStack() as inner:
        ph = Phase(nc, inner)
        w3, wh, lin, w3t = (ph.sb(n, [P, P]) for n in ("w3", "wh", "lin", "w3t"))
        turn_ps, lin_ps, product_ps = (ph.ps(n, [P, 512]) for n in ("turn", "lin", "product"))
        loaded, turned, copied, multiplied = (ph.sem(n) for n in ("loaded", "turned", "copied", "multiplied"))
        row_sp, row_v = split_rows(nc, ph, [(w[a], m[n]) for n, a in rows.items()])
        loads += [(w3[:, :], w["L1_gnn_W3"]), (wh[:, :], w["L1_gnn_Wh"]), (lin[:, :], w["L2_gnn_W"])]
        block = inner.enter_context(nc.Block())

        @block.sync
        def _(sp):
            for to, of in loads:
                sp.dma_start(to, of).then_inc(loaded, 16)
            row_sp(sp)

        @block.tensor
        def _(pe):
            pe.wait_ge(loaded, 16 * len(loads))
            nc.tensor.transpose(turn_ps[:, 0:P], w3[:, :], k["ident"][:, :]).then_inc(turned, 1)
            nc.tensor.transpose(lin_ps[:, 0:P], lin[:, :], k["ident"][:, :]).then_inc(turned, 1)
            pe.wait_ge(copied, 1)
            nc.tensor.matmul(product_ps[:, 0:P], w3t[:, :], wh[:, :], start=True, stop=True).then_inc(multiplied, 1)

        @block.vector
        def _(v):
            row_v(v)
            v.wait_ge(loaded, 16 * len(loads))
            nc.vector.tensor_scalar(m["eps_row"][:, :], m["eps_row"][:, :], 1.0, None, ALU.add)
            v.wait_ge(turned, 1)
            nc.vector.tensor_copy(w3t[:, :], turn_ps[:, 0:P]).then_inc(copied, 1)
            v.wait_ge(turned, 2)
            nc.vector.tensor_copy(m["lin_t"][:, :], lin_ps[:, 0:P])
            v.wait_ge(multiplied, 1)
            nc.vector.tensor_copy(m["W3Wh"][:, :], product_ps[:, 0:P])
    return m


def bond_rows(nc, k, edge_attr, m, bonds):
    with nc.cleanup_on_exit(), ExitStack() as ctx:
        ph = Phase(nc, ctx)
        sb, ps, sem = ph.sb, ph.ps, ph.sem
        rows = sb("rows", [P, 2, J, P])
        idx = sb("idx", [P, 2, J], I32)
        rows_t = sb("rows_t", [P, 2, W])
        out = sb("out", [P, 2, W])
        turn_ps = [ps("turn0", [P, 512]), ps("turn1", [P, 512])]
        out_ps = [ps("out0", [P, 512]), ps("out1", [P, 512])]
        came = [sem("came0"), sem("came1")]
        stored = [sem("stored0"), sem("stored1")]
        staged, turned, rows_down, made, out_down, passed, passed_sp = (sem(n) for n in (
            "staged", "turned", "rows_down", "made", "out_down", "passed", "passed_sp"))
        block = ctx.enter_context(nc.Block())

        @block.gpsimd
        def _(pool):
            def body(i):
                for par in range(2):
                    g = 2 * i + par
                    wait(pool, staged, g + 1, passed)
                    wait(pool, turned, g - 1, passed)
                    for j in range(J):
                        nc.gpsimd.indirect_dma_start(rows[:, par, j, :], None, edge_attr,
                                                     bass.IndirectOffsetOnAxis(ap=idx[:, par, j:j + 1], axis=0)).then_inc(came[par], 16)
            loop(pool, body)

        @block.sync
        def _(sp):
            def body(i):
                for par in range(2):
                    g = 2 * i + par
                    wait(sp, out_down, g + 1, passed_sp)
                    sp.dma_start(block_of(bonds, g), out[:, par, :]).then_inc(stored[par], 16)
            loop(sp, body)
            for par in range(2):
                sp.wait_ge(stored[par], 16 * (G // 2))

        @block.scalar
        def _(act):
            def body(i):
                for par in range(2):
                    g = 2 * i + par
                    wait(act, turned, g + 1)
                    wait(act, made, g - 1)
                    nc.scalar.copy(rows_t[:, par, :], turn_ps[par][:, :]).then_inc(rows_down, 1)
            loop(act, body)

        @block.vector
        def _(v):
            def body(i):
                for par in range(2):
                    g = 2 * i + par
                    wait(v, came[par], 16 * J * i)
                    nc.vector.tensor_copy(idx[:, par, :], k["edge_r"][:, ds(g * J, J)]).then_inc(staged, 1)
                    wait(v, made, g)
                    if par or not isinstance(i, int) or i:
                        before = 1 - par
                        wait(v, stored[before], 16 * (i if par else i - 1))
                        nc.vector.tensor_copy(out[:, before, :], out_ps[before][:, :]).then_inc(out_down, 1)
            loop(v, body)
            v.wait_ge(made, G)
            v.wait_ge(stored[1], 16 * (G // 2 - 1))
            nc.vector.tensor_copy(out[:, 1, :], out_ps[1][:, :]).then_inc(out_down, 1)

        @block.tensor
        def _(pe):
            def body(i):
                for par in range(2):
                    g = 2 * i + par
                    wait(pe, came[par], 16 * J * (i + 1))
                    wait(pe, rows_down, g - 1)
                    for j in range(J):
                        t = nc.tensor.transpose(turn_ps[par][:, j * P:(j + 1) * P], rows[:, par, j, :], k["ident"][:, :])
                    t.then_inc(turned, 1)
                    wait(pe, rows_down, g + 1)
                    wait(pe, out_down, g - 1)
                    nc.tensor.matmul(out_ps[par][:, :], k["one_rows"][:, :], m["bond_b"][:, :], start=True, stop=False)
                    for j in range(J):
                        t = nc.tensor.matmul(out_ps[par][:, j * P:(j + 1) * P], rows_t[:, par, j * P:(j + 1) * P], m["bond"][:, :],
                                             start=False, stop=j == J - 1)
                    t.then_inc(made, 1)
            loop(pe, body)


def node_rows(nc, k, x, sums, out1, out2, *, gcn=False, first=(), bias1=None, residual=None, norm=True,
              weighted=False, second=None, bias2=None, relu2=False, outside=False):
    width = P + 1 if weighted else P
    with nc.cleanup_on_exit(), ExitStack() as ctx:
        ph = Phase(nc, ctx)
        sb, ps, sem = ph.sb, ph.ps, ph.sem
        x_in = sb("x_in", [P, 2, J, P])
        s_in = sb("s_in", [P, 2, J, width])
        r_in = sb("r_in", [P, 2, W]) if residual is not None else None
        u = sb("u", [P, 2, W])
        u_t = sb("u_t", [P, 2, W])
        x_t = sb("x_t", [P, 2, W])
        y = sb("y", [P, 2, W])
        o1 = sb("o1", [P, 2, J, P])
        o1_t = sb("o1_t", [P, 2, W])
        o2 = sb("o2", [P, 2, J, P])
        parts = sb("parts", [P, 2, J, 6])
        moments = sb("moments", [P, 2, J, 2])
        spread = sb("spread", [P, 2, J])
        inverse = sb("inverse", [P, 2, J])
        low = sb("low", [P, 2, J])
        share = sb("share", [P, 2, J])
        minus_half = sb("minus_half", [P, J])
        tu_ps, tx_ps, t2_ps = (ps(n, [P, 512]) for n in ("tu", "tx", "t2"))
        m1_ps = [ps("m10", [P, 512]), ps("m11", [P, 512])]
        m2_ps = [ps("m20", [P, 512]), ps("m21", [P, 512])]
        came, stored1, stored2 = ([sem(n + "0"), sem(n + "1")] for n in ("came", "stored1", "stored2"))
        (u_step, u_made, y_made, halved, measured, joined, spread_in, raised, o1_made, o2_made, tu, tx, u_down, x_down,
         m1, t2, o1_down, m2, lows, passed, passed_sp, passed_v) = (sem(n) for n in (
            "u_step", "u_made", "y_made", "halved", "measured", "joined", "spread_in", "raised", "o1_made", "o2_made",
            "tu", "tx", "u_down", "x_down", "m1", "t2", "o1_down", "m2", "lows", "passed", "passed_sp", "passed_v"))
        loads = 2 + (residual is not None)
        used = y_made if (residual is not None or not gcn) else u_made
        block = ctx.enter_context(nc.Block())

        @block.sync
        def _(sp):
            def front(i, g, par):
                wait(sp, used, g - 1, passed_sp)
                if len(first) == 2:
                    wait(sp, tx, g - 1, passed_sp)
                flat = x_in[:, par, :, :].rearrange("p j d -> p (j d)")
                if outside and isinstance(g, int) and g == G - 1:
                    sp.dma_start(flat[0:LASTP, :], x_rows(x, last=True)).then_inc(came[par], 16)
                else:
                    source = block_of(x_rows(x), g) if outside else rows_of(x, g)
                    sp.dma_start(flat, source).then_inc(came[par], 16)
                sp.dma_start(s_in[:, par, :, :].rearrange("p j d -> p (j d)"), rows_of(sums, g)).then_inc(came[par], 16)
                if residual is not None:
                    sp.dma_start(r_in[:, par, :], rows_of(residual, g)).then_inc(came[par], 16)

            def back(i, g, par):
                wait(sp, o1_made, g + 1, passed_sp)
                sp.dma_start(rows_of(out1, g), o1[:, par, :, :].rearrange("p j d -> p (j d)")).then_inc(stored1[par], 16)
                wait(sp, o2_made, g + 1, passed_sp)
                sp.dma_start(rows_of(out2, g), o2[:, par, :, :].rearrange("p j d -> p (j d)")).then_inc(stored2[par], 16)
            paced(sp, (front, 2), (back, -2 if norm else 0))
            for par in range(2):
                sp.wait_ge(stored1[par], 16 * (G // 2))
                sp.wait_ge(stored2[par], 16 * (G // 2))

        @block.gpsimd
        def _(pool):
            nc.gpsimd.memset(minus_half[:, :], -0.5).then_inc(halved, 1)
            pool.wait_ge(halved, 1)
            if norm:
                def body(i):
                    for par in range(2):
                        wait(pool, spread_in, 2 * i + par + 1, passed)
                        nc.gpsimd.tensor_tensor(inverse[:, par, :], spread[:, par, :], minus_half[:, :], ALU.pow).then_inc(raised, 1)
                loop(pool, body)

        @block.vector
        def _(v):
            def front(i, g, par):
                wait(v, came[par], 16 * loads * (i + 1))
                dinv = k["dinv"][:, ds(g * J, J)].unsqueeze(2).to_broadcast([P, J, P])
                u3 = u[:, par, :].rearrange("p (j d) -> p j d", j=J)
                wait(v, tu, g - 1)
                nc.vector.tensor_tensor(u3, x_in[:, par, :, :], dinv, ALU.mult).then_inc(u_step, 1)
                wait(v, u_step, 2 * g + 1)
                nc.vector.tensor_tensor(u3, u3, s_in[:, par, :, :], ALU.add).then_inc(u_step, 1)
                wait(v, u_step, 2 * g + 2)
                nc.vector.tensor_tensor(u3, u3, dinv, ALU.mult).then_inc(u_made, 1)

            def measure(i, g, par):
                wait(v, o1_made, g - 1)
                if gcn:
                    wait(v, m1, g + 1)
                    nc.vector.tensor_tensor(y[:, par, :], m1_ps[par][:, :], r_in[:, par, :], ALU.add).then_inc(y_made, 1)
                elif weighted:
                    wait(v, came[par], 16 * loads * (i + 1))
                    nc.vector.tensor_scalar(low[:, par, :], s_in[:, par, :, P], 0.5, None, ALU.is_lt).then_inc(lows, 1)
                    wait(v, lows, 3 * g + 1)
                    nc.vector.tensor_tensor(low[:, par, :], low[:, par, :], s_in[:, par, :, P], ALU.add).then_inc(lows, 1)
                    wait(v, lows, 3 * g + 2)
                    nc.vector.reciprocal(share[:, par, :], low[:, par, :]).then_inc(lows, 1)
                    wait(v, lows, 3 * g + 3)
                    for j in range(J):
                        last = nc.vector.scalar_tensor_tensor(y[:, par, j * P:(j + 1) * P], s_in[:, par, j, 0:P], share[:, par, j:j + 1],
                                                              x_in[:, par, j, :], ALU.mult, ALU.add)
                    last.then_inc(y_made, 1)
                else:
                    wait(v, came[par], 16 * loads * (i + 1))
                    nc.vector.tensor_tensor(y[:, par, :], x_in[:, par, :, :].rearrange("p j d -> p (j d)"),
                                            s_in[:, par, :, :].rearrange("p j d -> p (j d)"), ALU.add).then_inc(y_made, 1)
                wait(v, y_made, g + 1)
                for j in range(J):
                    last = nc.vector.bn_stats(parts[:, par, j, :], y[:, par, j * P:(j + 1) * P])
                last.then_inc(measured, 1)
                wait(v, measured, g + 1, passed_v)
                for j in range(J):
                    last = nc.vector.bn_aggr(moments[:, par, j, :], parts[:, par, j, :])
                last.then_inc(joined, 1)
                wait(v, joined, g + 1)
                nc.vector.tensor_scalar(spread[:, par, :], moments[:, par, :, 1], LN_EPS, None, ALU.add).then_inc(spread_in, 1)

            def apply(i, g, par):
                wait(v, stored1[par], 16 * i)
                if second is None:
                    wait(v, o2_made, g - 1)
                else:
                    wait(v, t2, g - 1)
                wait(v, raised, g + 1)
                for j in range(J):
                    last = nc.vector.tensor_scalar(o1[:, par, j, :], y[:, par, j * P:(j + 1) * P], moments[:, par, j, 0:1],
                                                   inverse[:, par, j:j + 1], ALU.subtract, ALU.mult)
                last.then_inc(o1_made, 1)

            stages = [(measure, 0), (apply, -1)] if norm else []
            paced(v, *([(front, 1)] if gcn else []), *stages)

        @block.scalar
        def _(act):
            def turn_down(i, g, par):
                wait(act, tu, g + 1)
                wait(act, m1, g - 1)
                nc.scalar.copy(u_t[:, par, :], tu_ps[:, :]).then_inc(u_down, 1)
                if len(first) == 2:
                    wait(act, tx, g + 1)
                    nc.scalar.copy(x_t[:, par, :], tx_ps[:, :]).then_inc(x_down, 1)

            def relu_out(i, g, par):
                wait(act, m1, g + 1)
                wait(act, stored1[par], 16 * i)
                wait(act, o2_made, g - 1)
                nc.scalar.activation(o1[:, par, :, :].rearrange("p j d -> p (j d)"), m1_ps[par][:, :], ACT.Relu).then_inc(o1_made, 1)

            def scale_out(i, g, par):
                wait(act, stored2[par], 16 * i)
                wait(act, o1_made, g + 1)
                for j in range(J):
                    last = nc.scalar.activation(o2[:, par, j, :], o1[:, par, j, :], ACT.Copy, scale=k["dinv"][:, ds(g * J + j)])
                last.then_inc(o2_made, 1)

            def out_down(i, g, par):
                wait(act, t2, g + 1)
                wait(act, m2, g - 1)
                nc.scalar.copy(o1_t[:, par, :], t2_ps[:, :]).then_inc(o1_down, 1)

            def second_out(i, g, par):
                wait(act, stored2[par], 16 * i)
                wait(act, m2, g + 1)
                nc.scalar.activation(o2[:, par, :, :].rearrange("p j d -> p (j d)"), m2_ps[par][:, :],
                                     ACT.Relu if relu2 else ACT.Copy).then_inc(o2_made, 1)

            stages = [(turn_down, 1)] if gcn else []
            if not norm:
                stages += [(relu_out, 0), (scale_out, 0)]
            elif second is None:
                stages += [(scale_out, -1)]
            else:
                stages += [(out_down, -1), (second_out, -2)]
            paced(act, *stages)

        @block.tensor
        def _(pe):
            def turn(i, g, par):
                wait(pe, u_made, g + 1)
                wait(pe, u_down, g)
                for j in range(J):
                    t = nc.tensor.transpose(tu_ps[:, j * P:(j + 1) * P], u[:, par, j * P:(j + 1) * P], k["ident"][:, :])
                t.then_inc(tu, 1)
                if len(first) == 2:
                    wait(pe, x_down, g)
                    for j in range(J):
                        t = nc.tensor.transpose(tx_ps[:, j * P:(j + 1) * P], x_in[:, par, j, :], k["ident"][:, :])
                    t.then_inc(tx, 1)

            def product(i, g, par):
                wait(pe, u_down, g + 1)
                if len(first) == 2:
                    wait(pe, x_down, g + 1)
                wait(pe, y_made if norm else o1_made, g - 1)
                sources = (u_t, x_t)[0:len(first)]
                if bias1 is not None:
                    nc.tensor.matmul(m1_ps[par][:, :], k["one_rows"][:, :], bias1[:, :], start=True, stop=False)
                for j in range(J):
                    for n, (a, b) in enumerate(zip(sources, first)):
                        t = nc.tensor.matmul(m1_ps[par][:, j * P:(j + 1) * P], a[:, par, j * P:(j + 1) * P], b[:, :],
                                             start=n == 0 and bias1 is None,
                                             stop=n == len(first) - 1 and (bias1 is None or j == J - 1))
                t.then_inc(m1, 1)

            def turn_out(i, g, par):
                wait(pe, o1_made, g + 1)
                wait(pe, o1_down, g)
                for j in range(J):
                    t = nc.tensor.transpose(t2_ps[:, j * P:(j + 1) * P], o1[:, par, j, :], k["ident"][:, :])
                t.then_inc(t2, 1)

            def second_product(i, g, par):
                wait(pe, o1_down, g + 1)
                wait(pe, o2_made, g - 1)
                nc.tensor.matmul(m2_ps[par][:, :], k["one_rows"][:, :], bias2[:, :], start=True, stop=False)
                for j in range(J):
                    t = nc.tensor.matmul(m2_ps[par][:, j * P:(j + 1) * P], o1_t[:, par, j * P:(j + 1) * P], second[:, :],
                                         start=False, stop=j == J - 1)
                t.then_inc(m2, 1)

            stages = [(product, 0), (turn, 1)] if gcn else []
            if second is not None:
                stages += [(second_product, -2), (turn_out, -1)]
            if stages:
                paced(pe, *stages)


def batch_norm(nc, ph, stats, gain, shift, bias, halves):
    sb, sem = ph.sb, ph.sem
    moments, spread, power, root = sb("moments", [P, halves, 2]), sb("spread", [P, halves]), sb("power", [P, halves]), sb("root", [P, halves])
    affine, mean = sb("affine", [P, halves, 2]), sb("mean", [P, halves])
    stepped, spread_in, raised, done = sem("stepped"), sem("spread_in"), sem("raised"), sem("affine_in")

    def pool_part(pool):
        nc.gpsimd.memset(power[:, :], -0.5).then_inc(stepped, 1)
        pool.wait_ge(spread_in, 1)
        pool.wait_ge(stepped, 1)
        nc.gpsimd.tensor_tensor(root[:, :], spread[:, :], power[:, :], ALU.pow).then_inc(raised, 1)

    def v_part(v):
        n = sem("n")
        count = [0]

        def step(ins):
            count[0] += 1
            ins.then_inc(n, 1)
            v.wait_ge(n, count[0])

        for h in range(halves):
            step(nc.vector.bn_aggr(moments[:, h, :], stats[:, h, :]))
        nc.vector.tensor_scalar(spread[:, :], moments[:, :, 1], BN_EPS, None, ALU.add).then_inc(spread_in, 1)
        step(nc.vector.tensor_tensor(mean[:, :], moments[:, :, 0], bias, ALU.add))
        step(nc.vector.tensor_tensor(mean[:, :], bias, mean[:, :], ALU.subtract))
        v.wait_ge(raised, 1)
        step(nc.vector.tensor_tensor(affine[:, :, 0], root[:, :], gain, ALU.mult))
        step(nc.vector.tensor_tensor(mean[:, :], mean[:, :], affine[:, :, 0], ALU.mult))
        nc.vector.tensor_tensor(affine[:, :, 1], mean[:, :], shift, ALU.add).then_inc(done, 1)
    return affine, done, pool_part, v_part


def group_stats(nc, stats, h, g, product, last):
    if last:
        product = product.rearrange("p (j n) -> p j n", j=J)[:, :, 0:LASTP]
    return nc.vector.bn_stats(stats[:, h, ds(g * 6, 6)], product)


def gin_in(nc, k, m, layer, h_rows, sums, z_cols, stats):
    with nc.cleanup_on_exit(), ExitStack() as ctx:
        ph = Phase(nc, ctx)
        sb, ps, sem = ph.sb, ph.ps, ph.sem
        h_in, s_in, z, z_t = (sb(n, [P, 2, W]) for n in ("h_in", "s_in", "z", "z_t"))
        turn_ps = [ps("turn0", [P, 512]), ps("turn1", [P, 512])]
        wide_ps = [[ps(f"wide{n}{h}", [P, 512]) for h in range(2)] for n in range(2)]
        came, stored = ([sem(n + "0"), sem(n + "1")] for n in ("came", "stored"))
        z_made, turned, z_down, wide, counted, passed_sp = (sem(n) for n in (
            "z_made", "turned", "z_down", "wide", "counted", "passed_sp"))
        block = ctx.enter_context(nc.Block())

        @block.sync
        def _(sp):
            def front(i, g, par):
                wait(sp, z_made, g - 1, passed_sp)
                sp.dma_start(h_in[:, par, :], rows_of(h_rows, g)).then_inc(came[par], 16)
                sp.dma_start(s_in[:, par, :], rows_of(sums, g)).then_inc(came[par], 16)

            def back(i, g, par):
                wait(sp, z_down, g + 1, passed_sp)
                sp.dma_start(block_of(z_cols, g), z_t[:, par, :]).then_inc(stored[par], 16)
            paced(sp, (front, 2), (back, -1))
            for par in range(2):
                sp.wait_ge(stored[par], 16 * (G // 2))

        @block.vector
        def _(v):
            def front(i, g, par):
                wait(v, came[par], 32 * (i + 1))
                wait(v, turned, g - 1)
                nc.vector.scalar_tensor_tensor(z[:, par, :], h_in[:, par, :], m["eps_row"][:, layer:layer + 1], s_in[:, par, :],
                                               ALU.mult, ALU.add).then_inc(z_made, 1)

            def back(i, g, par):
                last = isinstance(g, int) and g == G - 1
                for h in range(2):
                    wait(v, wide, 2 * g + h + 1)
                    group_stats(nc, stats, h, g, wide_ps[par][h][:, :], last).then_inc(counted, 1)
            paced(v, (front, 1), (back, 0))

        @block.scalar
        def _(act):
            def body(i):
                for par in range(2):
                    g = 2 * i + par
                    wait(act, turned, g + 1)
                    wait(act, wide, 2 * (g - 1))
                    wait(act, stored[par], 16 * i)
                    nc.scalar.copy(z_t[:, par, :], turn_ps[par][:, :]).then_inc(z_down, 1)
            loop(act, body)

        @block.tensor
        def _(pe):
            def front(i, g, par):
                wait(pe, z_made, g + 1)
                wait(pe, z_down, g - 1)
                for j in range(J):
                    t = nc.tensor.transpose(turn_ps[par][:, j * P:(j + 1) * P], z[:, par, j * P:(j + 1) * P], k["ident"][:, :])
                t.then_inc(turned, 1)

            def back(i, g, par):
                wait(pe, z_down, g + 1)
                wait(pe, counted, 2 * (g - 1))
                for h in range(2):
                    nc.tensor.matmul(wide_ps[par][h][:, :], m["gin1"][:, layer, h * P:(h + 1) * P], z_t[:, par, :],
                                     start=True, stop=True).then_inc(wide, 1)
            paced(pe, (back, 0), (front, 1))


def gin_middle(nc, k, m, layer, z_cols, stats, y_cols, stats2):
    with nc.cleanup_on_exit(), ExitStack() as ctx:
        ph = Phase(nc, ctx)
        sb, ps, sem = ph.sb, ph.ps, ph.sem
        z_t, y_t = (sb(n, [P, 2, W]) for n in ("z_t", "y_t"))
        wide_sb = sb("wide_sb", [P, 2, 2, W])
        wide_ps = [[ps(f"wide{n}{h}", [P, 512]) for h in range(2)] for n in range(2)]
        y_ps = [ps("y0", [P, 512]), ps("y1", [P, 512])]
        came, stored = ([sem(n + "0"), sem(n + "1")] for n in ("came", "stored"))
        wide, wide_down, product, y_down, counted, passed_sp = (sem(n) for n in (
            "wide", "wide_down", "product", "y_down", "counted", "passed_sp"))
        affine, affine_in, pool_part, v_part = batch_norm(nc, ph, stats, m["g1"][:, layer, :], m["be1"][:, layer, :],
                                                          m["b1"][:, layer, :], 2)
        block = ctx.enter_context(nc.Block())

        @block.gpsimd
        def _(pool):
            pool_part(pool)

        @block.sync
        def _(sp):
            def front(i, g, par):
                wait(sp, wide, 2 * (g - 1), passed_sp)
                sp.dma_start(z_t[:, par, :], block_of(z_cols, g)).then_inc(came[par], 16)

            def back(i, g, par):
                wait(sp, y_down, g + 1, passed_sp)
                sp.dma_start(block_of(y_cols, g), y_t[:, par, :]).then_inc(stored[par], 16)
            paced(sp, (front, 2), (back, -1))
            for par in range(2):
                sp.wait_ge(stored[par], 16 * (G // 2))

        @block.scalar
        def _(act):
            act.wait_ge(affine_in, 1)

            def body(i):
                for par in range(2):
                    g = 2 * i + par
                    wait(act, product, g - 1)
                    for h in range(2):
                        wait(act, wide, 2 * g + h + 1)
                        nc.scalar.activation(wide_sb[:, par, h, :], wide_ps[par][h][:, :], ACT.Relu, bias=affine[:, h, 1:2],
                                             scale=affine[:, h, 0:1]).then_inc(wide_down, 1)
            loop(act, body)

        @block.vector
        def _(v):
            v_part(v)

            def body(i, last=False):
                for par in range(2):
                    g = 2 * i + par
                    wait(v, product, g + 1)
                    group_stats(nc, stats2, 0, g, y_ps[par][:, :], isinstance(g, int) and g == G - 1).then_inc(counted, 1)
                    wait(v, stored[par], 16 * i)
                    nc.vector.tensor_copy(y_t[:, par, :], y_ps[par][:, :]).then_inc(y_down, 1)
            loop(v, body)

        @block.tensor
        def _(pe):
            def front(i, g, par):
                wait(pe, came[par], 16 * (i + 1))
                wait(pe, wide_down, 2 * (g - 1))
                for h in range(2):
                    nc.tensor.matmul(wide_ps[par][h][:, :], m["gin1"][:, layer, h * P:(h + 1) * P], z_t[:, par, :],
                                     start=True, stop=True).then_inc(wide, 1)

            def back(i, g, par):
                wait(pe, wide_down, 2 * g + 2)
                wait(pe, y_down, g - 1)
                for h in range(2):
                    t = nc.tensor.matmul(y_ps[par][:, :], m["gin2"][:, layer, h, :], wide_sb[:, par, h, :], start=h == 0, stop=h == 1)
                t.then_inc(product, 1)
            paced(pe, (front, 1), (back, 0))


def gin_out(nc, k, m, layer, y_cols, stats2, h_rows):
    with nc.cleanup_on_exit(), ExitStack() as ctx:
        ph = Phase(nc, ctx)
        sb, ps, sem = ph.sb, ph.ps, ph.sem
        y_t, h_t, h_sb = (sb(n, [P, 2, W]) for n in ("y_t", "h_t", "h_sb"))
        turn_ps = [ps("turn0", [P, 512]), ps("turn1", [P, 512])]
        came, stored = ([sem(n + "0"), sem(n + "1")] for n in ("came", "stored"))
        normed, turned, h_down, passed_sp = (sem(n) for n in ("normed", "turned", "h_down", "passed_sp"))
        affine, affine_in, pool_part, v_part = batch_norm(nc, ph, stats2, m["gn"][:, layer:layer + 1],
                                                          m["bet"][:, layer:layer + 1], m["b2"][:, layer:layer + 1], 1)
        block = ctx.enter_context(nc.Block())

        @block.gpsimd
        def _(pool):
            pool_part(pool)

        @block.sync
        def _(sp):
            def front(i, g, par):
                wait(sp, normed, g - 1, passed_sp)
                sp.dma_start(y_t[:, par, :], block_of(y_cols, g)).then_inc(came[par], 16)

            def back(i, g, par):
                wait(sp, h_down, g + 1, passed_sp)
                sp.dma_start(rows_of(h_rows, g), h_sb[:, par, :]).then_inc(stored[par], 16)
            paced(sp, (front, 2), (back, -1))
            for par in range(2):
                sp.wait_ge(stored[par], 16 * (G // 2))

        @block.scalar
        def _(act):
            act.wait_ge(affine_in, 1)

            def body(i):
                for par in range(2):
                    g = 2 * i + par
                    wait(act, came[par], 16 * (i + 1))
                    wait(act, turned, g - 1)
                    nc.scalar.activation(h_t[:, par, :], y_t[:, par, :], ACT.Relu, bias=affine[:, 0, 1:2],
                                         scale=affine[:, 0, 0:1]).then_inc(normed, 1)
            loop(act, body)

        @block.vector
        def _(v):
            v_part(v)

            def body(i):
                for par in range(2):
                    g = 2 * i + par
                    wait(v, turned, g + 1)
                    wait(v, stored[par], 16 * i)
                    nc.vector.tensor_copy(h_sb[:, par, :], turn_ps[par][:, :]).then_inc(h_down, 1)
            loop(v, body)

        @block.tensor
        def _(pe):
            def body(i):
                for par in range(2):
                    g = 2 * i + par
                    wait(pe, normed, g + 1)
                    wait(pe, h_down, g - 1)
                    for j in range(J):
                        t = nc.tensor.transpose(turn_ps[par][:, j * P:(j + 1) * P], h_t[:, par, j * P:(j + 1) * P], k["ident"][:, :])
                    t.then_inc(turned, 1)
            loop(pe, body)


def final_rows(nc, k, m, y_cols, stats2, x, out):
    layer = LAYERS - 1
    with nc.cleanup_on_exit(), ExitStack() as ctx:
        ph = Phase(nc, ctx)
        sb, ps, sem = ph.sb, ph.ps, ph.sem
        y_t, h_t, x_in, y, o = (sb(n, [P, 2, W]) for n in ("y_t", "h_t", "x_in", "y", "o"))
        parts, aggregate = sb("parts", [P, 2, J, 6]), sb("aggregate", [P, 2, J, 2])
        spread_r, inverse, minus_half = sb("spread_r", [P, 2, J]), sb("inverse", [P, 2, J]), sb("minus_half", [P, J])
        out_ps = [ps("out0", [P, 512]), ps("out1", [P, 512])]
        came, stored = ([sem(n + "0"), sem(n + "1")] for n in ("came", "stored"))
        normed, product, summed, measured, joined, rows_spread, halved, raised_r, o_made, passed_sp, passed, passed_v = (sem(n) for n in (
            "normed", "product", "summed", "measured", "joined", "rows_spread", "halved", "raised_r", "o_made", "passed_sp", "passed", "passed_v"))
        affine, affine_in, pool_part, v_part = batch_norm(nc, ph, stats2, m["gn"][:, layer:layer + 1],
                                                          m["bet"][:, layer:layer + 1], m["b2"][:, layer:layer + 1], 1)
        block = ctx.enter_context(nc.Block())

        @block.gpsimd
        def _(pool):
            pool_part(pool)
            nc.gpsimd.memset(minus_half[:, :], -0.5).then_inc(halved, 1)
            pool.wait_ge(halved, 1)

            def body(i):
                for par in range(2):
                    wait(pool, rows_spread, 2 * i + par + 1, passed)
                    nc.gpsimd.tensor_tensor(inverse[:, par, :], spread_r[:, par, :], minus_half[:, :], ALU.pow).then_inc(raised_r, 1)
            loop(pool, body)

        @block.sync
        def _(sp):
            def front(i, g, par):
                wait(sp, normed, g - 1, passed_sp)
                sp.dma_start(y_t[:, par, :], block_of(y_cols, g)).then_inc(came[par], 16)
                wait(sp, summed, g - 1, passed_sp)
                sp.dma_start(x_in[:, par, :], rows_of(x, g)).then_inc(came[par], 16)

            def back(i, g, par):
                wait(sp, o_made, g + 1, passed_sp)
                if isinstance(g, int) and g == G - 1:
                    sp.dma_start(x_rows(out, last=True), o[0:LASTP, par, :]).then_inc(stored[par], 16)
                else:
                    sp.dma_start(block_of(x_rows(out), g), o[:, par, :]).then_inc(stored[par], 16)
            paced(sp, (front, 2), (back, -2))
            for par in range(2):
                sp.wait_ge(stored[par], 16 * (G // 2))

        @block.scalar
        def _(act):
            act.wait_ge(affine_in, 1)

            def body(i):
                for par in range(2):
                    g = 2 * i + par
                    wait(act, came[par], 32 * (i + 1))
                    wait(act, product, g - 1)
                    nc.scalar.activation(h_t[:, par, :], y_t[:, par, :], ACT.Relu, bias=affine[:, 0, 1:2],
                                         scale=affine[:, 0, 0:1]).then_inc(normed, 1)
            loop(act, body)

        @block.tensor
        def _(pe):
            def body(i):
                for par in range(2):
                    g = 2 * i + par
                    wait(pe, normed, g + 1)
                    wait(pe, summed, g - 1)
                    nc.tensor.matmul(out_ps[par][:, :], k["one_rows"][:, :], m["final_b"][:, :], start=True, stop=False)
                    for j in range(J):
                        t = nc.tensor.matmul(out_ps[par][:, j * P:(j + 1) * P], h_t[:, par, j * P:(j + 1) * P], m["final"][:, :],
                                             start=False, stop=j == J - 1)
                    t.then_inc(product, 1)
            loop(pe, body)

        @block.vector
        def _(v):
            v_part(v)

            def measure(i, g, par):
                wait(v, product, g + 1)
                wait(v, o_made, g - 1)
                nc.vector.tensor_tensor(y[:, par, :], out_ps[par][:, :], x_in[:, par, :], ALU.add).then_inc(summed, 1)
                wait(v, summed, g + 1)
                for j in range(J):
                    last = nc.vector.bn_stats(parts[:, par, j, :], y[:, par, j * P:(j + 1) * P])
                last.then_inc(measured, 1)
                wait(v, measured, g + 1, passed_v)
                for j in range(J):
                    last = nc.vector.bn_aggr(aggregate[:, par, j, :], parts[:, par, j, :])
                last.then_inc(joined, 1)
                wait(v, joined, g + 1)
                nc.vector.tensor_scalar(spread_r[:, par, :], aggregate[:, par, :, 1], LN_EPS, None, ALU.add).then_inc(rows_spread, 1)

            def apply(i, g, par):
                wait(v, stored[par], 16 * i)
                wait(v, raised_r, g + 1)
                for j in range(J):
                    last = nc.vector.tensor_scalar(o[:, par, j * P:(j + 1) * P], y[:, par, j * P:(j + 1) * P],
                                                   aggregate[:, par, j, 0:1], inverse[:, par, j:j + 1], ALU.subtract, ALU.mult)
                last.then_inc(o_made, 1)
            paced(v, (measure, 0), (apply, -1))


INPUTS = ["x", "src", "dst", "edge_attr_128", "edge_attr_3", "edge_weight", "L0_gnn_W_up0", "L0_gnn_W_up1", "L0_gnn_mlp_w0",
          "L0_gnn_mlp_b0", "L0_gnn_mlp_w1", "L0_gnn_mlp_b1", "L0_gnn_mlp_w2", "L0_gnn_mlp_b2", "L0_gnn_W_out0",
          "L0_gnn_W_out1", "L1_gnn_W1", "L1_gnn_R1", "L1_gnn_W2", "L1_gnn_R2", "L1_gnn_W3", "L1_gnn_Wh", "L1_gnn_bh",
          "L2_gnn_W", "L2_gnn_b", "L3_gnn_W_atom", "L3_gnn_b_atom", "L3_gnn_W_bond", "L3_gnn_b_bond", "L3_gnn_eps",
          "L3_gnn_W1", "L3_gnn_b1", "L3_gnn_g1", "L3_gnn_be1", "L3_gnn_W2", "L3_gnn_b2", "L3_gnn_gn", "L3_gnn_bet",
          "L3_gnn_W_out", "L3_gnn_b_out"]


def program(nc, w, out):
    def scratch(name, shape):
        return nc.dram_tensor(name, shape, F32, kind="Internal").ap()

    x = w["x"]
    d = {"sorted_r": scratch("sorted_r", [NP, 8]), "sorted_s": scratch("sorted_s", [NP, 8]),
         "line_r": scratch("line_r", [NP + P]), "line_s": scratch("line_s", [NP + P]),
         "sum_r": scratch("sum_r", [NP, P]), "sum_s": scratch("sum_s", [NP, P + 1])}
    groups = [scratch(f"groups{n}", [G, P, W]) for n in range(3)]
    messages, bonds, z_cols = groups
    y_cols = messages
    x1, x2, x3, xa, xb, scaled, h = (scratch(n, [NP, P]) for n in ("x1", "x2", "x3", "xa", "xb", "scaled", "h"))
    with ExitStack() as ctx:
        k = fixed_tiles(nc, ctx)
        k["line"] = {"r": d["line_r"], "s": d["line_s"]}
        count_and_rank(nc, k, d, w["src"], w["dst"], w["edge_weight"], w["edge_attr_3"])
        order_tables(nc, k, d)
        with ExitStack() as inner:
            t = tensor_product_weights(nc, k, {n[len("L0_gnn_"):]: a for n, a in w.items() if n.startswith("L0")}, inner)
            edge_products(nc, k, x, t, messages)
        segment_sum(nc, k, "r", d["sum_r"], messages=messages)
        m = load_weights(nc, k, ctx, w)
        node_rows(nc, k, x, d["sum_r"], x1, scaled, outside=True)
        segment_sum(nc, k, "r", d["sum_r"], table=scaled)
        node_rows(nc, k, x1, d["sum_r"], xa, scaled, gcn=True, first=(m["W1"], m["R1"]), norm=False)
        segment_sum(nc, k, "r", d["sum_r"], table=scaled)
        node_rows(nc, k, xa, d["sum_r"], xb, scaled, gcn=True, first=(m["W2"], m["R2"]), norm=False)
        segment_sum(nc, k, "r", d["sum_r"], table=scaled)
        node_rows(nc, k, xb, d["sum_r"], x2, h, gcn=True, first=(m["W3Wh"],), bias1=m["bh"], residual=x1,
                  second=m["lin_t"], bias2=m["lin_b"], relu2=True)
        segment_sum(nc, k, "s", d["sum_s"], width=P + 1, table=h, weight=k["weight_s"])
        node_rows(nc, k, x2, d["sum_s"], x3, h, weighted=True, second=m["atom"], bias2=m["atom_b"])
        bond_rows(nc, k, w["edge_attr_128"], m, bonds)
        stats = ctx.enter_context(nc.sbuf_tensor("stats", [P, 2, G * 6], F32))
        stats2 = ctx.enter_context(nc.sbuf_tensor("stats2", [P, 1, G * 6], F32))
        for layer in range(LAYERS):
            segment_sum(nc, k, "r", d["sum_r"], table=h, added=bonds)
            gin_in(nc, k, m, layer, h, d["sum_r"], z_cols, stats)
            gin_middle(nc, k, m, layer, z_cols, stats, y_cols, stats2)
            if layer < LAYERS - 1:
                gin_out(nc, k, m, layer, y_cols, stats2, h)
        final_rows(nc, k, m, y_cols, stats2, x3, out)


def kernel(**inputs):
    import concourse.bacc as bacc
    from concourse.bass_utils import run_bass_kernel_spmd

    nc = bacc.Bacc("TRN2", target_bir_lowering=False, num_devices=1)
    arrays, handles = {}, {}
    for name in INPUTS:
        a = np.ascontiguousarray(inputs[name])
        arrays["in_" + name] = a
        handles[name] = nc.dram_tensor("in_" + name, a.shape, mybir.dt.from_np(a.dtype), kind="ExternalInput").ap()
    out = nc.dram_tensor("out_nodes", (N, P), F32, kind="ExternalOutput").ap()
    program(nc, handles, out)
    return run_bass_kernel_spmd(nc, [arrays], core_ids=[0]).results[0]["out_nodes"]
```

```python
from contextlib import ExitStack

import numpy as np

import concourse.bass as bass
from concourse import mybir

F32 = mybir.dt.float32
F16 = mybir.dt.float16
BF16 = mybir.dt.bfloat16
I32 = mybir.dt.int32
ALU = mybir.AluOpType
ACT = mybir.ActivationFunctionType

P = 128
N = 50000
J = 4
G = (N + P * J - 1) // (P * J)
T = G * J
NP = T * P
W = J * P
FULL = N // T
REST = N - FULL * T
LASTP = (N - (G - 1) * W) // J
PAD = NP - 1
ZERO = NP
RING = 4
MUL = 32
NB = 8
HID = 64
AVG = 16.0
LN_EPS = 1e-5
BN_EPS = 1e-5
LAYERS = 3


def ds(i, n=1):
    return slice(i, i + n) if isinstance(i, int) else bass.DynSlice(i, n)


def block_of(t, g):
    return t[g] if isinstance(g, int) else t[bass.DynSlice(g, 1)].rearrange("a p f -> (a p) f")


def rows_of(t, g):
    return block_of(t[0:NP].rearrange("(g p j) d -> g p (j d)", p=P, j=J), g)


def x_rows(t, last=False):
    if last:
        return t[(G - 1) * W:N, :].rearrange("(p j) d -> p (j d)", j=J)
    return t[0:(G - 1) * W, :].rearrange("(g p j) d -> g p (j d)", p=P, j=J)


def loop(eng, body):
    body(0)
    with eng.Fori(1, G // 2 - 1) as i:
        body(i)
    body(G // 2 - 1)


def shifted_pairs(eng, group):
    for q in range(3):
        group(0, q)
    with eng.Fori(1, G // 2 - 1) as i:
        group(i, 1)
        group(i, 2)
    group(G // 2 - 1, 1, last=True)


def paced(eng, *stages, ring=2):
    leads = [lead for _, lead in stages]
    low, high = min(leads), max(leads)
    begin = -((low - ring) // ring) * ring
    end = (G - 1 - high) // ring * ring

    def step(i, q):
        for part, lead in stages:
            g = ring * i + q + lead
            if not isinstance(g, int) or 0 <= g < G:
                part(i + (q + lead) // ring, g, (q + lead) % ring)

    for n in range(-high, begin):
        step(n // ring, n % ring)
    with eng.Fori(begin // ring, end // ring) as i:
        for q in range(ring):
            step(i, q)
    for n in range(end, G - low):
        step(n // ring, n % ring)


class Phase:

    def __init__(self, nc, ctx):
        self.nc, self.ctx = nc, ctx
        self.n = 0

    def sb(self, name, shape, dt=F32):
        return self.ctx.enter_context(self.nc.sbuf_tensor(f"{name}_{self.nc.next_id()}", shape, dt))

    def ps(self, name, shape, dt=F32):
        return self.ctx.enter_context(self.nc.psum_tensor(f"{name}_{self.nc.next_id()}", shape, dt))

    def sem(self, name):
        return self.nc.alloc_semaphore(name=f"{name}_{self.nc.next_id()}")


def wait(eng, sem, value, passed=None):
    if isinstance(value, int):
        if value > 0:
            eng.wait_ge(sem, value)
        return
    eng.wait_ge(sem, value)
    if passed is not None:
        eng.sem_inc(passed, 1)


def fixed_tiles(nc, ctx):
    def sb(name, shape, dt=F32):
        return ctx.enter_context(nc.sbuf_tensor(name, shape, dt))

    k = {
        "ident": sb("ident", [P, P]), "ident16": sb("ident16", [P, P], F16),
        "below": sb("below", [P, P]), "below16": sb("below16", [P, P], F16),
        "ones": sb("ones", [P, P]), "cols16": sb("cols16", [P, T], F16),
        "dinv": sb("dinv", [P, T]), "one_rows": sb("one_rows", [3, P], BF16),
        "eps": sb("eps", [P, 1]),
    }
    for c in "rs":
        k["key_" + c] = sb("key_" + c, [P, T])
        k["before_" + c] = sb("before_" + c, [P, T])
        k["from_" + c] = sb("from_" + c, [P, T], I32)
        k["last_" + c] = sb("last_" + c, [P, T], I32)
    k["edge_r"] = sb("edge_r", [P, T], I32)
    k["weight_r"] = sb("weight_r", [P, T])
    k["weight_s"] = sb("weight_s", [P, T])
    k["vec_r"] = sb("vec_r", [P, T, 3])
    return k


def count_and_rank(nc, k, d, src, dst, edge_weight, edge_attr_3):
    with nc.cleanup_on_exit(), ExitStack() as ctx:
        ph = Phase(nc, ctx)
        sb, ps, sem = ph.sb, ph.ps, ph.sem
        key = [sb("key0", [P, T], I32), sb("key1", [P, T], I32)]
        other = sb("other", [P, T], I32)
        number = sb("number", [P, T], I32)
        cols_i = sb("cols_i", [P, T], I32)
        part = sb("part", [P, 2, T], I32)
        lo = [sb("lo0", [P, T]), sb("lo1", [P, T])]
        hi = [sb("hi0", [P, T]), sb("hi1", [P, T])]
        attr = sb("attr", [P, T * 3])
        weight = sb("weight", [P, T])
        fields = [sb("fields0", [P, T, 8]), sb("fields1", [P, T, 8])]
        one_lo = sb("one_lo", [P, 2, 4, P], F16)
        one_hi = sb("one_hi", [P, 2, 4, T], F16)
        lo_t = sb("lo_t", [P, 2, 4, P])
        lo_t16 = sb("lo_t16", [P, 2, 4, P], F16)
        same16 = sb("same16", [P, 2, 2, P], F16)
        table = sb("table", [P, 2, T])
        count = sb("count", [P, 2, T])
        begin = sb("begin", [P, 2, T])
        total = sb("total", [P, T])
        scan = sb("scan", [P, T])
        picked = sb("picked", [P, 2, T])
        found = sb("found", [P, 2, 2, J])
        found_i = sb("found_i", [P, 2, 2, J], I32)
        high_bits = sb("high_bits", [P, 2, 2, J], I32)
        degree = sb("degree", [P, T])
        ones_row = sb("ones_row", [P, T])
        idx = sb("idx", [P, 2, 2, J], I32)
        out_rows = sb("out_rows", [P, 2, 2, J, 8])
        run_ps = [ps("run0", [P, 512]), ps("run1", [P, 512])]
        look_ps = [ps("look0", [P, 512]), ps("look1", [P, 512])]
        turn_ps = [ps("turn0", [P, 1024], F16), ps("turn1", [P, 1024], F16)]
        same_ps = [ps("same0", [P, 512]), ps("same1", [P, 512])]

        fills, loaded, iotas = sem("fills"), sem("loaded"), sem("iotas")
        made, ready = sem("made"), sem("ready")
        hot, counted, hist, begun = sem("hot"), sem("counted"), sem("hist"), sem("begun")
        summed, hot2 = sem("summed"), sem("hot2")
        turned, turned_out, tabled = sem("turned"), sem("turned_out"), sem("tabled")
        same, masked, looked, ranked, updated = sem("same"), sem("masked"), sem("looked"), sem("ranked"), sem("updated")
        whole, shifted, fielded = sem("whole"), sem("shifted"), sem("fielded")
        rooted, staged = sem("rooted"), sem("staged")
        sent = [sem("sent0"), sem("sent1")]
        passed = sem("passed")
        block = ctx.enter_context(nc.Block())

        def edges(t, c=1):
            return (t[0:FULL * T * c].rearrange("(p t) -> p t", t=T * c),
                    t[FULL * T * c:N * c].rearrange("(a t) -> a t", a=1))

        @block.sync
        def _(sp):
            sp.wait_ge(fills, 6)
            flat = edge_attr_3.rearrange("n c -> (n c)")
            for tile, array, c in ((key[0], dst, 1), (key[1], src, 1), (other, dst, 1),
                                   (weight, edge_weight, 1), (attr, flat, 3)):
                a, b = edges(array, c)
                sp.dma_start(tile[0:FULL, :], a).then_inc(loaded, 16)
                sp.dma_start(tile[FULL:FULL + 1, 0:REST * c], b).then_inc(loaded, 16)
            a, b = edges(src)
            sp.dma_start(number[0:FULL, :], a).then_inc(loaded, 16)
            sp.dma_start(number[FULL:FULL + 1, 0:REST], b).then_inc(loaded, 16)

        @block.gpsimd
        def _(pool):
            nc.gpsimd.memset(k["ones"][:, :], 1.0).then_inc(made, 1)
            nc.gpsimd.iota(cols_i[:, :], pattern=[[1, T]], base=0, channel_multiplier=0).then_inc(iotas, 1)
            nc.gpsimd.iota(part[:, 0, :], pattern=[[1, T]], base=0, channel_multiplier=T).then_inc(iotas, 1)
            pool.wait_ge(made, 1)
            nc.gpsimd.affine_select(out=k["ident"][:, :], in_=k["ones"][:, :], compare_op=ALU.is_equal, fill=0.0,
                                    base=0, pattern=[[-1, P]], channel_multiplier=1).then_inc(made, 1)
            nc.gpsimd.affine_select(out=k["below"][:, :], in_=k["ones"][:, :], compare_op=ALU.is_gt, fill=0.0,
                                    base=0, pattern=[[1, P]], channel_multiplier=-1).then_inc(made, 1)

            def body(i):
                for par in range(2):
                    g = 2 * i + par
                    wait(pool, staged, g + 1, passed)
                    wait(pool, fielded, 2 * (g + 1), passed)
                    for c in range(2):
                        for j in range(J):
                            nc.gpsimd.indirect_dma_start(
                                d[f"sorted_{'rs'[c]}"], bass.IndirectOffsetOnAxis(ap=idx[:, par, c, j:j + 1], axis=0),
                                out_rows[:, par, c, j, :], None).then_inc(sent[par], 16)
            loop(pool, body)
            pool.wait_ge(sent[0], 16 * J * G)
            pool.wait_ge(sent[1], 16 * J * G)

        @block.vector
        def _(v):
            steps = [0]

            def step(ins):
                steps[0] += 1
                ins.then_inc(ready, 1)
                v.wait_ge(ready, steps[0])

            for tile, value in ((key[0], PAD), (key[1], PAD), (other, 0), (number, 0), (weight, 0), (attr, 0)):
                nc.vector.memset(tile[:, :], value).then_inc(fills, 1)
            nc.vector.memset(k["eps"][:, :], LN_EPS)
            nc.vector.memset(k["one_rows"][:, :], 1.0)
            nc.vector.memset(ones_row[:, :], 1.0)
            nc.vector.memset(fields[0][:, :, :], 0.0)
            step(nc.vector.memset(fields[1][:, :, :], 0.0))
            v.wait_ge(made, 3)
            nc.vector.tensor_copy(k["ident16"][:, :], k["ident"][:, :])
            nc.vector.tensor_copy(k["below16"][:, :], k["below"][:, :])
            v.wait_ge(iotas, 2)
            nc.vector.tensor_copy(k["cols16"][:, :], cols_i[:, :])
            v.wait_ge(loaded, 16 * 12)
            f0, f1 = fields
            nc.vector.tensor_copy(f0[:, :, 0], key[0][:, :])
            nc.vector.tensor_copy(f0[:, :, 1], number[:, :])
            nc.vector.tensor_scalar(f0[:, :, 2], part[:, 0, :], float(N - 1), None, ALU.min)
            nc.vector.tensor_copy(f0[:, :, 3], weight[:, :])
            nc.vector.tensor_copy(f0[:, :, 4:7], attr[:, :].rearrange("p (t c) -> p t c", c=3))
            nc.vector.tensor_copy(f1[:, :, 0], key[1][:, :])
            nc.vector.tensor_copy(f1[:, :, 1], other[:, :])
            step(nc.vector.tensor_copy(f1[:, :, 3], weight[:, :]))
            for c in range(2):
                step(nc.vector.tensor_scalar(part[:, 0, :], key[c][:, :], 2, P - 1, ALU.logical_shift_right, ALU.bitwise_and))
                step(nc.vector.tensor_copy(lo[c][:, :], part[:, 0, :]))
                step(nc.vector.tensor_scalar(part[:, 0, :], key[c][:, :], 9, 2, ALU.logical_shift_right, ALU.logical_shift_left))
                step(nc.vector.tensor_scalar(part[:, 1, :], key[c][:, :], J - 1, None, ALU.bitwise_and))
                step(nc.vector.tensor_tensor(part[:, 0, :], part[:, 0, :], part[:, 1, :], ALU.bitwise_or))
                step(nc.vector.tensor_copy(hi[c][:, :], part[:, 0, :]))

            def one_hots(t, slot, done, orders=(0, 1)):
                for c in orders:
                    nc.vector.tensor_scalar(one_lo[:, c, slot, :], k["cols16"][:, 0:P], lo[c][:, ds(t)], None, ALU.is_equal)
                    nc.vector.tensor_scalar(one_hi[:, c, slot, :], k["cols16"][:, :], hi[c][:, ds(t)], None,
                                            ALU.is_equal).then_inc(done, 1)

            def count_body(i):
                for r in range(4):
                    wait(v, counted, 2 * (4 * i + r - 3))
                    one_hots(4 * i + r, r, hot)
            count_body(0)
            with v.Fori(1, G) as i:
                count_body(i)
            v.wait_ge(counted, 2 * T)
            for c in range(2):
                step(nc.vector.tensor_copy(count[:, c, :], run_ps[c][:, 0:T]))
            v.sem_inc(hist, 1)
            step(nc.vector.tensor_scalar(degree[:, :], count[:, 0, :], 1.0, None, ALU.add))
            v.sem_inc(hist, 1)
            for c in range(2):
                v.wait_ge(summed, c + 1)
                step(nc.vector.tensor_copy(total[:, :], look_ps[c][:, 0:T]))
                step(nc.vector.tensor_tensor_scan(scan[:, :], ones_row[:, :], total[:, :], 0.0, ALU.mult, ALU.add))
                step(nc.vector.tensor_tensor(scan[:, :], scan[:, :], total[:, :], ALU.subtract))
                step(nc.vector.tensor_tensor(begin[:, c, :], scan[:, :], same_ps[c][:, 0:T], ALU.add))
            v.sem_inc(begun, 1)
            for c in range(2):
                last_i = k["last_" + "rs"[c]]
                step(nc.vector.tensor_tensor(scan[:, :], begin[:, c, :], count[:, c, :], ALU.add))
                step(nc.vector.tensor_scalar(scan[:, :], scan[:, :], 1.0, 0.0, ALU.subtract, ALU.max))
                step(nc.vector.tensor_copy(last_i[:, :], scan[:, :]))
                step(nc.vector.tensor_scalar(part[:, 0, :], last_i[:, :], 9, 9, ALU.logical_shift_right, ALU.logical_shift_left))
                step(nc.vector.tensor_scalar(part[:, 1, :], last_i[:, :], P - 1, 2, ALU.bitwise_and, ALU.logical_shift_left))
                step(nc.vector.tensor_tensor(part[:, 0, :], part[:, 0, :], part[:, 1, :], ALU.bitwise_or))
                step(nc.vector.tensor_scalar(part[:, 1, :], last_i[:, :], 7, J - 1, ALU.logical_shift_right, ALU.bitwise_and))
                step(nc.vector.tensor_tensor(part[:, 0, :], part[:, 0, :], part[:, 1, :], ALU.bitwise_or))
                step(nc.vector.tensor_copy(scan[:, :], part[:, 0, :]))
                step(nc.vector.tensor_scalar(total[:, :], count[:, c, :], 1.0, None, ALU.min))
                step(nc.vector.scalar_tensor_tensor(scan[:, :], scan[:, :], float(ZERO), total[:, :], ALU.subtract, ALU.mult))
                step(nc.vector.tensor_scalar(scan[:, :], scan[:, :], float(ZERO), None, ALU.add))
                step(nc.vector.tensor_copy(last_i[:, :], scan[:, :]))
            v.wait_ge(rooted, 1)
            nc.vector.reciprocal(k["dinv"][:, :], degree[:, :])

            def mask(t, slot):
                for c in range(2):
                    wait(v, same, 2 * t + c + 1)
                    nc.vector.tensor_tensor(same16[:, c, slot, :], same_ps[c][:, 0:P], k["below16"][:, :],
                                            ALU.mult).then_inc(masked, 1)

            def rank_group(i, q, last=False):
                g = 2 * i + q
                par, before = q % 2, (q - 1) % 2
                for r in range(4):
                    t = 4 * g + r
                    if not (last and r == 3):
                        mask(t + 1, (r + 1) % 2)
                    for c in range(2):
                        wait(v, looked, 2 * t + c + 1)
                        wait(v, ranked, 2 * t + c - 1)
                        if r == 0:
                            wait(v, whole, g - 1)
                        nc.vector.tensor_tensor_reduce(picked[:, c, :], look_ps[c][:, 0:T], one_hi[:, c, r, :], 1.0, 0.0,
                                                       ALU.mult, ALU.add, found[:, par, c, r:r + 1]).then_inc(ranked, 1)
                        if not (last and r >= 1):
                            wait(v, updated, 2 * t)
                            one_hots(t + 3, (r + 3) % 4, hot2, (c,))
                    if q and r < 3:
                        index_step(r, g - 1, i, before)

            def index_step(r, g, i, par):
                if r == 0:
                    wait(v, ranked, 8 * (g + 1))
                    nc.vector.tensor_copy(found_i[:, par, :, :], found[:, par, :, :]).then_inc(whole, 1)
                elif r == 1:
                    wait(v, whole, g + 1)
                    nc.vector.tensor_scalar(high_bits[:, par, :, :], found_i[:, par, :, :], P - 1, 9, ALU.bitwise_and,
                                            ALU.logical_shift_left).then_inc(shifted, 1)
                else:
                    wait(v, shifted, g + 1)
                    wait(v, sent[par], 16 * 2 * J * i)
                    nc.vector.scalar_tensor_tensor(idx[:, par, :, :], found_i[:, par, :, :], 7, high_bits[:, par, :, :],
                                                   ALU.logical_shift_right, ALU.bitwise_or).then_inc(staged, 1)
            for t in range(3):
                one_hots(t, t, hot2)
            mask(0, 0)
            shifted_pairs(v, rank_group)
            for r in range(3):
                index_step(r, G - 1, G // 2 - 1, 1)

        @block.scalar
        def _(act):
            act.wait_ge(hist, 2)
            nc.scalar.activation(degree[:, :], degree[:, :], ACT.Sqrt).then_inc(rooted, 1)

            def transposed(t, slot):
                for c in range(2):
                    wait(act, turned, 2 * t + c + 1)
                    wait(act, updated, 2 * (t - 3))
                    nc.scalar.copy(lo_t16[:, c, slot, :], turn_ps[c][:, 0:P])
                    nc.scalar.copy(lo_t[:, c, slot, :], turn_ps[c][:, 0:P]).then_inc(turned_out, 1)

            def running(c, need):
                wait(act, updated, need)
                nc.scalar.copy(table[:, c, :], run_ps[c][:, 0:T]).then_inc(tabled, 1)

            def fields_out(g, i, par):
                wait(act, sent[par], 16 * 2 * J * i)
                for c in range(2):
                    nc.scalar.copy(out_rows[:, par, c, :, :], fields[c][:, ds(g * J, J), :]).then_inc(fielded, 1)

            def group(i, q, last=False):
                g = 2 * i + q
                for r in range(4):
                    t = 4 * g + r
                    if last and r == 3:
                        continue
                    for c in range(2):
                        running(c, 2 * t + c + 1)
                        if c == 0 and not (last and r == 2):
                            transposed(t + 2, (r + 2) % 4)
                    if q and r == 1:
                        fields_out(g - 1, i, (q - 1) % 2)
            transposed(0, 0)
            transposed(1, 1)
            act.wait_ge(summed, 3)
            for c in range(2):
                nc.scalar.copy(table[:, c, :], run_ps[c][:, 0:T]).then_inc(tabled, 1)
            shifted_pairs(act, group)
            fields_out(G - 1, G // 2 - 1, 1)

        @block.tensor
        def _(pe):
            def count_body(i, first=False, last=False):
                for r in range(4):
                    for c in range(2):
                        wait(pe, hot, 2 * (4 * i + r) + c + 1)
                        nc.tensor.matmul(run_ps[c][:, 0:T], one_lo[:, c, r, :], one_hi[:, c, r, :],
                                         start=first and r == 0, stop=last and r == 3).then_inc(counted, 1)
            count_body(0, first=True)
            with pe.Fori(1, G - 1) as i:
                count_body(i)
            count_body(G - 1, last=True)
            pe.wait_ge(hist, 2)
            pe.wait_ge(made, 3)
            for c in range(2):
                nc.tensor.matmul(look_ps[c][:, 0:T], k["ones"][:, :], count[:, c, :], start=True, stop=True)
                nc.tensor.matmul(same_ps[c][:, 0:T], k["below"][:, :], count[:, c, :], start=True, stop=True).then_inc(summed, 1)
            pe.wait_ge(begun, 1)
            for c in range(2):
                last = nc.tensor.matmul(run_ps[c][:, 0:T], k["ident"][:, :], begin[:, c, :], start=True, stop=True)
            last.then_inc(summed, 1)

            def turn(t, slot):
                for c in range(2):
                    wait(pe, hot2, 2 * t + c + 1)
                    wait(pe, turned_out, 2 * t)
                    nc.tensor.transpose(turn_ps[c][:, 0:P], one_lo[:, c, slot, :], k["ident16"][:, :]).then_inc(turned, 1)

            def alike(t, slot):
                for c in range(2):
                    wait(pe, turned_out, 2 * t + c + 1)
                    wait(pe, masked, 2 * t)
                    nc.tensor.matmul(same_ps[c][:, 0:P], lo_t16[:, c, slot, :], lo_t16[:, c, slot, :],
                                     start=True, stop=True).then_inc(same, 1)

            def body(i, last=False):
                for r in range(4):
                    t = 4 * i + r
                    if not (last and r == 3):
                        alike(t + 1, (r + 1) % 4)
                    for c in range(2):
                        if c and not (last and r >= 2):
                            turn(t + 2, (r + 2) % 4)
                        wait(pe, tabled, 2 * t + c + 1)
                        wait(pe, masked, 2 * t + c + 1)
                        wait(pe, ranked, 2 * (t - 1) + c + 1)
                        nc.tensor.matmul(look_ps[c][:, 0:T], lo_t[:, c, r, :], table[:, c, :], start=True, stop=False)
                        nc.tensor.matmul(look_ps[c][:, 0:T], same16[:, c, r % 2, :], one_hi[:, c, r, :],
                                         start=False, stop=True).then_inc(looked, 1)
                        nc.tensor.matmul(run_ps[c][:, 0:T], one_lo[:, c, r, :], one_hi[:, c, r, :],
                                         start=False, stop=True, skip_group_check=True).then_inc(updated, 1)
            turn(0, 0)
            turn(1, 1)
            alike(0, 0)
            body(0)
            with pe.Fori(1, G - 1) as i:
                body(i)
            body(G - 1, last=True)


def order_tables(nc, k, d):
    H = T // J
    with nc.cleanup_on_exit(), ExitStack() as ctx:
        ph = Phase(nc, ctx)
        sb, ps, sem = ph.sb, ph.ps, ph.sem
        fields = [sb("fields0", [P, T, 8]), sb("fields1", [P, T, 8])]
        zeros = sb("zeros", [1, P + 1])
        turned_sb = sb("turned_sb", [H, 2, J, P])
        target = sb("target", [P, T])
        turn_ps = [ps("turn0", [H, 512]), ps("turn1", [H, 512])]
        loaded, made, ready, stored = sem("loaded"), sem("made"), sem("ready"), sem("stored")
        cut, turned, copied = sem("cut"), sem("turned"), sem("copied")
        block = ctx.enter_context(nc.Block())

        @block.sync
        def _(sp):
            for n, c in enumerate("rs"):
                sp.dma_start(fields[n][:, :, :], d["sorted_" + c].rearrange("(p t) f -> p t f", t=512)[:, 0:T, :]).then_inc(loaded, 16)
            sp.wait_ge(made, 1)
            for name, width in (("sum_r", P), ("sum_s", P + 1)):
                sp.dma_start(d[name][ZERO:ZERO + 1, :], zeros[:, 0:width]).then_inc(stored, 16)
            for n, c in enumerate("rs"):
                sp.wait_ge(copied, n + 1)
                sp.dma_start(d["line_" + c].rearrange("(b r e) -> r b e", r=H, e=P), turned_sb[:, n, :, :]).then_inc(stored, 16)
            sp.wait_ge(stored, 16 * 4)

        @block.tensor
        def _(pe):
            for n, c in enumerate("rs"):
                pe.wait_ge(cut, n + 1)
                for b in range(J):
                    last = nc.tensor.transpose(turn_ps[n][:, b * P:(b + 1) * P], k["key_" + c][:, b * H:(b + 1) * H], k["ident"][:, :])
                last.then_inc(turned, 1)

        @block.vector
        def _(v):
            steps = [0]

            def step(ins):
                steps[0] += 1
                ins.then_inc(ready, 1)
                v.wait_ge(ready, steps[0])

            nc.vector.memset(zeros[:, :], 0.0).then_inc(made, 1)
            v.wait_ge(loaded, 32)
            for n, c in enumerate("rs"):
                nc.vector.tensor_copy(k["key_" + c][:, :], fields[n][:, :, 0]).then_inc(cut, 1)
                nc.vector.tensor_copy(k["from_" + c][:, :], fields[n][:, :, 1])
                nc.vector.tensor_copy(k["weight_" + c][:, :], fields[n][:, :, 3])
            nc.vector.tensor_copy(k["edge_r"][:, :], fields[0][:, :, 2])
            nc.vector.tensor_copy(k["vec_r"][:, :, :], fields[0][:, :, 4:7])
            for n, c in enumerate("rs"):
                v.wait_ge(cut, n + 1)
                step(nc.vector.memset(k["before_" + c][:, :], -1.0))
                step(nc.vector.tensor_scalar(target[:, 1:T], k["key_" + c][:, 0:T - 1], 1.0, k["ident"][:, P - 1:P],
                                             ALU.add, ALU.mult))
                step(nc.vector.tensor_scalar(k["before_" + c][:, 1:T], target[:, 1:T], -1.0, None, ALU.add))
                v.wait_ge(turned, n + 1)
                nc.vector.tensor_copy(turned_sb[:, n, :, :], turn_ps[n][:, :].rearrange("r (b e) -> r b e", b=J)).then_inc(copied, 1)


def segment_sum(nc, k, c, sums, width=P, table=None, messages=None, added=None, weight=None, beside=None):
    with nc.cleanup_on_exit(), ExitStack() as ctx:
        ph = Phase(nc, ctx)
        sb, ps, sem = ph.sb, ph.ps, ph.sem
        key, before, source = (k[n + c] for n in ("key_", "before_", "from_"))
        rows = sb("rows", [P, RING, J, width])
        plus = sb("plus", [P, RING, W]) if added is not None else None
        relu = sb("relu", [P, 2, J, P]) if added is not None else None
        line = sb("line", [P, RING, W])
        equal = sb("equal", [P, 2, 2, 3 * P])
        carry = sb("carry", [P, 2, 2, 2 * P])
        sum_sb = sb("sum_sb", [P, 2, J, width])
        idx = sb("idx", [P, RING, J], I32)
        sum_ps = [ps(f"sum{n}", [P, 512]) for n in range(4)]
        came, lined, plussed, sent = ([sem(f"{n}{r}") for r in range(RING)] for n in ("came", "lined", "plussed", "sent"))
        staged, built, summed, taken = (sem(n) for n in ("staged", "built", "summed", "taken"))
        both, ready, ones_in, passed, passed_sp = (sem(n) for n in ("both", "ready", "ones_in", "passed", "passed_sp"))
        other = beside(ph) if beside is not None else {e: [] for e in ("sp", "pool", "act", "v", "pe", "stored")}
        block = ctx.enter_context(nc.Block())
        line_rows = k["line"][c].rearrange("(g w) -> g w", w=W)
        source_rows = relu if added is not None else rows

        def psum(par, pair):
            return sum_ps[2 * par + pair]

        @block.sync
        def _(sp):
            def front(i, g, slot):
                wait(sp, built, g - 3, passed_sp)
                sp.dma_start(line[:, slot, :], line_rows[ds(g), :].to_broadcast([P, W])).then_inc(lined[slot], 16)
                if added is not None:
                    wait(sp, ready, g - 3, passed_sp)
                    sp.dma_start(plus[:, slot, :], block_of(added, g)).then_inc(plussed[slot], 16)
                if messages is not None:
                    wait(sp, summed, 2 * (g - 3), passed_sp)
                    sp.dma_start(rows[:, slot, :, :].rearrange("p j d -> p (j d)"), block_of(messages, g)).then_inc(came[slot], 16)

            def store(i, g, slot):
                wait(sp, taken, 2 * (g + 1), passed_sp)
                sp.dma_start(rows_of(sums, g), sum_sb[:, slot % 2, :, :].rearrange("p j d -> p (j d)")).then_inc(sent[slot % 2], 16)
            paced(sp, (front, 4), (store, 0), *[(part(sp), lead) for part, lead in other["sp"]], ring=RING)
            for par in range(2):
                sp.wait_ge(sent[par], 16 * (G // 2))
                for stored in other["stored"]:
                    sp.wait_ge(stored[par], 16 * (G // 2))

        @block.gpsimd
        def _(pool):
            def gather(i, g, slot):
                wait(pool, staged, g + 1, passed)
                if added is not None:
                    wait(pool, both, g - 3, passed)
                else:
                    wait(pool, summed, 2 * (g - 3), passed)
                for j in range(J):
                    nc.gpsimd.indirect_dma_start(rows[:, slot, j, 0:P], None, table,
                                                 bass.IndirectOffsetOnAxis(ap=idx[:, slot, j:j + 1], axis=0)).then_inc(came[slot], 16)
            if width > P:
                nc.gpsimd.memset(rows[:, :, :, P:width], 1.0).then_inc(ones_in, 1)
            stages = [(gather, 0)] if table is not None else []
            stages += [(part(pool), lead) for part, lead in other["pool"]]
            if stages:
                paced(pool, *stages, ring=RING)

        @block.scalar
        def _(act):
            def stage(i, g, slot):
                wait(act, came[slot], 16 * J * i)
                nc.scalar.copy(idx[:, slot, :], source[:, ds(g * J, J)]).then_inc(staged, 1)

            def relu_part(i, g, slot):
                wait(act, both, g + 1)
                wait(act, summed, 2 * (g - 1))
                nc.scalar.activation(relu[:, slot % 2, :, :].rearrange("p j d -> p (j d)"), plus[:, slot, :], ACT.Relu).then_inc(ready, 1)

            def take(i, g, slot):
                par = slot % 2
                wait(act, sent[par], 16 * (2 * i + slot // 2))
                for pair in range(2):
                    wait(act, summed, 2 * g + pair + 1)
                    nc.scalar.copy(sum_sb[:, par, 2 * pair:2 * pair + 2, :].rearrange("p j d -> p (j d)"),
                                   psum(par, pair)[:, 0:2 * width]).then_inc(taken, 1)
            stages = [(take, 0)]
            if added is not None:
                stages = [(relu_part, 1)] + stages
            if table is not None:
                stages += [(stage, 4)]
            paced(act, *stages, *[(part(act), lead) for part, lead in other["act"]], ring=RING)

        @block.vector
        def _(v):
            def build(i, g, slot):
                par = slot % 2
                wait(v, lined[slot], 16 * (i + 1))
                wait(v, summed, 2 * (g - 1))
                for pair in range(2):
                    keys = line[:, slot, 2 * pair * P:2 * (pair + 1) * P]
                    t = g * J + 2 * pair
                    for n, (to, of) in enumerate(((equal[:, par, pair, 0:2 * P], keys), (equal[:, par, pair, 2 * P:3 * P], keys[:, P:2 * P]))):
                        if weight is None:
                            nc.vector.tensor_scalar(to, of, key[:, ds(t + n)], None, ALU.is_equal)
                        else:
                            nc.vector.tensor_scalar(to, of, key[:, ds(t + n)], weight[:, ds(t + n)], ALU.is_equal, ALU.mult)
                    last = nc.vector.tensor_scalar(carry[:, par, pair, :], keys, before[:, ds(t)], None, ALU.is_equal)
                last.then_inc(built, 1)

            def add(i, g, slot):
                wait(v, came[slot], 16 * J * (i + 1))
                wait(v, plussed[slot], 16 * (i + 1))
                nc.vector.tensor_tensor(plus[:, slot, :], plus[:, slot, :], rows[:, slot, :, :].rearrange("p j d -> p (j d)"),
                                        ALU.add).then_inc(both, 1)
            stages = [(build, 1)] + ([(add, 1)] if added is not None else [])
            paced(v, *stages, *[(part(v), lead) for part, lead in other["v"]], ring=RING)

        @block.tensor
        def _(pe):
            def sum_part(i, g, slot):
                par = slot % 2
                held = par if added is not None else slot
                wait(pe, built, g + 1)
                if added is not None:
                    wait(pe, ready, g + 1)
                else:
                    wait(pe, came[slot], 16 * (J if table is not None else 1) * (i + 1))
                wait(pe, taken, 2 * (g - 1))
                for pair in range(2):
                    first = isinstance(g, int) and g == 0 and pair == 0
                    bank, a, b = psum(par, pair), 2 * pair, 2 * pair + 1
                    nc.tensor.matmul(bank[:, 0:width], equal[:, par, pair, 0:P], source_rows[:, held, a, :], start=True, stop=False,
                                     skip_group_check=True)
                    nc.tensor.matmul(bank[:, width:2 * width], equal[:, par, pair, P:2 * P], source_rows[:, held, a, :], start=False,
                                     stop=False, skip_group_check=True)
                    last = nc.tensor.matmul(bank[:, width:2 * width], equal[:, par, pair, 2 * P:3 * P], source_rows[:, held, b, :],
                                            start=False, stop=first, skip_group_check=True)
                    if not first:
                        wait(pe, taken, 2 * g + pair)
                        before_sb = sum_sb[:, par, 1, :] if pair else sum_sb[:, 1 - par, J - 1, :]
                        for n in range(2):
                            last = nc.tensor.matmul(bank[:, n * width:(n + 1) * width], carry[:, par, pair, n * P:(n + 1) * P],
                                                    before_sb, start=False, stop=n == 1, skip_group_check=True)
                    last.then_inc(summed, 1)
            if width > P:
                pe.wait_ge(ones_in, 1)
            paced(pe, (sum_part, 0), *[(part(pe), lead) for part, lead in other["pe"]], ring=RING)


def split_rows(nc, ph, biases):
    n = len(biases)
    row, rest = ph.sb("row", [1, n, P]), ph.sb("rest", [1, n, P])
    pieces = [ph.sb(f"piece{r}", [1, n, J, P], BF16) for r in range(3)]
    came, cut, spread = ph.sem("row_came"), ph.sem("row_cut"), ph.sem("row_spread")

    def sp_part(sp):
        for b, (bias, _) in enumerate(biases):
            sp.dma_start(row[:, b, :], bias.rearrange("(a n) -> a n", a=1)).then_inc(came, 16)
        sp.wait_ge(cut, 5)
        for b, (_, tile) in enumerate(biases):
            for r in range(3):
                sp.dma_start(tile[r:r + 1, :], pieces[r][:, b, :, :].rearrange("p j d -> p (j d)")).then_inc(spread, 16)
        sp.wait_ge(spread, 16 * 3 * n)

    def v_part(v):
        v.wait_ge(came, 16 * n)
        of = row
        for r in range(3):
            wide = of[:, :, :].unsqueeze(2).to_broadcast([1, n, J, P])
            nc.vector.tensor_copy(pieces[r][:, :, :, :], wide).then_inc(cut, 1)
            v.wait_ge(cut, 2 * r + 1)
            if r < 2:
                nc.vector.tensor_tensor(rest[:, :, :], of[:, :, :], pieces[r][:, :, 0, :], ALU.subtract).then_inc(cut, 1)
                v.wait_ge(cut, 2 * r + 2)
                of = rest
    return sp_part, v_part


def tensor_product_weights(nc, k, w, ctx):
    t = {n: ctx.enter_context(nc.sbuf_tensor("tp_" + n, s, F32)) for n, s in {
        "up": [P, P], "mlp0": [J * NB, J, HID], "mlp1": [HID, HID], "mlp2": [HID, P], "mb0": [HID, 1], "mb1": [HID, 1],
        "out": [P, 2, P], "basis": [P, T, NB], "unit": [P, T, 3], "dir": [P, T, 3]}.items()}
    t["mb2"] = ctx.enter_context(nc.sbuf_tensor("tp_mb2", [3, W], BF16))
    with nc.cleanup_on_exit(), ExitStack() as inner:
        ph = Phase(nc, inner)
        sb, sem = ph.sb, ph.sem
        out1 = sb("out1", [P, 2, MUL])
        centre_i = sb("centre_i", [P, NB], I32)
        centre = sb("centre", [P, NB])
        clipped = sb("clipped", [P, T])
        away = sb("away", [P, T, NB])
        square = sb("square", [P, T, 3])
        length = sb("length", [P, T])
        cleared, loaded, ready, numbered, away_in, rooted, squared, waved = (sem(n) for n in (
            "cleared", "loaded", "ready", "numbered", "away_in", "rooted", "squared", "waved"))
        row_sp, row_v = split_rows(nc, ph, [(w["mlp_b2"], t["mb2"])])
        block = inner.enter_context(nc.Block())

        @block.sync
        def _(sp):
            sp.wait_ge(cleared, 3)
            sp.dma_start(t["up"][0:MUL, 0:MUL], w["W_up0"]).then_inc(loaded, 16)
            for c in range(3):
                sp.dma_start(t["up"][MUL + c:P:3, MUL * (c + 1):MUL * (c + 2)], w["W_up1"]).then_inc(loaded, 16)
            for j in range(J):
                sp.dma_start(t["mlp0"][j * NB:(j + 1) * NB, j, :], w["mlp_w0"]).then_inc(loaded, 16)
            sp.dma_start(t["mlp1"][:, :], w["mlp_w1"]).then_inc(loaded, 16)
            sp.dma_start(t["mlp2"][:, :], w["mlp_w2"]).then_inc(loaded, 16)
            sp.dma_start(t["mb0"][:, :], w["mlp_b0"].rearrange("(n a) -> n a", a=1)).then_inc(loaded, 16)
            sp.dma_start(t["mb1"][:, :], w["mlp_b1"].rearrange("(n a) -> n a", a=1)).then_inc(loaded, 16)
            sp.dma_start(t["out"][0:2 * MUL, 0, 0:MUL], w["W_out0"]).then_inc(loaded, 16)
            for half in range(2):
                sp.dma_start(out1[half * 2 * MUL:(half + 1) * 2 * MUL, 0, :], w["W_out1"]).then_inc(loaded, 16)
            row_sp(sp)

        @block.gpsimd
        def _(pool):
            nc.gpsimd.iota(centre_i[:, :], pattern=[[1, NB]], base=0, channel_multiplier=0).then_inc(numbered, 1)

        @block.scalar
        def _(act):
            act.wait_ge(squared, 1)
            nc.scalar.activation(length[:, :], length[:, :], ACT.Sqrt).then_inc(rooted, 1)
            act.wait_ge(away_in, 1)
            nc.scalar.activation(t["basis"][:, :, :], away[:, :, :], ACT.Exp, scale=-0.5 * (NB - 1) ** 2).then_inc(waved, 1)

        @block.vector
        def _(v):
            steps = [0]

            def step(ins):
                steps[0] += 1
                ins.then_inc(ready, 1)
                v.wait_ge(ready, steps[0])

            for name in ("up", "mlp0", "out"):
                tile = t[name]
                nc.vector.memset(tile[:, :] if name == "up" else tile[:, :, :], 0.0).then_inc(cleared, 1)
            row_v(v)
            step(nc.vector.tensor_tensor(square[:, :, :], k["vec_r"][:, :, :], k["vec_r"][:, :, :], ALU.mult))
            step(nc.vector.tensor_tensor(length[:, :], square[:, :, 0], square[:, :, 1], ALU.add))
            nc.vector.tensor_tensor(length[:, :], length[:, :], square[:, :, 2], ALU.add).then_inc(squared, 1)
            weight = k["weight_r"]
            v.wait_ge(numbered, 1)
            step(nc.vector.tensor_copy(centre[:, :], centre_i[:, :]))
            step(nc.vector.tensor_scalar(centre[:, :], centre[:, :], 1.0 / (NB - 1), None, ALU.mult))
            step(nc.vector.tensor_scalar(clipped[:, :], weight[:, :], 0.0, 1.0, ALU.max, ALU.min))
            step(nc.vector.tensor_tensor(away[:, :, :], clipped[:, :].unsqueeze(2).to_broadcast([P, T, NB]),
                                         centre[:, :].unsqueeze(1).to_broadcast([P, T, NB]), ALU.subtract))
            nc.vector.tensor_tensor(away[:, :, :], away[:, :, :], away[:, :, :], ALU.mult).then_inc(away_in, 1)
            v.wait_ge(rooted, 1)
            step(nc.vector.tensor_scalar(length[:, :], length[:, :], 1e-12, None, ALU.add))
            step(nc.vector.reciprocal(length[:, :], length[:, :]))
            step(nc.vector.tensor_tensor(t["unit"][:, :, :], k["vec_r"][:, :, :],
                                         length[:, :].unsqueeze(2).to_broadcast([P, T, 3]), ALU.mult))
            step(nc.vector.tensor_scalar(t["dir"][:, :, :], t["unit"][:, :, :], 3.0 ** 0.5, None, ALU.mult))
            step(nc.vector.tensor_scalar(clipped[:, :], weight[:, :], 1.0, NB ** 0.5, ALU.is_le, ALU.mult))
            v.wait_ge(waved, 1)
            nc.vector.tensor_tensor(t["basis"][:, :, :], t["basis"][:, :, :],
                                    clipped[:, :].unsqueeze(2).to_broadcast([P, T, NB]), ALU.mult)
            v.wait_ge(loaded, 16 * 15)
            nc.vector.tensor_scalar(t["up"][:, :], t["up"][:, :], MUL ** -0.5, None, ALU.mult)
            scale = (2 * MUL) ** -0.5 / AVG
            nc.vector.tensor_scalar(t["out"][0:2 * MUL, 0, 0:MUL], t["out"][0:2 * MUL, 0, 0:MUL], scale, None, ALU.mult)
            for c in range(3):
                half, at = (c + 1) % 2, (c + 1) // 2
                rows = slice(half * 2 * MUL, (half + 1) * 2 * MUL)
                nc.vector.tensor_scalar(t["out"][rows, at, MUL + c:P:3], out1[rows, 0, :], scale, None, ALU.mult)
    return t


def edge_products(nc, k, x, t, messages):
    with nc.cleanup_on_exit(), ExitStack() as ctx:
        ph = Phase(nc, ctx)
        sb, ps, sem = ph.sb, ph.ps, ph.sem
        rows = sb("rows", [P, 2, J, P])
        idx = sb("idx", [P, 2, J], I32)
        wave = sb("wave", [P, 2, J * NB])
        wave_t = sb("wave_t", [J * NB, 2, P])
        rows_t = sb("rows_t", [P, 2, W])
        hid0 = sb("hid0", [HID, 2, W])
        hid1 = sb("hid1", [HID, 2, W])
        gate = sb("gate", [P, 2, J, P])
        up = sb("up", [P, 2, J, P])
        mixed = sb("mixed", [P, 2, J, 2 * P])
        along = sb("along", [P, J, MUL])
        part = sb("part", [P, 3, J, MUL])
        dot = sb("dot", [P, J, MUL])
        mixed_t = sb("mixed_t", [P, 2, 2, W])
        out = sb("out", [P, 2, W])
        wave_ps = ps("wave", [J * NB, 512])
        turn_ps = ps("turn", [P, 512])
        up_ps = ps("up", [P, J, P])
        hid_ps = ps("hid", [HID, 512])
        gate_ps = ps("gate", [P, J, P])
        mix_ps = [ps("mix0", [P, 512]), ps("mix1", [P, 512])]
        out_ps = ps("out", [P, 512])
        came = [sem("came0"), sem("came1")]
        stored = [sem("stored0"), sem("stored1")]
        (staged, waved, wave_up, wave_down, rows_up, rows_down, up_up, up_down, hid0_up, hid0_down, hid1_up, hid1_down,
         gate_up, gate_down, dots, mixed_in, mix0_up, mix0_down, mix1_up, mix1_down, out_up, out_down, passed, passed_sp,
         passed_pe) = (sem(n) for n in (
            "staged", "waved", "wave_up", "wave_down", "rows_up", "rows_down", "up_up", "up_down", "hid0_up", "hid0_down",
            "hid1_up", "hid1_down", "gate_up", "gate_down", "dots", "mixed_in", "mix0_up", "mix0_down", "mix1_up", "mix1_down",
            "out_up", "out_down", "passed", "passed_sp", "passed_pe"))
        block = ctx.enter_context(nc.Block())

        @block.gpsimd
        def _(pool):
            def gather(i, g, par):
                wait(pool, staged, g + 1, passed)
                wait(pool, rows_up, g - 1, passed)
                for j in range(J):
                    nc.gpsimd.indirect_dma_start(rows[:, par, j, :], None, x,
                                                 bass.IndirectOffsetOnAxis(ap=idx[:, par, j:j + 1], axis=0)).then_inc(came[par], 16)
            paced(pool, (gather, 0))

        @block.sync
        def _(sp):
            def store(i, g, par):
                wait(sp, out_down, g + 1, passed_sp)
                sp.dma_start(block_of(messages, g), out[:, par, :]).then_inc(stored[par], 16)
            paced(sp, (store, 0))
            for par in range(2):
                sp.wait_ge(stored[par], 16 * (G // 2))

        @block.scalar
        def _(act):
            def down(to, of, up_sem, down_sem, used, func=ACT.Copy, bias=None):
                def part(i, g, par):
                    wait(act, up_sem, g + 1)
                    wait(act, used, g - 1)
                    if bias is None:
                        nc.scalar.copy(to(par), of).then_inc(down_sem, 1)
                    else:
                        nc.scalar.activation(to(par), of, func, bias=bias).then_inc(down_sem, 1)
                return part

            def out_part(i, g, par):
                wait(act, out_up, g + 1)
                wait(act, stored[par], 16 * i)
                nc.scalar.copy(out[:, par, :], out_ps[:, :]).then_inc(out_down, 1)

            paced(act,
                  (down(lambda q: hid1[:, q, :], hid_ps[:, :], hid1_up, hid1_down, gate_up, func=ACT.Silu, bias=t["mb1"][:, :]), 1),
                  (down(lambda q: gate[:, q, :, :], gate_ps[:, :, :], gate_up, gate_down, mixed_in), 0),
                  (out_part, -3),
                  (down(lambda q: hid0[:, q, :], hid_ps[:, :], hid0_up, hid0_down, hid1_up, func=ACT.Silu, bias=t["mb0"][:, :]), 2),
                  (down(lambda q: up[:, q, :, :], up_ps[:, :, :], up_up, up_down, mixed_in), 0),
                  (down(lambda q: mixed_t[:, q, 1, :], mix_ps[1][:, :], mix1_up, mix1_down, out_up), -2),
                  (down(lambda q: wave_t[:, q, :], wave_ps[:, 0:P], wave_up, wave_down, hid0_up), 3),
                  (down(lambda q: rows_t[:, q, :], turn_ps[:, :], rows_up, rows_down, up_up), 1))

        @block.vector
        def _(v):
            def stage(i, g, par):
                wait(v, wave_up, g - 1)
                nc.vector.tensor_copy(wave[:, par, :], t["basis"][:, ds(g * J, J), :].rearrange("p t n -> p (t n)")).then_inc(waved, 1)
                wait(v, came[par], 16 * J * i)
                nc.vector.tensor_copy(idx[:, par, :], k["from_r"][:, ds(g * J, J)]).then_inc(staged, 1)

            def mix(i, g, par):
                wait(v, gate_down, g + 1)
                wait(v, up_down, g + 1)
                wait(v, mix1_up, g - 1)
                f, w, m = up[:, par, :, :], gate[:, par, :, :], mixed[:, par, :, :]
                unit, along_dir = (t[n][:, ds(g * J, J), :] for n in ("unit", "dir"))
                nc.vector.tensor_tensor(along[:, :, :], w[:, :, MUL:2 * MUL], f[:, :, 0:MUL], ALU.mult)
                for c in range(3):
                    last = nc.vector.tensor_tensor(part[:, c, :, :], f[:, :, MUL * (c + 1):MUL * (c + 2)],
                                                   unit[:, :, c:c + 1].to_broadcast([P, J, MUL]), ALU.mult)
                last.then_inc(dots, 1)
                nc.vector.tensor_tensor(m[:, :, 0:MUL], w[:, :, 0:MUL], f[:, :, 0:MUL], ALU.mult)
                for c in range(3):
                    at = 2 * MUL * (c + 1)
                    nc.vector.tensor_tensor(m[:, :, at + MUL:at + 2 * MUL], w[:, :, 2 * MUL:3 * MUL],
                                            f[:, :, MUL * (c + 1):MUL * (c + 2)], ALU.mult)
                wait(v, dots, 3 * g + 1)
                nc.vector.tensor_tensor(dot[:, :, :], part[:, 0, :, :], part[:, 1, :, :], ALU.add).then_inc(dots, 1)
                for c in range(3):
                    at = 2 * MUL * (c + 1)
                    nc.vector.tensor_tensor(m[:, :, at:at + MUL], along[:, :, :],
                                            along_dir[:, :, c:c + 1].to_broadcast([P, J, MUL]), ALU.mult)
                wait(v, dots, 3 * g + 2)
                nc.vector.tensor_tensor(part[:, 0, :, :], dot[:, :, :], part[:, 2, :, :], ALU.add).then_inc(dots, 1)
                wait(v, dots, 3 * g + 3)
                nc.vector.tensor_tensor(m[:, :, MUL:2 * MUL], part[:, 0, :, :], w[:, :, 3 * MUL:4 * MUL], ALU.mult).then_inc(mixed_in, 1)

            def mix_down(i, g, par):
                wait(v, mix0_up, g + 1)
                wait(v, out_up, g - 1)
                nc.vector.tensor_copy(mixed_t[:, par, 0, :], mix_ps[0][:, :]).then_inc(mix0_down, 1)

            def head(i, g, par):
                wait(v, mixed_in, g)
            paced(v, (stage, 4), (mix_down, -2), (head, -1), (mix, -1))

        @block.tensor
        def _(pe):
            def hid1_part(i, g, par):
                wait(pe, hid0_down, g + 1, passed_pe)
                wait(pe, hid1_down, g, passed_pe)
                nc.tensor.matmul(hid_ps[:, :], t["mlp1"][:, :], hid0[:, par, :], start=True, stop=True).then_inc(hid1_up, 1)

            def gate_part(i, g, par):
                wait(pe, hid1_down, g + 1)
                wait(pe, gate_down, g)
                nc.tensor.matmul(gate_ps[:, :, :].rearrange("p j d -> p (j d)"), k["one_rows"][:, :], t["mb2"][:, :], start=True, stop=False)
                for j in range(J):
                    m = nc.tensor.matmul(gate_ps[:, j, :], hid1[:, par, j * P:(j + 1) * P], t["mlp2"][:, :], start=False, stop=j == J - 1)
                m.then_inc(gate_up, 1)

            def out_part(i, g, par):
                wait(pe, mix0_down, g + 1)
                wait(pe, mix1_down, g + 1)
                wait(pe, out_down, g)
                for j in range(J):
                    for h in range(2):
                        m = nc.tensor.matmul(out_ps[:, j * P:(j + 1) * P], mixed_t[:, par, h, j * P:(j + 1) * P], t["out"][:, h, :],
                                             start=h == 0, stop=h == 1)
                m.then_inc(out_up, 1)

            def hid0_part(i, g, par):
                wait(pe, wave_down, g + 1)
                wait(pe, hid1_down, g)
                for j in range(J):
                    m = nc.tensor.matmul(hid_ps[:, j * P:(j + 1) * P], t["mlp0"][:, j, :], wave_t[:, par, :], start=True, stop=True)
                m.then_inc(hid0_up, 1)

            def up_part(i, g, par):
                wait(pe, rows_down, g + 1)
                wait(pe, up_down, g)
                for j in range(J):
                    m = nc.tensor.matmul(up_ps[:, j, :], rows_t[:, par, j * P:(j + 1) * P], t["up"][:, :], start=True, stop=True)
                m.then_inc(up_up, 1)

            def mix_part(i, g, par):
                wait(pe, mixed_in, g + 1)
                for h, down, up_sem in ((0, mix0_down, mix0_up), (1, mix1_down, mix1_up)):
                    wait(pe, down, g)
                    for j in range(J):
                        m = nc.tensor.transpose(mix_ps[h][:, j * P:(j + 1) * P], mixed[:, par, j, h * P:(h + 1) * P], k["ident"][:, :])
                    m.then_inc(up_sem, 1)

            def wave_part(i, g, par):
                wait(pe, waved, g + 1)
                wait(pe, wave_down, g)
                nc.tensor.transpose(wave_ps[:, 0:P], wave[:, par, :], k["ident"][:, :]).then_inc(wave_up, 1)

            def rows_part(i, g, par):
                wait(pe, came[par], 16 * J * (i + 1))
                wait(pe, rows_down, g)
                for j in range(J):
                    m = nc.tensor.transpose(turn_ps[:, j * P:(j + 1) * P], rows[:, par, j, :], k["ident"][:, :])
                m.then_inc(rows_up, 1)

            paced(pe, (hid1_part, 1), (gate_part, 0), (out_part, -3), (hid0_part, 2), (up_part, 0), (mix_part, -2),
                  (wave_part, 3), (rows_part, 1))


def load_weights(nc, k, ctx, w):
    shapes = {"W1": [P, P], "R1": [P, P], "W2": [P, P], "R2": [P, P], "W3Wh": [P, P], "lin_t": [P, P],
              "atom": [P, P], "bond": [P, P],
              "gin1": [P, LAYERS, 2 * P], "gin2": [P, LAYERS, 2, P], "final": [P, P],
              "eps_row": [P, LAYERS], "b1": [P, LAYERS, 2], "g1": [P, LAYERS, 2], "be1": [P, LAYERS, 2],
              "b2": [P, LAYERS], "gn": [P, LAYERS], "bet": [P, LAYERS]}
    m = {n: ctx.enter_context(nc.sbuf_tensor("w_" + n, s, F32)) for n, s in shapes.items()}
    rows = {"bh": "L1_gnn_bh", "lin_b": "L2_gnn_b", "atom_b": "L3_gnn_b_atom", "bond_b": "L3_gnn_b_bond", "final_b": "L3_gnn_b_out"}
    for n in rows:
        m[n] = ctx.enter_context(nc.sbuf_tensor("w_" + n, [3, W], BF16))

    def row(a):
        return a.rearrange("(a n) -> a n", a=1)

    loads = [(m["W1"][:, :], w["L1_gnn_W1"]), (m["R1"][:, :], w["L1_gnn_R1"]), (m["W2"][:, :], w["L1_gnn_W2"]),
             (m["R2"][:, :], w["L1_gnn_R2"]), (m["atom"][:, :], w["L3_gnn_W_atom"]), (m["bond"][:, :], w["L3_gnn_W_bond"]),
             (m["final"][:, :], w["L3_gnn_W_out"]),
             (m["eps_row"][:, :], row(w["L3_gnn_eps"]).to_broadcast([P, LAYERS]))]
    for i in range(LAYERS):
        loads.append((m["gin1"][:, i, :], w["L3_gnn_W1"][i]))
        for h in range(2):
            loads.append((m["gin2"][:, i, h, :], w["L3_gnn_W2"][i, h * P:(h + 1) * P, :]))
            for n in ("b1", "g1", "be1"):
                loads.append((m[n][:, i, h:h + 1], w["L3_gnn_" + n][i, h * P:(h + 1) * P].rearrange("(p a) -> p a", a=1)))
        for n in ("b2", "gn", "bet"):
            loads.append((m[n][:, i:i + 1], w["L3_gnn_" + n][i].rearrange("(p a) -> p a", a=1)))
    with nc.cleanup_on_exit(), ExitStack() as inner:
        ph = Phase(nc, inner)
        w3, wh, lin, w3t = (ph.sb(n, [P, P]) for n in ("w3", "wh", "lin", "w3t"))
        turn_ps, lin_ps, product_ps = (ph.ps(n, [P, 512]) for n in ("turn", "lin", "product"))
        loaded, turned, copied, multiplied = (ph.sem(n) for n in ("loaded", "turned", "copied", "multiplied"))
        row_sp, row_v = split_rows(nc, ph, [(w[a], m[n]) for n, a in rows.items()])
        loads += [(w3[:, :], w["L1_gnn_W3"]), (wh[:, :], w["L1_gnn_Wh"]), (lin[:, :], w["L2_gnn_W"])]
        block = inner.enter_context(nc.Block())

        @block.sync
        def _(sp):
            for to, of in loads:
                sp.dma_start(to, of).then_inc(loaded, 16)
            row_sp(sp)

        @block.tensor
        def _(pe):
            pe.wait_ge(loaded, 16 * len(loads))
            nc.tensor.transpose(turn_ps[:, 0:P], w3[:, :], k["ident"][:, :]).then_inc(turned, 1)
            nc.tensor.transpose(lin_ps[:, 0:P], lin[:, :], k["ident"][:, :]).then_inc(turned, 1)
            pe.wait_ge(copied, 1)
            nc.tensor.matmul(product_ps[:, 0:P], w3t[:, :], wh[:, :], start=True, stop=True).then_inc(multiplied, 1)

        @block.vector
        def _(v):
            row_v(v)
            v.wait_ge(loaded, 16 * len(loads))
            nc.vector.tensor_scalar(m["eps_row"][:, :], m["eps_row"][:, :], 1.0, None, ALU.add)
            v.wait_ge(turned, 1)
            nc.vector.tensor_copy(w3t[:, :], turn_ps[:, 0:P]).then_inc(copied, 1)
            v.wait_ge(turned, 2)
            nc.vector.tensor_copy(m["lin_t"][:, :], lin_ps[:, 0:P])
            v.wait_ge(multiplied, 1)
            nc.vector.tensor_copy(m["W3Wh"][:, :], product_ps[:, 0:P])
    return m


def bond_rows(nc, k, edge_attr, m, bonds):
    def make(ph):
        sb, ps, sem = ph.sb, ph.ps, ph.sem
        rows = sb("bond_rows", [P, RING, J, P])
        idx = sb("bond_idx", [P, RING, J], I32)
        rows_t = sb("bond_rows_t", [P, 2, W])
        out = sb("bond_out", [P, 2, W])
        turn_ps = [ps("bond_turn0", [P, 512]), ps("bond_turn1", [P, 512])]
        out_ps = [ps("bond_out0", [P, 512]), ps("bond_out1", [P, 512])]
        came = [sem(f"bond_came{r}") for r in range(RING)]
        stored = [sem("bond_stored0"), sem("bond_stored1")]
        staged, turned, rows_down, made, out_down, passed, passed_sp = (sem("bond_" + n) for n in (
            "staged", "turned", "rows_down", "made", "out_down", "passed", "passed_sp"))

        def gather_in(pool):
            def gather(i, g, slot):
                wait(pool, staged, g + 1, passed)
                wait(pool, turned, g - 3, passed)
                for j in range(J):
                    nc.gpsimd.indirect_dma_start(rows[:, slot, j, :], None, edge_attr,
                                                 bass.IndirectOffsetOnAxis(ap=idx[:, slot, j:j + 1], axis=0)).then_inc(came[slot], 16)
            return gather

        def store_in(sp):
            def store(i, g, slot):
                wait(sp, out_down, g + 1, passed_sp)
                sp.dma_start(block_of(bonds, g), out[:, slot % 2, :]).then_inc(stored[slot % 2], 16)
            return store

        def rows_down_in(act):
            def part(i, g, slot):
                par = slot % 2
                wait(act, turned, g + 1)
                wait(act, made, g - 1)
                nc.scalar.copy(rows_t[:, par, :], turn_ps[par][:, :]).then_inc(rows_down, 1)
            return part

        def stage_in(v):
            def stage(i, g, slot):
                wait(v, came[slot], 16 * J * i)
                nc.vector.tensor_copy(idx[:, slot, :], k["edge_r"][:, ds(g * J, J)]).then_inc(staged, 1)
            return stage

        def out_down_in(v):
            def part(i, g, slot):
                par = slot % 2
                wait(v, made, g + 1)
                wait(v, stored[par], 16 * (2 * i + slot // 2))
                nc.vector.tensor_copy(out[:, par, :], out_ps[par][:, :]).then_inc(out_down, 1)
            return part

        def turn_in(pe):
            def turn(i, g, slot):
                par = slot % 2
                wait(pe, came[slot], 16 * J * (i + 1))
                wait(pe, rows_down, g - 1)
                for j in range(J):
                    t = nc.tensor.transpose(turn_ps[par][:, j * P:(j + 1) * P], rows[:, slot, j, :], k["ident"][:, :])
                t.then_inc(turned, 1)
            return turn

        def product_in(pe):
            def product(i, g, slot):
                par = slot % 2
                wait(pe, rows_down, g + 1)
                wait(pe, out_down, g - 1)
                nc.tensor.matmul(out_ps[par][:, :], k["one_rows"][:, :], m["bond_b"][:, :], start=True, stop=False)
                for j in range(J):
                    t = nc.tensor.matmul(out_ps[par][:, j * P:(j + 1) * P], rows_t[:, par, j * P:(j + 1) * P], m["bond"][:, :],
                                         start=False, stop=j == J - 1)
                t.then_inc(made, 1)
            return product

        return {"pool": [(gather_in, 1)], "sp": [(store_in, -2)], "act": [(rows_down_in, 0)],
                "v": [(stage_in, 4), (out_down_in, -1)], "pe": [(turn_in, 0), (product_in, -1)], "stored": [stored]}
    return make


def node_rows(nc, k, x, sums, out1, out2, *, gcn=False, first=(), bias1=None, residual=None, norm=True,
              weighted=False, second=None, bias2=None, relu2=False, outside=False):
    width = P + 1 if weighted else P
    with nc.cleanup_on_exit(), ExitStack() as ctx:
        ph = Phase(nc, ctx)
        sb, ps, sem = ph.sb, ph.ps, ph.sem
        x_in = sb("x_in", [P, 2, J, P])
        s_in = sb("s_in", [P, 2, J, width])
        r_in = sb("r_in", [P, 2, W]) if residual is not None else None
        u = sb("u", [P, 2, W])
        u_t = sb("u_t", [P, 2, W])
        x_t = sb("x_t", [P, 2, W])
        y = sb("y", [P, 2, W])
        o1 = sb("o1", [P, 2, J, P])
        o1_t = sb("o1_t", [P, 2, W])
        o2 = sb("o2", [P, 2, J, P])
        parts = sb("parts", [P, 2, J, 6])
        moments = sb("moments", [P, 2, J, 2])
        spread = sb("spread", [P, 2, J])
        inverse = sb("inverse", [P, 2, J])
        low = sb("low", [P, 2, J])
        share = sb("share", [P, 2, J])
        minus_half = sb("minus_half", [P, J])
        idx = sb("idx", [P, 2, J], I32)
        tu_ps, tx_ps, t2_ps = (ps(n, [P, 512]) for n in ("tu", "tx", "t2"))
        m1_ps = [ps("m10", [P, 512]), ps("m11", [P, 512])]
        m2_ps = [ps("m20", [P, 512]), ps("m21", [P, 512])]
        came, r_came, gathered, stored1, stored2 = ([sem(n + "0"), sem(n + "1")] for n in (
            "came", "r_came", "gathered", "stored1", "stored2"))
        (u_step, u_made, y_made, halved, measured, joined, spread_in, raised, o1_made, o2_made, tu, tx, u_down, x_down,
         m1, t2, o1_down, m2, lows, staged, passed, passed_sp, passed_v) = (sem(n) for n in (
            "u_step", "u_made", "y_made", "halved", "measured", "joined", "spread_in", "raised", "o1_made", "o2_made",
            "tu", "tx", "u_down", "x_down", "m1", "t2", "o1_down", "m2", "lows", "staged", "passed", "passed_sp", "passed_v"))
        last_edge = k["last_s" if weighted else "last_r"]
        late = -2 if gcn else -1
        used = u_made if gcn else y_made
        block = ctx.enter_context(nc.Block())

        @block.sync
        def _(sp):
            def front(i, g, par):
                wait(sp, used, g - 1, passed_sp)
                if len(first) == 2:
                    wait(sp, tx, g - 1, passed_sp)
                flat = x_in[:, par, :, :].rearrange("p j d -> p (j d)")
                if outside and isinstance(g, int) and g == G - 1:
                    sp.dma_start(flat[0:LASTP, :], x_rows(x, last=True)).then_inc(came[par], 16)
                else:
                    source = block_of(x_rows(x), g) if outside else rows_of(x, g)
                    sp.dma_start(flat, source).then_inc(came[par], 16)

            def r_front(i, g, par):
                wait(sp, y_made, g - 1, passed_sp)
                sp.dma_start(r_in[:, par, :], rows_of(residual, g)).then_inc(r_came[par], 16)

            def back1(i, g, par):
                wait(sp, o1_made, g + 1, passed_sp)
                sp.dma_start(rows_of(out1, g), o1[:, par, :, :].rearrange("p j d -> p (j d)")).then_inc(stored1[par], 16)

            def back2(i, g, par):
                wait(sp, o2_made, g + 1, passed_sp)
                sp.dma_start(rows_of(out2, g), o2[:, par, :, :].rearrange("p j d -> p (j d)")).then_inc(stored2[par], 16)
            stages = [(front, 3), (r_front, 2)] if residual is not None else [(front, 2)]
            if gcn and norm:
                paced(sp, (back1, -2), *stages, (back2, -3))
            else:
                paced(sp, *stages, (back1, -2 if norm else -1), (back2, -2 if norm else -1))
            for par in range(2):
                sp.wait_ge(stored1[par], 16 * (G // 2))
                sp.wait_ge(stored2[par], 16 * (G // 2))

        @block.gpsimd
        def _(pool):
            nc.gpsimd.memset(minus_half[:, :], -0.5).then_inc(halved, 1)
            pool.wait_ge(halved, 1)

            def gather(i, g, par):
                wait(pool, staged, g + 1, passed)
                wait(pool, used, g - 1, passed)
                for j in range(J):
                    nc.gpsimd.indirect_dma_start(s_in[:, par, j, :], None, sums,
                                                 bass.IndirectOffsetOnAxis(ap=idx[:, par, j:j + 1], axis=0)).then_inc(gathered[par], 16)

            def raise_part(i, g, par):
                wait(pool, spread_in, g + 1, passed)
                nc.gpsimd.tensor_tensor(inverse[:, par, :], spread[:, par, :], minus_half[:, :], ALU.pow).then_inc(raised, 1)
            paced(pool, (gather, 2), *([(raise_part, -1 if gcn else 0)] if norm else []))

        @block.vector
        def _(v):
            def front(i, g, par):
                wait(v, came[par], 16 * (i + 1))
                wait(v, gathered[par], 16 * J * (i + 1))
                dinv = k["dinv"][:, ds(g * J, J)].unsqueeze(2).to_broadcast([P, J, P])
                u3 = u[:, par, :].rearrange("p (j d) -> p j d", j=J)
                wait(v, tu, g - 1)
                nc.vector.tensor_tensor(u3, x_in[:, par, :, :], dinv, ALU.mult).then_inc(u_step, 1)
                wait(v, u_step, 2 * g + 1)
                nc.vector.tensor_tensor(u3, u3, s_in[:, par, :, :], ALU.add).then_inc(u_step, 1)
                wait(v, u_step, 2 * g + 2)
                nc.vector.tensor_tensor(u3, u3, dinv, ALU.mult).then_inc(u_made, 1)

            def measure(i, g, par):
                wait(v, o1_made, g - 1)
                if gcn:
                    wait(v, m1, g + 1)
                    wait(v, r_came[par], 16 * (i + 1))
                    nc.vector.tensor_tensor(y[:, par, :], m1_ps[par][:, :], r_in[:, par, :], ALU.add).then_inc(y_made, 1)
                elif weighted:
                    wait(v, came[par], 16 * (i + 1))
                    wait(v, gathered[par], 16 * J * (i + 1))
                    nc.vector.tensor_scalar(low[:, par, :], s_in[:, par, :, P], 0.5, None, ALU.is_lt).then_inc(lows, 1)
                    wait(v, lows, 3 * g + 1)
                    nc.vector.tensor_tensor(low[:, par, :], low[:, par, :], s_in[:, par, :, P], ALU.add).then_inc(lows, 1)
                    wait(v, lows, 3 * g + 2)
                    nc.vector.reciprocal(share[:, par, :], low[:, par, :]).then_inc(lows, 1)
                    wait(v, lows, 3 * g + 3)
                    for j in range(J):
                        last = nc.vector.scalar_tensor_tensor(y[:, par, j * P:(j + 1) * P], s_in[:, par, j, 0:P], share[:, par, j:j + 1],
                                                              x_in[:, par, j, :], ALU.mult, ALU.add)
                    last.then_inc(y_made, 1)
                else:
                    wait(v, came[par], 16 * (i + 1))
                    wait(v, gathered[par], 16 * J * (i + 1))
                    nc.vector.tensor_tensor(y[:, par, :], x_in[:, par, :, :].rearrange("p j d -> p (j d)"),
                                            s_in[:, par, :, :].rearrange("p j d -> p (j d)"), ALU.add).then_inc(y_made, 1)
                wait(v, y_made, g + 1)
                for j in range(J):
                    last = nc.vector.bn_stats(parts[:, par, j, :], y[:, par, j * P:(j + 1) * P])
                last.then_inc(measured, 1)
                wait(v, measured, g + 1, passed_v)
                for j in range(J):
                    last = nc.vector.bn_aggr(moments[:, par, j, :], parts[:, par, j, :])
                last.then_inc(joined, 1)
                wait(v, joined, g + 1)
                nc.vector.tensor_scalar(spread[:, par, :], moments[:, par, :, 1], LN_EPS, None, ALU.add).then_inc(spread_in, 1)

            def apply(i, g, par):
                wait(v, stored1[par], 16 * i)
                if second is None:
                    wait(v, o2_made, g - 1)
                else:
                    wait(v, t2, g - 1)
                wait(v, raised, g + 1)
                for j in range(J):
                    last = nc.vector.tensor_scalar(o1[:, par, j, :], y[:, par, j * P:(j + 1) * P], moments[:, par, j, 0:1],
                                                   inverse[:, par, j:j + 1], ALU.subtract, ALU.mult)
                last.then_inc(o1_made, 1)

            def stage(i, g, par):
                wait(v, gathered[par], 16 * J * i)
                nc.vector.tensor_copy(idx[:, par, :], last_edge[:, ds(g * J, J)]).then_inc(staged, 1)

            stages = [(stage, 3), (front, 1)] if gcn else [(stage, 2)]
            stages += [(measure, 0), (apply, -1)] if norm else []
            paced(v, *stages)

        @block.scalar
        def _(act):
            def turn_down(i, g, par):
                wait(act, tu, g + 1)
                wait(act, m1, g - 1)
                nc.scalar.copy(u_t[:, par, :], tu_ps[:, :]).then_inc(u_down, 1)
                if len(first) == 2:
                    wait(act, tx, g + 1)
                    nc.scalar.copy(x_t[:, par, :], tx_ps[:, :]).then_inc(x_down, 1)

            def relu_out(i, g, par):
                wait(act, m1, g + 1)
                wait(act, stored1[par], 16 * i)
                wait(act, o2_made, g - 1)
                nc.scalar.activation(o1[:, par, :, :].rearrange("p j d -> p (j d)"), m1_ps[par][:, :], ACT.Relu).then_inc(o1_made, 1)

            def scale_out(i, g, par):
                wait(act, stored2[par], 16 * i)
                wait(act, o1_made, g + 1)
                for j in range(J):
                    last = nc.scalar.activation(o2[:, par, j, :], o1[:, par, j, :], ACT.Copy, scale=k["dinv"][:, ds(g * J + j)])
                last.then_inc(o2_made, 1)

            def out_down(i, g, par):
                wait(act, t2, g + 1)
                wait(act, m2, g - 1)
                nc.scalar.copy(o1_t[:, par, :], t2_ps[:, :]).then_inc(o1_down, 1)

            def second_out(i, g, par):
                wait(act, stored2[par], 16 * i)
                wait(act, m2, g + 1)
                nc.scalar.activation(o2[:, par, :, :].rearrange("p j d -> p (j d)"), m2_ps[par][:, :],
                                     ACT.Relu if relu2 else ACT.Copy).then_inc(o2_made, 1)

            stages = [(turn_down, 1)] if gcn else []
            if not norm:
                stages += [(relu_out, 0), (scale_out, 0)]
            elif second is None:
                stages += [(scale_out, -1)]
            else:
                stages = [(out_down, late), (second_out, late - 1)] + stages
            paced(act, *stages)

        @block.tensor
        def _(pe):
            def turn(i, g, par):
                wait(pe, u_made, g + 1)
                wait(pe, u_down, g)
                for j in range(J):
                    t = nc.tensor.transpose(tu_ps[:, j * P:(j + 1) * P], u[:, par, j * P:(j + 1) * P], k["ident"][:, :])
                t.then_inc(tu, 1)
                if len(first) == 2:
                    wait(pe, x_down, g)
                    for j in range(J):
                        t = nc.tensor.transpose(tx_ps[:, j * P:(j + 1) * P], x_in[:, par, j, :], k["ident"][:, :])
                    t.then_inc(tx, 1)

            def product(i, g, par):
                wait(pe, u_down, g + 1)
                if len(first) == 2:
                    wait(pe, x_down, g + 1)
                wait(pe, y_made if norm else o1_made, g - 1)
                sources = (u_t, x_t)[0:len(first)]
                if bias1 is not None:
                    nc.tensor.matmul(m1_ps[par][:, :], k["one_rows"][:, :], bias1[:, :], start=True, stop=False)
                for j in range(J):
                    for n, (a, b) in enumerate(zip(sources, first)):
                        t = nc.tensor.matmul(m1_ps[par][:, j * P:(j + 1) * P], a[:, par, j * P:(j + 1) * P], b[:, :],
                                             start=n == 0 and bias1 is None,
                                             stop=n == len(first) - 1 and (bias1 is None or j == J - 1))
                t.then_inc(m1, 1)

            def turn_out(i, g, par):
                wait(pe, o1_made, g + 1)
                wait(pe, o1_down, g)
                for j in range(J):
                    t = nc.tensor.transpose(t2_ps[:, j * P:(j + 1) * P], o1[:, par, j, :], k["ident"][:, :])
                t.then_inc(t2, 1)

            def second_product(i, g, par):
                wait(pe, o1_down, g + 1)
                wait(pe, o2_made, g - 1)
                nc.tensor.matmul(m2_ps[par][:, :], k["one_rows"][:, :], bias2[:, :], start=True, stop=False)
                for j in range(J):
                    t = nc.tensor.matmul(m2_ps[par][:, j * P:(j + 1) * P], o1_t[:, par, j * P:(j + 1) * P], second[:, :],
                                         start=False, stop=j == J - 1)
                t.then_inc(m2, 1)

            if gcn:
                stages = [(turn_out, late)] if second is not None else []
                stages += [(product, 0)]
                stages += [(second_product, late - 1)] if second is not None else []
                stages += [(turn, 1)]
            else:
                stages = [(second_product, late - 1), (turn_out, late)] if second is not None else []
            if stages:
                paced(pe, *stages)


def batch_norm(nc, ph, stats, gain, shift, bias, halves):
    sb, sem = ph.sb, ph.sem
    moments, spread, power, root = sb("moments", [P, halves, 2]), sb("spread", [P, halves]), sb("power", [P, halves]), sb("root", [P, halves])
    affine, mean = sb("affine", [P, halves, 2]), sb("mean", [P, halves])
    stepped, spread_in, raised, done = sem("stepped"), sem("spread_in"), sem("raised"), sem("affine_in")

    def pool_part(pool):
        nc.gpsimd.memset(power[:, :], -0.5).then_inc(stepped, 1)
        pool.wait_ge(spread_in, 1)
        pool.wait_ge(stepped, 1)
        nc.gpsimd.tensor_tensor(root[:, :], spread[:, :], power[:, :], ALU.pow).then_inc(raised, 1)

    def v_part(v):
        n = sem("n")
        count = [0]

        def step(ins):
            count[0] += 1
            ins.then_inc(n, 1)
            v.wait_ge(n, count[0])

        for h in range(halves):
            step(nc.vector.bn_aggr(moments[:, h, :], stats[:, h, :]))
        nc.vector.tensor_scalar(spread[:, :], moments[:, :, 1], BN_EPS, None, ALU.add).then_inc(spread_in, 1)
        step(nc.vector.tensor_tensor(mean[:, :], moments[:, :, 0], bias, ALU.add))
        step(nc.vector.tensor_tensor(mean[:, :], bias, mean[:, :], ALU.subtract))
        v.wait_ge(raised, 1)
        step(nc.vector.tensor_tensor(affine[:, :, 0], root[:, :], gain, ALU.mult))
        step(nc.vector.tensor_tensor(mean[:, :], mean[:, :], affine[:, :, 0], ALU.mult))
        nc.vector.tensor_tensor(affine[:, :, 1], mean[:, :], shift, ALU.add).then_inc(done, 1)
    return affine, done, pool_part, v_part


def group_stats(nc, stats, h, g, product, last):
    if last:
        product = product.rearrange("p (j n) -> p j n", j=J)[:, :, 0:LASTP]
    return nc.vector.bn_stats(stats[:, h, ds(g * 6, 6)], product)


def gin_in(nc, k, m, layer, h_rows, sums, z_cols, stats):
    with nc.cleanup_on_exit(), ExitStack() as ctx:
        ph = Phase(nc, ctx)
        sb, ps, sem = ph.sb, ph.ps, ph.sem
        h_in, s_in, z, z_t = (sb(n, [P, 2, W]) for n in ("h_in", "s_in", "z", "z_t"))
        idx = sb("idx", [P, 2, J], I32)
        turn_ps = [ps("turn0", [P, 512]), ps("turn1", [P, 512])]
        wide_ps = [[ps(f"wide{n}{h}", [P, 512]) for h in range(2)] for n in range(2)]
        came, gathered, stored = ([sem(n + "0"), sem(n + "1")] for n in ("came", "gathered", "stored"))
        z_made, turned, z_down, wide, counted, staged, passed_sp, passed = (sem(n) for n in (
            "z_made", "turned", "z_down", "wide", "counted", "staged", "passed_sp", "passed"))
        block = ctx.enter_context(nc.Block())

        @block.sync
        def _(sp):
            def front(i, g, par):
                wait(sp, z_made, g - 1, passed_sp)
                sp.dma_start(h_in[:, par, :], rows_of(h_rows, g)).then_inc(came[par], 16)

            def back(i, g, par):
                wait(sp, z_down, g + 1, passed_sp)
                sp.dma_start(block_of(z_cols, g), z_t[:, par, :]).then_inc(stored[par], 16)
            paced(sp, (front, 2), (back, -1))
            for par in range(2):
                sp.wait_ge(stored[par], 16 * (G // 2))

        @block.gpsimd
        def _(pool):
            def gather(i, g, par):
                wait(pool, staged, g + 1, passed)
                wait(pool, z_made, g - 1, passed)
                for j in range(J):
                    nc.gpsimd.indirect_dma_start(s_in[:, par, j * P:(j + 1) * P], None, sums,
                                                 bass.IndirectOffsetOnAxis(ap=idx[:, par, j:j + 1], axis=0)).then_inc(gathered[par], 16)
            paced(pool, (gather, 0))

        @block.vector
        def _(v):
            def front(i, g, par):
                wait(v, came[par], 16 * (i + 1))
                wait(v, gathered[par], 16 * J * (i + 1))
                wait(v, turned, g - 1)
                nc.vector.scalar_tensor_tensor(z[:, par, :], h_in[:, par, :], m["eps_row"][:, layer:layer + 1], s_in[:, par, :],
                                               ALU.mult, ALU.add).then_inc(z_made, 1)

            def back(i, g, par):
                last = isinstance(g, int) and g == G - 1
                for h in range(2):
                    wait(v, wide, 2 * g + h + 1)
                    group_stats(nc, stats, h, g, wide_ps[par][h][:, :], last).then_inc(counted, 1)
            paced(v, (front, 1), (back, 0))

        @block.scalar
        def _(act):
            def stage(i, g, par):
                wait(act, gathered[par], 16 * J * i)
                nc.scalar.copy(idx[:, par, :], k["last_r"][:, ds(g * J, J)]).then_inc(staged, 1)

            def turn_down(i, g, par):
                wait(act, turned, g + 1)
                wait(act, wide, 2 * (g - 1))
                wait(act, stored[par], 16 * i)
                nc.scalar.copy(z_t[:, par, :], turn_ps[par][:, :]).then_inc(z_down, 1)
            paced(act, (stage, 3), (turn_down, 0))

        @block.tensor
        def _(pe):
            def front(i, g, par):
                wait(pe, z_made, g + 1)
                wait(pe, z_down, g - 1)
                for j in range(J):
                    t = nc.tensor.transpose(turn_ps[par][:, j * P:(j + 1) * P], z[:, par, j * P:(j + 1) * P], k["ident"][:, :])
                t.then_inc(turned, 1)

            def back(i, g, par):
                wait(pe, z_down, g + 1)
                wait(pe, counted, 2 * (g - 1))
                for h in range(2):
                    nc.tensor.matmul(wide_ps[par][h][:, :], m["gin1"][:, layer, h * P:(h + 1) * P], z_t[:, par, :],
                                     start=True, stop=True).then_inc(wide, 1)
            paced(pe, (back, 0), (front, 1))


def gin_middle(nc, k, m, layer, z_cols, stats, y_cols, stats2):
    with nc.cleanup_on_exit(), ExitStack() as ctx:
        ph = Phase(nc, ctx)
        sb, ps, sem = ph.sb, ph.ps, ph.sem
        z_t, y_t = (sb(n, [P, 2, W]) for n in ("z_t", "y_t"))
        wide_sb = sb("wide_sb", [P, 2, 2, W])
        wide_ps = [[ps(f"wide{n}{h}", [P, 512]) for h in range(2)] for n in range(2)]
        y_ps = [ps("y0", [P, 512]), ps("y1", [P, 512])]
        came, stored = ([sem(n + "0"), sem(n + "1")] for n in ("came", "stored"))
        wide, wide_down, product, y_down, counted, passed_sp = (sem(n) for n in (
            "wide", "wide_down", "product", "y_down", "counted", "passed_sp"))
        affine, affine_in, pool_part, v_part = batch_norm(nc, ph, stats, m["g1"][:, layer, :], m["be1"][:, layer, :],
                                                          m["b1"][:, layer, :], 2)
        block = ctx.enter_context(nc.Block())

        @block.gpsimd
        def _(pool):
            pool_part(pool)

        @block.sync
        def _(sp):
            def front(i, g, par):
                wait(sp, wide, 2 * (g - 1), passed_sp)
                sp.dma_start(z_t[:, par, :], block_of(z_cols, g)).then_inc(came[par], 16)

            def back(i, g, par):
                wait(sp, y_down, g + 1, passed_sp)
                sp.dma_start(block_of(y_cols, g), y_t[:, par, :]).then_inc(stored[par], 16)
            paced(sp, (front, 2), (back, -1))
            for par in range(2):
                sp.wait_ge(stored[par], 16 * (G // 2))

        @block.scalar
        def _(act):
            act.wait_ge(affine_in, 1)

            def body(i):
                for par in range(2):
                    g = 2 * i + par
                    wait(act, product, g - 1)
                    for h in range(2):
                        wait(act, wide, 2 * g + h + 1)
                        nc.scalar.activation(wide_sb[:, par, h, :], wide_ps[par][h][:, :], ACT.Relu, bias=affine[:, h, 1:2],
                                             scale=affine[:, h, 0:1]).then_inc(wide_down, 1)
            loop(act, body)

        @block.vector
        def _(v):
            v_part(v)

            def body(i):
                for par in range(2):
                    g = 2 * i + par
                    wait(v, product, g + 1)
                    group_stats(nc, stats2, 0, g, y_ps[par][:, :], isinstance(g, int) and g == G - 1).then_inc(counted, 1)
                    wait(v, stored[par], 16 * i)
                    nc.vector.tensor_copy(y_t[:, par, :], y_ps[par][:, :]).then_inc(y_down, 1)
            loop(v, body)

        @block.tensor
        def _(pe):
            def front(i, g, par):
                wait(pe, came[par], 16 * (i + 1))
                wait(pe, wide_down, 2 * (g - 1))
                for h in range(2):
                    nc.tensor.matmul(wide_ps[par][h][:, :], m["gin1"][:, layer, h * P:(h + 1) * P], z_t[:, par, :],
                                     start=True, stop=True).then_inc(wide, 1)

            def back(i, g, par):
                wait(pe, wide_down, 2 * g + 2)
                wait(pe, y_down, g - 1)
                for h in range(2):
                    t = nc.tensor.matmul(y_ps[par][:, :], m["gin2"][:, layer, h, :], wide_sb[:, par, h, :], start=h == 0, stop=h == 1)
                t.then_inc(product, 1)
            paced(pe, (front, 1), (back, 0))


def gin_out(nc, k, m, layer, y_cols, stats2, h_rows):
    with nc.cleanup_on_exit(), ExitStack() as ctx:
        ph = Phase(nc, ctx)
        sb, ps, sem = ph.sb, ph.ps, ph.sem
        y_t = sb("y_t", [P, RING, W])
        h_t, h_sb = (sb(n, [P, 2, W]) for n in ("h_t", "h_sb"))
        turn_ps = [ps("turn0", [P, 512]), ps("turn1", [P, 512])]
        came = [sem(f"came{r}") for r in range(RING)]
        stored = [sem("stored0"), sem("stored1")]
        normed, turned, h_down, passed_sp = (sem(n) for n in ("normed", "turned", "h_down", "passed_sp"))
        affine, affine_in, pool_part, v_part = batch_norm(nc, ph, stats2, m["gn"][:, layer:layer + 1],
                                                          m["bet"][:, layer:layer + 1], m["b2"][:, layer:layer + 1], 1)
        block = ctx.enter_context(nc.Block())

        @block.gpsimd
        def _(pool):
            pool_part(pool)

        @block.sync
        def _(sp):
            def front(i, g, slot):
                wait(sp, normed, g - 3, passed_sp)
                sp.dma_start(y_t[:, slot, :], block_of(y_cols, g)).then_inc(came[slot], 16)

            def back(i, g, slot):
                wait(sp, h_down, g + 1, passed_sp)
                sp.dma_start(rows_of(h_rows, g), h_sb[:, slot % 2, :]).then_inc(stored[slot % 2], 16)
            paced(sp, (back, -1), (front, 4), ring=RING)
            for par in range(2):
                sp.wait_ge(stored[par], 16 * (G // 2))

        @block.scalar
        def _(act):
            act.wait_ge(affine_in, 1)

            def norm(i, g, slot):
                wait(act, came[slot], 16 * (i + 1))
                wait(act, turned, g - 1)
                nc.scalar.activation(h_t[:, slot % 2, :], y_t[:, slot, :], ACT.Relu, bias=affine[:, 0, 1:2],
                                     scale=affine[:, 0, 0:1]).then_inc(normed, 1)
            paced(act, (norm, 0), ring=RING)

        @block.vector
        def _(v):
            v_part(v)

            def body(i):
                for par in range(2):
                    g = 2 * i + par
                    wait(v, turned, g + 1)
                    wait(v, stored[par], 16 * i)
                    nc.vector.tensor_copy(h_sb[:, par, :], turn_ps[par][:, :]).then_inc(h_down, 1)
            loop(v, body)

        @block.tensor
        def _(pe):
            def body(i):
                for par in range(2):
                    g = 2 * i + par
                    wait(pe, normed, g + 1)
                    wait(pe, h_down, g - 1)
                    for j in range(J):
                        t = nc.tensor.transpose(turn_ps[par][:, j * P:(j + 1) * P], h_t[:, par, j * P:(j + 1) * P], k["ident"][:, :])
                    t.then_inc(turned, 1)
            loop(pe, body)


def final_rows(nc, k, m, y_cols, stats2, x, out):
    layer = LAYERS - 1
    with nc.cleanup_on_exit(), ExitStack() as ctx:
        ph = Phase(nc, ctx)
        sb, ps, sem = ph.sb, ph.ps, ph.sem
        y_t, x_in = sb("y_t", [P, RING, W]), sb("x_in", [P, RING, W])
        h_t, y, o = (sb(n, [P, 2, W]) for n in ("h_t", "y", "o"))
        parts, aggregate = sb("parts", [P, 2, J, 6]), sb("aggregate", [P, 2, J, 2])
        spread_r, inverse, minus_half = sb("spread_r", [P, 2, J]), sb("inverse", [P, 2, J]), sb("minus_half", [P, J])
        out_ps = [ps("out0", [P, 512]), ps("out1", [P, 512])]
        came = [sem(f"came{r}") for r in range(RING)]
        x_came = [sem(f"x_came{r}") for r in range(RING)]
        stored = [sem("stored0"), sem("stored1")]
        normed, product, summed, measured, joined, rows_spread, halved, raised_r, o_made, passed_sp, passed, passed_v = (sem(n) for n in (
            "normed", "product", "summed", "measured", "joined", "rows_spread", "halved", "raised_r", "o_made", "passed_sp", "passed", "passed_v"))
        affine, affine_in, pool_part, v_part = batch_norm(nc, ph, stats2, m["gn"][:, layer:layer + 1],
                                                          m["bet"][:, layer:layer + 1], m["b2"][:, layer:layer + 1], 1)
        block = ctx.enter_context(nc.Block())

        @block.gpsimd
        def _(pool):
            pool_part(pool)
            nc.gpsimd.memset(minus_half[:, :], -0.5).then_inc(halved, 1)
            pool.wait_ge(halved, 1)

            def body(i):
                for par in range(2):
                    wait(pool, rows_spread, 2 * i + par + 1, passed)
                    nc.gpsimd.tensor_tensor(inverse[:, par, :], spread_r[:, par, :], minus_half[:, :], ALU.pow).then_inc(raised_r, 1)
            loop(pool, body)

        @block.sync
        def _(sp):
            def front(i, g, slot):
                wait(sp, normed, g - 3, passed_sp)
                sp.dma_start(y_t[:, slot, :], block_of(y_cols, g)).then_inc(came[slot], 16)
                wait(sp, summed, g - 3, passed_sp)
                sp.dma_start(x_in[:, slot, :], rows_of(x, g)).then_inc(x_came[slot], 16)

            def back(i, g, slot):
                par = slot % 2
                wait(sp, o_made, g + 1, passed_sp)
                if isinstance(g, int) and g == G - 1:
                    sp.dma_start(x_rows(out, last=True), o[0:LASTP, par, :]).then_inc(stored[par], 16)
                else:
                    sp.dma_start(block_of(x_rows(out), g), o[:, par, :]).then_inc(stored[par], 16)
            paced(sp, (back, -2), (front, 4), ring=RING)
            for par in range(2):
                sp.wait_ge(stored[par], 16 * (G // 2))

        @block.scalar
        def _(act):
            act.wait_ge(affine_in, 1)

            def norm(i, g, slot):
                wait(act, came[slot], 16 * (i + 1))
                wait(act, product, g - 1)
                nc.scalar.activation(h_t[:, slot % 2, :], y_t[:, slot, :], ACT.Relu, bias=affine[:, 0, 1:2],
                                     scale=affine[:, 0, 0:1]).then_inc(normed, 1)
            paced(act, (norm, 0), ring=RING)

        @block.tensor
        def _(pe):
            def body(i):
                for par in range(2):
                    g = 2 * i + par
                    wait(pe, normed, g + 1)
                    wait(pe, summed, g - 1)
                    nc.tensor.matmul(out_ps[par][:, :], k["one_rows"][:, :], m["final_b"][:, :], start=True, stop=False)
                    for j in range(J):
                        t = nc.tensor.matmul(out_ps[par][:, j * P:(j + 1) * P], h_t[:, par, j * P:(j + 1) * P], m["final"][:, :],
                                             start=False, stop=j == J - 1)
                    t.then_inc(product, 1)
            loop(pe, body)

        @block.vector
        def _(v):
            v_part(v)

            def measure(i, g, slot):
                par = slot % 2
                wait(v, product, g + 1)
                wait(v, x_came[slot], 16 * (i + 1))
                wait(v, o_made, g - 1)
                nc.vector.tensor_tensor(y[:, par, :], out_ps[par][:, :], x_in[:, slot, :], ALU.add).then_inc(summed, 1)
                wait(v, summed, g + 1)
                for j in range(J):
                    last = nc.vector.bn_stats(parts[:, par, j, :], y[:, par, j * P:(j + 1) * P])
                last.then_inc(measured, 1)
                wait(v, measured, g + 1, passed_v)
                for j in range(J):
                    last = nc.vector.bn_aggr(aggregate[:, par, j, :], parts[:, par, j, :])
                last.then_inc(joined, 1)
                wait(v, joined, g + 1)
                nc.vector.tensor_scalar(spread_r[:, par, :], aggregate[:, par, :, 1], LN_EPS, None, ALU.add).then_inc(rows_spread, 1)

            def apply(i, g, slot):
                par = slot % 2
                wait(v, stored[par], 16 * (2 * i + slot // 2))
                wait(v, raised_r, g + 1)
                for j in range(J):
                    last = nc.vector.tensor_scalar(o[:, par, j * P:(j + 1) * P], y[:, par, j * P:(j + 1) * P],
                                                   aggregate[:, par, j, 0:1], inverse[:, par, j:j + 1], ALU.subtract, ALU.mult)
                last.then_inc(o_made, 1)
            paced(v, (measure, 0), (apply, -1), ring=RING)


INPUTS = ["x", "src", "dst", "edge_attr_128", "edge_attr_3", "edge_weight", "L0_gnn_W_up0", "L0_gnn_W_up1", "L0_gnn_mlp_w0",
          "L0_gnn_mlp_b0", "L0_gnn_mlp_w1", "L0_gnn_mlp_b1", "L0_gnn_mlp_w2", "L0_gnn_mlp_b2", "L0_gnn_W_out0",
          "L0_gnn_W_out1", "L1_gnn_W1", "L1_gnn_R1", "L1_gnn_W2", "L1_gnn_R2", "L1_gnn_W3", "L1_gnn_Wh", "L1_gnn_bh",
          "L2_gnn_W", "L2_gnn_b", "L3_gnn_W_atom", "L3_gnn_b_atom", "L3_gnn_W_bond", "L3_gnn_b_bond", "L3_gnn_eps",
          "L3_gnn_W1", "L3_gnn_b1", "L3_gnn_g1", "L3_gnn_be1", "L3_gnn_W2", "L3_gnn_b2", "L3_gnn_gn", "L3_gnn_bet",
          "L3_gnn_W_out", "L3_gnn_b_out"]


def program(nc, w, out):
    def scratch(name, shape):
        return nc.dram_tensor(name, shape, F32, kind="Internal").ap()

    x = w["x"]
    d = {"sorted_r": scratch("sorted_r", [P * 512, 8]), "sorted_s": scratch("sorted_s", [P * 512, 8]),
         "line_r": scratch("line_r", [NP]), "line_s": scratch("line_s", [NP]),
         "sum_r": scratch("sum_r", [NP + 1, P]), "sum_s": scratch("sum_s", [NP + 1, P + 1])}
    groups = [scratch(f"groups{n}", [G, P, W]) for n in range(3)]
    messages, bonds, z_cols = groups
    y_cols = messages
    x1, x2, x3, xa, xb, scaled, h = (scratch(n, [NP, P]) for n in ("x1", "x2", "x3", "xa", "xb", "scaled", "h"))
    with ExitStack() as ctx:
        k = fixed_tiles(nc, ctx)
        k["line"] = {"r": d["line_r"], "s": d["line_s"]}
        count_and_rank(nc, k, d, w["src"], w["dst"], w["edge_weight"], w["edge_attr_3"])
        order_tables(nc, k, d)
        with ExitStack() as inner:
            t = tensor_product_weights(nc, k, {n[len("L0_gnn_"):]: a for n, a in w.items() if n.startswith("L0")}, inner)
            edge_products(nc, k, x, t, messages)
        m = load_weights(nc, k, ctx, w)
        segment_sum(nc, k, "r", d["sum_r"], messages=messages, beside=bond_rows(nc, k, w["edge_attr_128"], m, bonds))
        node_rows(nc, k, x, d["sum_r"], x1, scaled, outside=True)
        segment_sum(nc, k, "r", d["sum_r"], table=scaled)
        node_rows(nc, k, x1, d["sum_r"], xa, scaled, gcn=True, first=(m["W1"], m["R1"]), norm=False)
        segment_sum(nc, k, "r", d["sum_r"], table=scaled)
        node_rows(nc, k, xa, d["sum_r"], xb, scaled, gcn=True, first=(m["W2"], m["R2"]), norm=False)
        segment_sum(nc, k, "r", d["sum_r"], table=scaled)
        node_rows(nc, k, xb, d["sum_r"], x2, h, gcn=True, first=(m["W3Wh"],), bias1=m["bh"], residual=x1,
                  second=m["lin_t"], bias2=m["lin_b"], relu2=True)
        segment_sum(nc, k, "s", d["sum_s"], width=P + 1, table=h, weight=k["weight_s"])
        node_rows(nc, k, x2, d["sum_s"], x3, h, weighted=True, second=m["atom"], bias2=m["atom_b"])
        stats = ctx.enter_context(nc.sbuf_tensor("stats", [P, 2, G * 6], F32))
        stats2 = ctx.enter_context(nc.sbuf_tensor("stats2", [P, 1, G * 6], F32))
        for layer in range(LAYERS):
            segment_sum(nc, k, "r", d["sum_r"], table=h, added=bonds)
            gin_in(nc, k, m, layer, h, d["sum_r"], z_cols, stats)
            gin_middle(nc, k, m, layer, z_cols, stats, y_cols, stats2)
            if layer < LAYERS - 1:
                gin_out(nc, k, m, layer, y_cols, stats2, h)
        final_rows(nc, k, m, y_cols, stats2, x3, out)


def kernel(**inputs):
    import concourse.bacc as bacc
    from concourse.bass_utils import run_bass_kernel_spmd

    nc = bacc.Bacc("TRN2", target_bir_lowering=False, num_devices=1)
    arrays, handles = {}, {}
    for name in INPUTS:
        a = np.ascontiguousarray(inputs[name])
        arrays["in_" + name] = a
        handles[name] = nc.dram_tensor("in_" + name, a.shape, mybir.dt.from_np(a.dtype), kind="ExternalInput").ap()
    out = nc.dram_tensor("out_nodes", (N, P), F32, kind="ExternalOutput").ap()
    program(nc, handles, out)
    return run_bass_kernel_spmd(nc, [arrays], core_ids=[0]).results[0]["out_nodes"]
```
